# Optimizing a Trainium2 kernel written in Bass

```python
import numpy as np
import jax
import jax.numpy as jnp

def _softmax(x, axis=-1):
    return jax.nn.softmax(x, axis=axis)

def _gelu(x):
    return jax.nn.gelu(x, approximate=True)

def _silu(x):
    return jax.nn.silu(x)

def _sigmoid(x):
    return jax.nn.sigmoid(x)

def _layernorm(x, axis=-1, eps=1e-05):
    m = jnp.mean(x, axis=axis, keepdims=True)
    v = jnp.var(x, axis=axis, keepdims=True)
    return (x - m) / jnp.sqrt(v + eps)

def _scatter_add(tgt, idx, src, axis=0):
    return tgt.at[idx].add(src)

def _segment_sum(src, seg, n):
    return jax.ops.segment_sum(src, seg, n)
kernel_name = 'mk_decoder_preln_d2_seqx_r8_c76c82'

def setup_inputs(seed: int=0):
    np.random.seed(seed)
    _w = jnp.asarray

    def _rec_inputs():
        import jax
        import jax.numpy as jnp
        _rk = jax.random.key(seed)
        x = -0.0002928 + 1 * jax.random.normal(jax.random.fold_in(_rk, 1), (4, 256, 256), jnp.float32)
        _lenS = 256 - jax.random.randint(jax.random.fold_in(_rk, 7), (4,), 0, max(1, 256 // 4) + 1, jnp.int32)
        _lenS2 = 1601 - jax.random.randint(jax.random.fold_in(_rk, 8), (4,), 0, max(1, 1601 // 4) + 1, jnp.int32)
        _ctx_512P = jax.random.normal(jax.random.fold_in(_rk, 11), (4, 16, 64), jnp.float32)
        _ctx_512c = jax.random.dirichlet(jax.random.fold_in(_rk, 511), 0.3 * jnp.ones((16,), jnp.float32), (4, 1601))
        _ctx_512t = jnp.einsum('bsk,bkd->bsd', _ctx_512c, _ctx_512P)
        _ctx_512t = _ctx_512t * jax.lax.rsqrt(jnp.mean(jnp.square(_ctx_512t)) + 1e-12) * 0.953939
        ctx_512 = 0.000227908 + 0.99994 * (_ctx_512t + 0.3 * jax.random.normal(jax.random.fold_in(_rk, 611), (4, 1601, 64), jnp.float32))
        return (x, ctx_512)
    x, ctx_512 = _rec_inputs()

    def _L0_attn_setup():
        import jax, jax.numpy as jnp
        import numpy as np
        HK, HV, DK, DV, K_CONV, CHUNK = (16, 32, 128, 128, 4, 64)
        DIM = 256
        EPS = 1e-06

        def _l2norm(x):
            return x * jax.lax.rsqrt(jnp.sum(x * x, -1, keepdims=True) + EPS)

        def _chunk_gated_delta_rule(q, k, v, g, beta):
            B, T, H, Dk = q.shape
            Dv = v.shape[-1]
            N = T // CHUNK
            scale = Dk ** (-0.5)

            def to_c(x):
                x = jnp.moveaxis(x, 1, 2)
                x = x.reshape(x.shape[0], x.shape[1], N, CHUNK, *x.shape[3:])
                return jnp.moveaxis(x, 2, 0)
            qc, kc, vc = (to_c(q), to_c(k), to_c(v))
            gc, bc = (to_c(g), to_c(beta))
            G = jnp.cumsum(gc, -1)
            diff = G[..., :, None] - G[..., None, :]
            strict = jnp.tril(jnp.ones((CHUNK, CHUNK), bool), -1)
            incl = jnp.tril(jnp.ones((CHUNK, CHUNK), bool))
            M = jnp.where(strict, bc[..., :, None] * jnp.exp(diff) * jnp.einsum('nbhtd,nbhsd->nbhts', kc, kc), 0.0)
            A = jnp.where(incl, scale * jnp.exp(diff) * jnp.einsum('nbhtd,nbhsd->nbhts', qc, kc), 0.0)
            I = jnp.eye(CHUNK, dtype=q.dtype)
            Tinv = jax.scipy.linalg.solve_triangular(I + M, jnp.broadcast_to(I, M.shape), lower=True)
            u0 = jnp.einsum('nbhts,nbhsd->nbhtd', Tinv, bc[..., None] * vc)
            w = jnp.einsum('nbhts,nbhsd->nbhtd', Tinv, (bc * jnp.exp(G))[..., None] * kc)
            kd = jnp.exp(G[..., -1:] - G)[..., None] * kc
            qd = scale * jnp.exp(G)[..., None] * qc
            gC = G[..., -1]

            def step(S, xs):
                u0_, w_, A_, kd_, qd_, gC_ = xs
                u = u0_ - jnp.einsum('bhcd,bhde->bhce', w_, S)
                o = jnp.einsum('bhts,bhse->bhte', A_, u) + jnp.einsum('bhcd,bhde->bhce', qd_, S)
                S = jnp.exp(gC_)[..., None, None] * S + jnp.einsum('bhcd,bhce->bhde', kd_, u)
                return (S, o)
            S0 = jnp.zeros((B, H, Dk, Dv), q.dtype)
            _, o = jax.lax.scan(step, S0, (u0, w, A, kd, qd, gC))
            o = jnp.moveaxis(o, 0, 2).reshape(B, H, T, Dv)
            return jnp.moveaxis(o, 1, 2)
        key = jax.random.key(seed)
        ks = jax.random.split(key, 8)
        B, T, D = (1, 512, DIM)
        key_dim, value_dim = (HK * DK, HV * DV)
        conv_dim = 2 * key_dim + value_dim
        s = 0.02
        return {'hidden_states': jax.random.normal(ks[0], (B, T, D), jnp.float32), 'W_qkvz': jax.random.normal(ks[1], (D, 2 * key_dim + 2 * value_dim), jnp.float32) * s, 'W_ba': jax.random.normal(ks[2], (D, 2 * HV), jnp.float32) * s, 'conv_w': jax.random.normal(ks[3], (conv_dim, K_CONV), jnp.float32) * 0.1, 'dt_bias': jnp.ones((HV,), jnp.float32), 'A_log': jnp.log(jax.random.uniform(ks[4], (HV,), jnp.float32, 0.001, 16.0)), 'norm_weight': jnp.ones((DV,), jnp.float32), 'W_out': jax.random.normal(ks[5], (value_dim, D), jnp.float32) * s}
    _L0_attn_all = _L0_attn_setup()
    _L0_attn_in = {k: v for k, v in _L0_attn_all.items() if k in ('W_qkvz', 'W_ba', 'conv_w', 'dt_bias', 'A_log', 'norm_weight', 'W_out')}
    del _L0_attn_all

    def _L0_xattn_setup():
        import jax, jax.numpy as jnp
        import numpy as np
        B, S, L = (2, 128, 128)
        DIM_Q, H, K, D_C, D_CQ, R = (256, 16, 128, 64, 192, 64)

        def _rope_tables(seq_len, dim, dtype):
            inv_freq = 1.0 / 10000.0 ** (jnp.arange(0, dim, 2, dtype=dtype) / dim)
            t = jnp.arange(seq_len, dtype=dtype)
            freqs = t[:, None] * inv_freq[None, :]
            sin = jnp.repeat(jnp.sin(freqs), 2, axis=-1)
            cos = jnp.repeat(jnp.cos(freqs), 2, axis=-1)
            return (sin, cos)

        def _rotate_half(x):
            h = x.shape[-1] // 2
            return jnp.concatenate([-x[..., h:], x[..., :h]], axis=-1)
        key = jax.random.key(seed)
        ks = jax.random.split(key, 8)
        s_in = 1.0 / np.sqrt(DIM_Q)
        s_k = 1.0 / np.sqrt(K)
        s_cq = 1.0 / np.sqrt(D_CQ)
        s_c = 1.0 / np.sqrt(D_C)
        return {'hidden_q': jax.random.normal(ks[0], (B, S, DIM_Q), jnp.float32), 'kv_c': jax.random.normal(ks[1], (B, L, D_C), jnp.float32), 'Wq': jax.random.normal(ks[2], (H * K, DIM_Q), jnp.float32) * s_in, 'w_kc_q': jax.random.normal(ks[3], (H, K, D_CQ), jnp.float32) * s_k, 'w_kc_kv': jax.random.normal(ks[4], (H, K, D_C), jnp.float32) * s_k, 'W_qr': jax.random.normal(ks[5], (H, D_CQ, R), jnp.float32) * s_cq / np.sqrt(R), 'W_kr': jax.random.normal(ks[6], (H, D_C, R), jnp.float32) * s_c, 'Wo': jax.random.normal(ks[7], (DIM_Q, H * K), jnp.float32) * s_k}
    _L0_xattn_all = _L0_xattn_setup()
    _L0_xattn_in = {k: v for k, v in _L0_xattn_all.items() if k in ('Wq', 'w_kc_q', 'w_kc_kv', 'W_qr', 'W_kr', 'Wo')}
    del _L0_xattn_all

    def _L0_ffn_setup():
        import jax, jax.numpy as jnp
        import numpy as np
        DIM_IN = 256
        DIM_HIDDEN = 1024
        key = jax.random.key(seed)
        k_x, k_g, k_u, k_d = jax.random.split(key, 4)
        s_in = 1.0 / np.sqrt(DIM_IN)
        s_hid = 1.0 / np.sqrt(DIM_HIDDEN)
        x = jax.random.normal(k_x, (4, 256, DIM_IN), dtype=jnp.float32)
        w_gate = jax.random.uniform(k_g, (DIM_HIDDEN, DIM_IN), jnp.float32, -s_in, s_in)
        w_up = jax.random.uniform(k_u, (DIM_HIDDEN, DIM_IN), jnp.float32, -s_in, s_in)
        w_down = jax.random.uniform(k_d, (DIM_IN, DIM_HIDDEN), jnp.float32, -s_hid, s_hid)
        return {'x': x, 'w_gate': w_gate, 'w_up': w_up, 'w_down': w_down}
    _L0_ffn_all = _L0_ffn_setup()
    _L0_ffn_in = {k: v for k, v in _L0_ffn_all.items() if k in ('w_gate', 'w_up', 'w_down')}
    del _L0_ffn_all

    def _L1_attn_setup():
        import jax, jax.numpy as jnp
        import numpy as np
        N_EMBD = 256
        N_Q_HEAD = 16
        N_KV_HEADS = 4
        HEAD_SIZE = N_EMBD // N_Q_HEAD
        GROUP = N_Q_HEAD // N_KV_HEADS
        ROPE_BASE = 10000.0

        def apply_rope(x, seq_offset=0):
            B, H, T, D = x.shape
            half = D // 2
            inv_freq = 1.0 / ROPE_BASE ** (jnp.arange(0, half, dtype=jnp.float32) / half)
            pos = jnp.arange(seq_offset, seq_offset + T, dtype=jnp.float32)
            ang = pos[:, None] * inv_freq[None, :]
            cos = jnp.cos(ang)[None, None].astype(x.dtype)
            sin = jnp.sin(ang)[None, None].astype(x.dtype)
            x1, x2 = (x[..., :half], x[..., half:])
            return jnp.concatenate([x1 * cos - x2 * sin, x2 * cos + x1 * sin], axis=-1)
        key = jax.random.key(seed)
        k0, k1, k2, k3, k4 = jax.random.split(key, 5)
        B, T = (4, 256)
        s = 1.0 / np.sqrt(N_EMBD)
        x = jax.random.normal(k0, (B, T, N_EMBD), dtype=jnp.float32)
        Wq = jax.random.normal(k1, (N_Q_HEAD * HEAD_SIZE, N_EMBD), dtype=jnp.float32) * s
        Wk = jax.random.normal(k2, (N_KV_HEADS * HEAD_SIZE, N_EMBD), dtype=jnp.float32) * s
        Wv = jax.random.normal(k3, (N_KV_HEADS * HEAD_SIZE, N_EMBD), dtype=jnp.float32) * s
        Wp = jax.random.normal(k4, (N_EMBD, N_Q_HEAD * HEAD_SIZE), dtype=jnp.float32) * s
        return {'x': x, 'Wq': Wq, 'Wk': Wk, 'Wv': Wv, 'Wp': Wp}
    _L1_attn_all = _L1_attn_setup()
    _L1_attn_in = {k: v for k, v in _L1_attn_all.items() if k in ('Wq', 'Wk', 'Wv', 'Wp')}
    del _L1_attn_all

    def _L1_xattn_setup():
        import jax, jax.numpy as jnp
        import numpy as np
        B, S, H, NH, L = (2, 256, 256, 16, 64)
        HD = H // NH
        key = jax.random.key(seed)
        k1, k2, k3, k4, k5 = jax.random.split(key, 5)
        scale = 0.02
        return {'q': jax.random.normal(k1, (B, S, H), dtype=jnp.float32), 'latent_kv': jax.random.normal(k2, (B, S, L), dtype=jnp.float32), 'Wq': jax.random.normal(k3, (H, H), dtype=jnp.float32) * scale, 'Wkv_expand': jax.random.normal(k4, (2 * H, L), dtype=jnp.float32) * scale, 'Wout': jax.random.normal(k5, (H, H), dtype=jnp.float32) * scale}
    _L1_xattn_all = _L1_xattn_setup()
    _L1_xattn_in = {k: v for k, v in _L1_xattn_all.items() if k in ('Wq', 'Wkv_expand', 'Wout')}
    del _L1_xattn_all

    def _L1_ffn_setup():
        import jax, jax.numpy as jnp
        import numpy as np
        B, S, H = (2, 256, 256)
        E, K, I = (64, 8, 96)

        def _moe_forward(hidden_states, gate_weight, w_gate, w_up, w_down):
            b, s, h = hidden_states.shape
            x = hidden_states.reshape(-1, h)
            logits = x.astype(jnp.float32) @ gate_weight.astype(jnp.float32).T
            scores = jax.nn.softmax(logits, axis=-1)
            topk_w, topk_idx = jax.lax.top_k(scores, K)
            topk_w = topk_w / jnp.sum(topk_w, axis=-1, keepdims=True)
            flat_ids = topk_idx.reshape(-1)
            expanded = jnp.repeat(x, K, axis=0)
            order = jnp.argsort(flat_ids)
            sorted_tokens = expanded[order]
            group_sizes = jnp.zeros((E,), jnp.int32).at[flat_ids].add(1)
            g = jax.lax.ragged_dot(sorted_tokens, w_gate, group_sizes)
            u = jax.lax.ragged_dot(sorted_tokens, w_up, group_sizes)
            out = jax.lax.ragged_dot(jax.nn.silu(g) * u, w_down, group_sizes)
            inv = jnp.argsort(order)
            outs = out[inv].reshape(-1, K, h)
            y = jnp.sum(outs * topk_w[:, :, None], axis=1)
            return y.reshape(b, s, h)
        key = jax.random.key(seed)
        k0, k1, k2, k3, k4 = jax.random.split(key, 5)
        hidden_states = jax.random.normal(k0, (B, S, H), dtype=jnp.float32)
        gate_weight = jax.random.normal(k1, (E, H), dtype=jnp.float32) * 0.02
        w_gate = jax.random.normal(k2, (E, H, I), dtype=jnp.float32) * 0.02
        w_up = jax.random.normal(k3, (E, H, I), dtype=jnp.float32) * 0.02
        w_down = jax.random.normal(k4, (E, I, H), dtype=jnp.float32) * 0.02
        return {'hidden_states': hidden_states, 'gate_weight': gate_weight, 'w_gate': w_gate, 'w_up': w_up, 'w_down': w_down}
    _L1_ffn_all = _L1_ffn_setup()
    _L1_ffn_in = {k: v for k, v in _L1_ffn_all.items() if k in ('gate_weight', 'w_gate', 'w_up', 'w_down')}
    del _L1_ffn_all
    return {'x': x, 'ctx_512': ctx_512, 'L0_attn_W_qkvz': _L0_attn_in['W_qkvz'], 'L0_attn_W_ba': _L0_attn_in['W_ba'], 'L0_attn_conv_w': _L0_attn_in['conv_w'], 'L0_attn_dt_bias': _L0_attn_in['dt_bias'], 'L0_attn_A_log': _L0_attn_in['A_log'], 'L0_attn_norm_weight': _L0_attn_in['norm_weight'], 'L0_attn_W_out': _L0_attn_in['W_out'], 'L0_xattn_Wq': _L0_xattn_in['Wq'], 'L0_xattn_w_kc_q': _L0_xattn_in['w_kc_q'], 'L0_xattn_w_kc_kv': _L0_xattn_in['w_kc_kv'], 'L0_xattn_W_qr': _L0_xattn_in['W_qr'], 'L0_xattn_W_kr': _L0_xattn_in['W_kr'], 'L0_xattn_Wo': _L0_xattn_in['Wo'], 'L0_ffn_w_gate': _L0_ffn_in['w_gate'], 'L0_ffn_w_up': _L0_ffn_in['w_up'], 'L0_ffn_w_down': _L0_ffn_in['w_down'], 'L1_attn_Wq': _L1_attn_in['Wq'], 'L1_attn_Wk': _L1_attn_in['Wk'], 'L1_attn_Wv': _L1_attn_in['Wv'], 'L1_attn_Wp': _L1_attn_in['Wp'], 'L1_xattn_Wq': _L1_xattn_in['Wq'], 'L1_xattn_Wkv_expand': _L1_xattn_in['Wkv_expand'], 'L1_xattn_Wout': _L1_xattn_in['Wout'], 'L1_ffn_gate_weight': _L1_ffn_in['gate_weight'], 'L1_ffn_w_gate': _L1_ffn_in['w_gate'], 'L1_ffn_w_up': _L1_ffn_in['w_up'], 'L1_ffn_w_down': _L1_ffn_in['w_down']}

def reference(x, ctx_512, L0_attn_W_qkvz, L0_attn_W_ba, L0_attn_conv_w, L0_attn_dt_bias, L0_attn_A_log, L0_attn_norm_weight, L0_attn_W_out, L0_xattn_Wq, L0_xattn_w_kc_q, L0_xattn_w_kc_kv, L0_xattn_W_qr, L0_xattn_W_kr, L0_xattn_Wo, L0_ffn_w_gate, L0_ffn_w_up, L0_ffn_w_down, L1_attn_Wq, L1_attn_Wk, L1_attn_Wv, L1_attn_Wp, L1_xattn_Wq, L1_xattn_Wkv_expand, L1_xattn_Wout, L1_ffn_gate_weight, L1_ffn_w_gate, L1_ffn_w_up, L1_ffn_w_down):
    import jax
    import jax.numpy as jnp

    def _L0_attn_ref(hidden_states, W_qkvz, W_ba, conv_w, dt_bias, A_log, norm_weight, W_out):
        import jax, jax.numpy as jnp
        import numpy as np
        HK, HV, DK, DV, K_CONV, CHUNK = (16, 32, 128, 128, 4, 64)
        DIM = 256
        EPS = 1e-06

        def _l2norm(x):
            return x * jax.lax.rsqrt(jnp.sum(x * x, -1, keepdims=True) + EPS)

        def _chunk_gated_delta_rule(q, k, v, g, beta):
            B, T, H, Dk = q.shape
            Dv = v.shape[-1]
            N = T // CHUNK
            scale = Dk ** (-0.5)

            def to_c(x):
                x = jnp.moveaxis(x, 1, 2)
                x = x.reshape(x.shape[0], x.shape[1], N, CHUNK, *x.shape[3:])
                return jnp.moveaxis(x, 2, 0)
            qc, kc, vc = (to_c(q), to_c(k), to_c(v))
            gc, bc = (to_c(g), to_c(beta))
            G = jnp.cumsum(gc, -1)
            diff = G[..., :, None] - G[..., None, :]
            strict = jnp.tril(jnp.ones((CHUNK, CHUNK), bool), -1)
            incl = jnp.tril(jnp.ones((CHUNK, CHUNK), bool))
            M = jnp.where(strict, bc[..., :, None] * jnp.exp(diff) * jnp.einsum('nbhtd,nbhsd->nbhts', kc, kc), 0.0)
            A = jnp.where(incl, scale * jnp.exp(diff) * jnp.einsum('nbhtd,nbhsd->nbhts', qc, kc), 0.0)
            I = jnp.eye(CHUNK, dtype=q.dtype)
            Tinv = jax.scipy.linalg.solve_triangular(I + M, jnp.broadcast_to(I, M.shape), lower=True)
            u0 = jnp.einsum('nbhts,nbhsd->nbhtd', Tinv, bc[..., None] * vc)
            w = jnp.einsum('nbhts,nbhsd->nbhtd', Tinv, (bc * jnp.exp(G))[..., None] * kc)
            kd = jnp.exp(G[..., -1:] - G)[..., None] * kc
            qd = scale * jnp.exp(G)[..., None] * qc
            gC = G[..., -1]

            def step(S, xs):
                u0_, w_, A_, kd_, qd_, gC_ = xs
                u = u0_ - jnp.einsum('bhcd,bhde->bhce', w_, S)
                o = jnp.einsum('bhts,bhse->bhte', A_, u) + jnp.einsum('bhcd,bhde->bhce', qd_, S)
                S = jnp.exp(gC_)[..., None, None] * S + jnp.einsum('bhcd,bhce->bhde', kd_, u)
                return (S, o)
            S0 = jnp.zeros((B, H, Dk, Dv), q.dtype)
            _, o = jax.lax.scan(step, S0, (u0, w, A, kd, qd, gC))
            o = jnp.moveaxis(o, 0, 2).reshape(B, H, T, Dv)
            return jnp.moveaxis(o, 1, 2)
        B, T, D = hidden_states.shape
        ratio = HV // HK
        key_dim = HK * DK
        qkvz = hidden_states @ W_qkvz
        ba = hidden_states @ W_ba
        qkvz = qkvz.reshape(B, T, HK, 2 * DK + 2 * ratio * DV)
        q = qkvz[..., :DK]
        k = qkvz[..., DK:2 * DK]
        v = qkvz[..., 2 * DK:2 * DK + ratio * DV].reshape(B, T, HV, DV)
        z = qkvz[..., 2 * DK + ratio * DV:].reshape(B, T, HV, DV)
        ba = ba.reshape(B, T, HK, 2 * ratio)
        b = ba[..., :ratio].reshape(B, T, HV)
        a = ba[..., ratio:].reshape(B, T, HV)
        mixed = jnp.concatenate([q.reshape(B, T, -1), k.reshape(B, T, -1), v.reshape(B, T, -1)], -1)
        xp = jnp.pad(mixed, ((0, 0), (K_CONV - 1, 0), (0, 0)))
        conv = sum((conv_w[:, j] * xp[:, j:j + T, :] for j in range(K_CONV)))
        mixed = jax.nn.silu(conv)
        q = mixed[..., :key_dim].reshape(B, T, HK, DK)
        k = mixed[..., key_dim:2 * key_dim].reshape(B, T, HK, DK)
        v = mixed[..., 2 * key_dim:].reshape(B, T, HV, DV)
        beta = jax.nn.sigmoid(b)
        g = -jnp.exp(A_log) * jax.nn.softplus(a + dt_bias)
        q = _l2norm(q)
        k = _l2norm(k)
        q = jnp.repeat(q, ratio, axis=2)
        k = jnp.repeat(k, ratio, axis=2)
        o = _chunk_gated_delta_rule(q, k, v, g, beta)
        xg = o * jax.nn.silu(z)
        xg = xg * jax.lax.rsqrt(jnp.mean(xg * xg, -1, keepdims=True) + 1e-06) * norm_weight
        return xg.reshape(B, T, -1) @ W_out

    def _L0_xattn_ref(hidden_q, kv_c, Wq, w_kc_q, w_kc_kv, W_qr, W_kr, Wo):
        import jax, jax.numpy as jnp
        import numpy as np
        B, S, L = (2, 128, 128)
        DIM_Q, H, K, D_C, D_CQ, R = (256, 16, 128, 64, 192, 64)

        def _rope_tables(seq_len, dim, dtype):
            inv_freq = 1.0 / 10000.0 ** (jnp.arange(0, dim, 2, dtype=dtype) / dim)
            t = jnp.arange(seq_len, dtype=dtype)
            freqs = t[:, None] * inv_freq[None, :]
            sin = jnp.repeat(jnp.sin(freqs), 2, axis=-1)
            cos = jnp.repeat(jnp.cos(freqs), 2, axis=-1)
            return (sin, cos)

        def _rotate_half(x):
            h = x.shape[-1] // 2
            return jnp.concatenate([-x[..., h:], x[..., :h]], axis=-1)
        b, s, _ = hidden_q.shape
        l = kv_c.shape[1]
        q_hk = (hidden_q @ Wq.T).reshape(b, s, H, K)
        q_big = jnp.einsum('bshk,hkq->bshq', q_hk, w_kc_q)
        sin, cos = _rope_tables(l, D_C, kv_c.dtype)
        kv_rope = kv_c * cos[None] + _rotate_half(kv_c) * sin[None]
        q_r = jnp.einsum('bshq,hqr->bhsr', q_big, W_qr)
        k_r = jnp.einsum('bld,hdr->bhlr', kv_rope, W_kr)
        scores = jnp.einsum('bhsr,bhlr->bhsl', q_r, k_r)
        attn = jax.nn.softmax(scores, axis=-1)
        ctx_c = jnp.einsum('bhsl,bld->bhsd', attn, kv_rope)
        ctx_lat = jnp.einsum('bhsd,hkd->bshk', ctx_c, w_kc_kv)
        out = ctx_lat.reshape(b, s, H * K) @ Wo.T
        return out

    def _L0_ffn_ref(x, w_gate, w_up, w_down):
        import jax, jax.numpy as jnp
        import numpy as np
        DIM_IN = 256
        DIM_HIDDEN = 1024
        gate = jnp.einsum('bsd,hd->bsh', x, w_gate)
        up = jnp.einsum('bsd,hd->bsh', x, w_up)
        gated = jax.nn.silu(gate) * up
        return jnp.einsum('bsh,dh->bsd', gated, w_down)

    def _L1_attn_ref(x, Wq, Wk, Wv, Wp):
        import jax, jax.numpy as jnp
        import numpy as np
        N_EMBD = 256
        N_Q_HEAD = 16
        N_KV_HEADS = 4
        HEAD_SIZE = N_EMBD // N_Q_HEAD
        GROUP = N_Q_HEAD // N_KV_HEADS
        ROPE_BASE = 10000.0

        def apply_rope(x, seq_offset=0):
            B, H, T, D = x.shape
            half = D // 2
            inv_freq = 1.0 / ROPE_BASE ** (jnp.arange(0, half, dtype=jnp.float32) / half)
            pos = jnp.arange(seq_offset, seq_offset + T, dtype=jnp.float32)
            ang = pos[:, None] * inv_freq[None, :]
            cos = jnp.cos(ang)[None, None].astype(x.dtype)
            sin = jnp.sin(ang)[None, None].astype(x.dtype)
            x1, x2 = (x[..., :half], x[..., half:])
            return jnp.concatenate([x1 * cos - x2 * sin, x2 * cos + x1 * sin], axis=-1)
        B, T, C = x.shape
        Q = (x @ Wq.T).reshape(B, T, N_Q_HEAD, HEAD_SIZE).transpose(0, 2, 1, 3)
        K = (x @ Wk.T).reshape(B, T, N_KV_HEADS, HEAD_SIZE).transpose(0, 2, 1, 3)
        V = (x @ Wv.T).reshape(B, T, N_KV_HEADS, HEAD_SIZE).transpose(0, 2, 1, 3)
        Q = apply_rope(Q, 0)
        K = apply_rope(K, 0)
        Qg = Q.reshape(B, N_KV_HEADS, GROUP, T, HEAD_SIZE)
        scale = 1.0 / jnp.sqrt(jnp.asarray(HEAD_SIZE, dtype=Q.dtype))
        scores = jnp.einsum('bkgtd,bksd->bkgts', Qg, K) * scale
        causal = jnp.tril(jnp.ones((T, T), dtype=bool))
        scores = jnp.where(causal, scores, jnp.finfo(scores.dtype).min)
        attn = jax.nn.softmax(scores, axis=-1)
        out = jnp.einsum('bkgts,bksd->bkgtd', attn, V)
        out = out.reshape(B, N_Q_HEAD, T, HEAD_SIZE).transpose(0, 2, 1, 3).reshape(B, T, N_Q_HEAD * HEAD_SIZE)
        return out @ Wp.T

    def _L1_xattn_ref(q, latent_kv, Wq, Wkv_expand, Wout):
        import jax, jax.numpy as jnp
        import numpy as np
        B, S, H, NH, L = (2, 256, 256, 16, 64)
        HD = H // NH
        b, sq, _ = q.shape
        sk = latent_kv.shape[1]
        qp = q @ Wq.T
        kv = latent_kv @ Wkv_expand.T
        k, v = jnp.split(kv, 2, axis=-1)
        qh = qp.reshape(b, sq, NH, HD).transpose(0, 2, 1, 3)
        kh = k.reshape(b, sk, NH, HD).transpose(0, 2, 1, 3)
        vh = v.reshape(b, sk, NH, HD).transpose(0, 2, 1, 3)
        inv_sqrt_d = 1.0 / jnp.sqrt(jnp.float32(HD))
        scores = jnp.einsum('bhqd,bhkd->bhqk', qh, kh) * inv_sqrt_d
        causal = jnp.tril(jnp.ones((sq, sk), dtype=bool))
        scores = jnp.where(causal, scores, jnp.finfo(scores.dtype).min)
        attn = jax.nn.softmax(scores, axis=-1)
        out = jnp.einsum('bhqk,bhkd->bhqd', attn, vh)
        out = out.transpose(0, 2, 1, 3).reshape(b, sq, H)
        return out @ Wout.T

    def _L1_ffn_ref(hidden_states, gate_weight, w_gate, w_up, w_down):
        import jax, jax.numpy as jnp
        import numpy as np
        B, S, H = (2, 256, 256)
        E, K, I = (64, 8, 96)

        def _moe_forward(hidden_states, gate_weight, w_gate, w_up, w_down):
            b, s, h = hidden_states.shape
            x = hidden_states.reshape(-1, h)
            logits = x.astype(jnp.float32) @ gate_weight.astype(jnp.float32).T
            scores = jax.nn.softmax(logits, axis=-1)
            topk_w, topk_idx = jax.lax.top_k(scores, K)
            topk_w = topk_w / jnp.sum(topk_w, axis=-1, keepdims=True)
            flat_ids = topk_idx.reshape(-1)
            expanded = jnp.repeat(x, K, axis=0)
            order = jnp.argsort(flat_ids)
            sorted_tokens = expanded[order]
            group_sizes = jnp.zeros((E,), jnp.int32).at[flat_ids].add(1)
            g = jax.lax.ragged_dot(sorted_tokens, w_gate, group_sizes)
            u = jax.lax.ragged_dot(sorted_tokens, w_up, group_sizes)
            out = jax.lax.ragged_dot(jax.nn.silu(g) * u, w_down, group_sizes)
            inv = jnp.argsort(order)
            outs = out[inv].reshape(-1, K, h)
            y = jnp.sum(outs * topk_w[:, :, None], axis=1)
            return y.reshape(b, s, h)
        return _moe_forward(hidden_states, gate_weight, w_gate, w_up, w_down)
    x = x + _L0_attn_ref(_layernorm(x, axis=-1), L0_attn_W_qkvz, L0_attn_W_ba, L0_attn_conv_w, L0_attn_dt_bias, L0_attn_A_log, L0_attn_norm_weight, L0_attn_W_out)
    x = x + _L0_xattn_ref(_layernorm(x, axis=-1), ctx_512, L0_xattn_Wq, L0_xattn_w_kc_q, L0_xattn_w_kc_kv, L0_xattn_W_qr, L0_xattn_W_kr, L0_xattn_Wo)
    x = x + _L0_ffn_ref(_layernorm(x, axis=-1), L0_ffn_w_gate, L0_ffn_w_up, L0_ffn_w_down)
    x = x + _L1_attn_ref(_layernorm(x, axis=-1), L1_attn_Wq, L1_attn_Wk, L1_attn_Wv, L1_attn_Wp)
    x = x + _L1_xattn_ref(_layernorm(x, axis=-1), ctx_512, L1_xattn_Wq, L1_xattn_Wkv_expand, L1_xattn_Wout)
    x = x + _L1_ffn_ref(_layernorm(x, axis=-1), L1_ffn_gate_weight, L1_ffn_w_gate, L1_ffn_w_up, L1_ffn_w_down)
    return x

_drawn_inputs = setup_inputs


def setup_inputs(seed=0):
    import zlib

    import numpy as np

    out = dict(_drawn_inputs(seed))
    spreads = {'L0_attn_dt_bias': (1.0, 0.6), 'L0_attn_norm_weight': (1.0, 0.6)}
    factors = {'L0_attn_W_ba': 8.0,
     'L0_attn_A_log': 8.0,
     'L1_xattn_Wq': 8.0,
     'L1_xattn_Wkv_expand': 3.05,
     'L1_xattn_Wout': 3.098,
     'L1_ffn_gate_weight': 8.0,
     'L1_ffn_w_gate': 8.0,
     'L1_ffn_w_up': 8.0,
     'L1_ffn_w_down': 8.0}
    for name, (base, spread) in spreads.items():
        noise = np.random.default_rng([zlib.crc32(name.encode()), seed]).standard_normal(out[name].shape)
        drawn = base * np.exp(spread * noise) if base else spread * noise
        out[name] = jnp.asarray(drawn.astype(out[name].dtype))
    for name, factor in factors.items():
        out[name] = (out[name] * factor).astype(out[name].dtype)
    return out
```

```python
from contextlib import ExitStack

import concourse.bass as bass
from concourse import mybir

F32 = mybir.dt.float32
ALU = mybir.AluOpType
ACT = mybir.ActivationFunctionType
AX_X = mybir.AxisListType.X

P = 128
B, SEQ, D = 4, 256, 256
NT = B * SEQ // P
KD = D // P
C = SEQ // P
NTOK = B * SEQ
BANK = 512


class Shared:

    def __init__(self, nc, ctx):
        self.nc, self.ctx = nc, ctx
        self.x = self.sb("x", [P, NT, D])
        self.xnT = self.sb("xnT", [P, KD, NTOK])
        self.ident = self.sb("ident", [P, 4, P])
        self.neghalf = self.sb("neghalf", [P, 16])
        self.sems = []
        self.bank = ctx.enter_context(nc.psum_tensor("bank", [P, 8, BANK], F32))

    def sb(self, name, shape):
        return self.ctx.enter_context(self.nc.sbuf_tensor(name, shape, F32))

    def sem(self, name):
        self.sems.append(self.nc.alloc_semaphore(name=name))
        return self.sems[-1]

    def end_layer(self):
        self.nc.clear_and_free_semaphores(self.sems)
        self.nc.all_engine_barrier()
        self.sems = []


def start(nc, m, x, ident4):
    s_load = m.sem("st_load")
    with nc.Block() as block:
        @block.sync
        def _(sp):
            for b in range(B):
                sp.dma_start(m.x[:, C * b:C * b + C, :], x[b].rearrange("(c p) d -> p c d", p=P)).then_inc(s_load, 16)
            sp.wait_ge(s_load, 16 * B + 16)

        @block.scalar
        def _(act):
            act.dma_start(m.ident[:], ident4.rearrange("p (n q) -> p n q", n=4)).then_inc(s_load, 16)

        @block.vector
        def _(dve):
            nc.vector.memset(m.neghalf[:], -0.5)


def finish(nc, m, out):
    s_out = m.sem("fin_out")
    with nc.Block() as block:
        @block.sync
        def _(sp):
            for b in range(B):
                sp.dma_start(out[b].rearrange("(c p) d -> p c d", p=P), m.x[:, C * b:C * b + C, :]).then_inc(s_out, 16)
            sp.wait_ge(s_out, 16 * B)


def layer_norm(nc, m, tag):
    s_stat, s_mv, s_eps, s_rstd = (m.sem(f"{tag}_{n}") for n in ("stat", "mv", "eps", "rstd"))
    s_xn, s_tr, s_copied = (m.sem(f"{tag}_{n}") for n in ("xn", "tr", "copied"))
    with ExitStack() as tmp:
        def sb(name, shape):
            return tmp.enter_context(nc.sbuf_tensor(f"{tag}_{name}", shape, F32))
        stat = sb("stats", [P, NT, 6])
        mv = sb("meanvar", [P, NT, 2])
        vare = sb("vare", [P, NT])
        rstd = sb("rstdv", [P, NT])
        xn = sb("xnorm", [P, NT, D])
        with nc.Block() as block:
            @block.vector
            def _(dve):
                for t in range(NT):
                    nc.vector.bn_stats(stat[:, t, :], m.x[:, t, :]).then_inc(s_stat, 1)
                for t in range(NT):
                    dve.wait_ge(s_stat, t + 1)
                    nc.vector.bn_aggr(mv[:, t, :], stat[:, t, :]).then_inc(s_mv, 1)
                dve.wait_ge(s_mv, NT)
                nc.vector.tensor_scalar(vare[:], mv[:, :, 1], 1e-5, None, ALU.add).then_inc(s_eps, 1)
                dve.wait_ge(s_rstd, 1)
                for t in range(NT):
                    nc.vector.tensor_scalar(xn[:, t, :], m.x[:, t, :], mv[:, t, 0:1], rstd[:, t:t + 1],
                                            ALU.subtract, ALU.mult).then_inc(s_xn, 1)

            @block.gpsimd
            def _(pool):
                pool.wait_ge(s_eps, 1)
                nc.gpsimd.tensor_tensor(rstd[:], vare[:], m.neghalf[:, 0:NT], ALU.pow).then_inc(s_rstd, 1)

            @block.tensor
            def _(pe):
                for t in range(NT):
                    pe.wait_ge(s_xn, t + 1)
                    for k in range(KD):
                        last = nc.tensor.transpose(m.bank[:, 2 * k + t // 4, P * (t % 4):P * (t % 4) + P],
                                                   xn[:, t, P * k:P * k + P], m.ident[:, 0, :])
                    last.then_inc(s_tr, 1)

            @block.scalar
            def _(act):
                for h in range(2):
                    act.wait_ge(s_tr, 4 * h + 4)
                    for k in range(KD):
                        nc.scalar.activation(m.xnT[:, k, BANK * h:BANK * h + BANK], m.bank[:, 2 * k + h, :],
                                             ACT.Copy).then_inc(s_copied, 1)
                act.wait_ge(s_copied, 2 * KD)


def two_slots(eng, n, lead, lag):
    lead(0, 0)
    with eng.Fori(0, n // 2 - 1) as p:
        lead(2 * p + 1, 1)
        lag(2 * p, 0)
        lead(2 * p + 2, 0)
        lag(2 * p + 1, 1)
    lead(n - 1, 1)
    lag(n - 2, 0)
    lag(n - 1, 1)


def gated_mlp(nc, m, tag, n, width, w_gate, w_up, w_down, weight=None):
    s_w = [m.sem(f"{tag}_w{s}") for s in range(2)]
    s_wd = [m.sem(f"{tag}_wd{s}") for s in range(2)]
    s_gu = m.sem(f"{tag}_gu")
    s_sg = m.sem(f"{tag}_sg")
    s_h = m.sem(f"{tag}_h")
    s_y = m.sem(f"{tag}_y")
    s_x = m.sem(f"{tag}_x")
    s_wc = m.sem(f"{tag}_wc")
    CY, CX, CH, CG = NT // 2, NT, 2, 4
    HALF = NTOK // 2
    with ExitStack() as tmp:
        def sb(name, shape):
            return tmp.enter_context(nc.sbuf_tensor(f"{tag}_{name}", shape, F32))
        wg = [sb(f"wg{s}", [P, KD, width]) for s in range(2)]
        wu = [sb(f"wu{s}", [P, KD, width]) for s in range(2)]
        wd = [sb(f"wd{s}", [width, D]) for s in range(2)]
        hT = [sb(f"hT{s}", [width, NTOK]) for s in range(2)]
        sg = sb("silu", [width, 2, HALF])
        wc = [sb(f"wc{s}", [P, NT]) for s in range(2)]

        def yb(t):
            return m.bank[:, 4 + t // 2, D * (t % 2):D * (t % 2) + D]

        with nc.Block() as block:
            @block.sync
            def _(sp):
                def load(e, s):
                    sp.wait_ge(s_gu, e * 2 - 2 + CG)
                    sp.dma_start(wg[s][:], w_gate[e]).then_inc(s_w[s], 16)
                    sp.dma_start(wu[s][:], w_up[e]).then_inc(s_w[s], 16)
                    if not (isinstance(e, int) and e == 0):
                        sp.wait_ge(s_y, e * (NT // 2) + CY - NT // 2)
                    sp.dma_start(wd[s][:], w_down[e]).then_inc(s_wd[s], 16)
                two_slots(sp, n, load, lambda e, s: None)

            @block.tensor
            def _(pe):
                pe.sem_inc(s_y, CY)
                pe.sem_inc(s_gu, CG)

                def gate_up(e, s):
                    pe.wait_ge(s_w[s], (e - s) * 16 + 32)
                    for hf in range(2):
                        pe.wait_ge(s_h, e * 2 - 1 + hf + CH)
                        for bank, w in ((hf, wg), (2 + hf, wu)):
                            for k in range(KD):
                                last = nc.tensor.matmul(m.bank[0:width, bank, :], w[s][:, k, :],
                                                        m.xnT[:, k, HALF * hf:HALF * hf + HALF],
                                                        start=(k == 0), stop=(k == KD - 1))
                        last.then_inc(s_gu, 1)

                def down(e, s):
                    pe.wait_ge(s_wd[s], (e - s) * 8 + 16)
                    for t in range(NT):
                        if t % 4 == 0:
                            pe.wait_ge(s_h, e * 2 + t // 4 + 1 + CH)
                        if t % 2 == 0:
                            pe.wait_ge(s_x, e * NT - NT + t + 2 + CX)
                        last = nc.tensor.matmul(yb(t), hT[s][:, P * t:P * t + P], wd[s][:], start=True, stop=True)
                        if t % 2:
                            last.then_inc(s_y, 1)
                two_slots(pe, n, gate_up, down)

            @block.scalar
            def _(act):
                def silu(e, s):
                    for hf in range(2):
                        act.wait_ge(s_gu, e * 2 + hf + 1 + CG)
                        act.wait_ge(s_h, e * 2 - 1 + hf + CH)
                        nc.scalar.activation(sg[:, hf, :], m.bank[0:width, hf, :], ACT.Silu).then_inc(s_sg, 1)
                two_slots(act, n, silu, lambda e, s: None)

            @block.vector
            def _(dve):
                dve.sem_inc(s_h, CH)
                dve.sem_inc(s_x, CX)

                def hidden(e, s):
                    for hf in range(2):
                        dve.wait_ge(s_sg, e * 2 + hf + 1)
                        if not (isinstance(e, int) and e == 0):
                            dve.wait_ge(s_y, e * (NT // 2) + CY - NT // 2)
                        nc.vector.tensor_tensor(hT[s][:, HALF * hf:HALF * hf + HALF], m.bank[0:width, 2 + hf, :],
                                                sg[:, hf, :], ALU.mult).then_inc(s_h, 1)

                def add(e, s):
                    if weight is not None:
                        dve.wait_ge(s_wc, e + 1)
                    for t in range(NT):
                        if t % 2 == 0:
                            dve.wait_ge(s_y, e * (NT // 2) + t // 2 + 1 + CY)
                        dve.wait_ge(s_x, e * NT - NT + t + 1 + CX)
                        if weight is None:
                            nc.vector.tensor_tensor(m.x[:, t, :], yb(t), m.x[:, t, :], ALU.add).then_inc(s_x, 1)
                        else:
                            nc.vector.scalar_tensor_tensor(out=m.x[:, t, :], in0=yb(t), scalar=wc[s][:, t:t + 1],
                                                           in1=m.x[:, t, :], op0=ALU.mult,
                                                           op1=ALU.add).then_inc(s_x, 1)
                two_slots(dve, n, hidden, add)

            if weight is not None:
                @block.gpsimd
                def _(pool):
                    def pick(e, s):
                        if not (isinstance(e, int) and e == 0):
                            pool.wait_ge(s_x, e * NT - NT + CX)
                        nc.gpsimd.tensor_copy(wc[s][:], weight[:, :, e]).then_inc(s_wc, 1)
                    two_slots(pool, n, pick, lambda e, s: None)


def route(nc, m, gate_w, weight):
    E, TOP = 64, 8
    s_in, s_lg, s_cp, s_mx, s_rep, s_sel, s_sub, s_exp, s_em, s_sum, s_rec, s_w = (
        m.sem(f"rt_{n}") for n in ("in", "lg", "cp", "mx", "rep", "sel", "sub", "exp", "em", "sum", "rec", "w"))
    with ExitStack() as tmp:
        def sb(name, shape):
            return tmp.enter_context(nc.sbuf_tensor(f"rt_{name}", shape, F32))
        gw = sb("gw", [P, KD, E])
        lg = sb("logits", [P, NT, E])
        top = sb("top", [P, NT, TOP])
        rest = sb("rest", [P, NT, E])
        sel = sb("sel", [P, NT, E])
        ex = sb("ex", [P, NT, E])
        em = sb("em", [P, NT, E])
        tot = sb("tot", [P, NT])
        rec = sb("rec", [P, NT])
        lgp = m.bank[:, 0, :].rearrange("p (t e) -> p t e", e=E)
        with nc.Block() as block:
            @block.sync
            def _(sp):
                sp.dma_start(gw[:], gate_w).then_inc(s_in, 16)

            @block.tensor
            def _(pe):
                pe.wait_ge(s_in, 16)
                for t in range(NT):
                    for k in range(KD):
                        last = nc.tensor.matmul(lgp[:, t, :], m.xnT[:, k, P * t:P * t + P], gw[:, k, :],
                                                start=(k == 0), stop=(k == KD - 1))
                last.then_inc(s_lg, 1)

            @block.vector
            def _(dve):
                dve.wait_ge(s_lg, 1)
                nc.vector.tensor_copy(lg[:], lgp).then_inc(s_cp, 1)
                dve.wait_ge(s_cp, 1)
                for t in range(NT):
                    nc.vector.max(top[:, t, :], lg[:, t, :]).then_inc(s_mx, 1)
                for t in range(NT):
                    dve.wait_ge(s_mx, t + 1)
                    nc.vector.match_replace(rest[:, t, :], top[:, t, :], lg[:, t, :], -3.0e38).then_inc(s_rep, 1)
                dve.wait_ge(s_rep, NT)
                nc.vector.tensor_tensor(sel[:], rest[:], lg[:], ALU.not_equal).then_inc(s_sel, 1)
                nc.vector.tensor_tensor(ex[:], lg[:], top[:, :, 0:1].to_broadcast([P, NT, E]),
                                        ALU.subtract).then_inc(s_sub, 1)
                dve.wait_ge(s_exp, 1)
                dve.wait_ge(s_sel, 1)
                nc.vector.tensor_tensor(em[:], ex[:], sel[:], ALU.mult).then_inc(s_em, 1)
                dve.wait_ge(s_em, 1)
                nc.vector.tensor_reduce(tot[:], em[:], AX_X, ALU.add).then_inc(s_sum, 1)
                dve.wait_ge(s_sum, 1)
                nc.vector.reciprocal(rec[:], tot[:]).then_inc(s_rec, 1)
                dve.wait_ge(s_rec, 1)
                nc.vector.tensor_tensor(weight[:], em[:], rec[:].unsqueeze(2).to_broadcast([P, NT, E]),
                                        ALU.mult).then_inc(s_w, 1)

            @block.scalar
            def _(act):
                act.wait_ge(s_sub, 1)
                nc.scalar.activation(ex[:], ex[:], ACT.Exp).then_inc(s_exp, 1)



def causal_attention(nc, m, tag, wq, wk, wv, wo, ctxT, cos, sin):
    G, GH, HD = wq.shape[0], 4, 16
    NV = wq.shape[3]
    VH = wv.shape[3] // HD
    SCALE = float(HD) ** -0.5
    KC, SK = (wk.shape[2], wk.shape[1])
    HALF = NTOK // 2
    E = GH * HD
    W = P + 2 * P
    s_w, s_wo, s_cst = m.sem(f"{tag}_w"), m.sem(f"{tag}_wo"), m.sem(f"{tag}_cst")
    s_proj = m.sem(f"{tag}_proj")
    s_pair = m.sem(f"{tag}_pair")
    s_qk = m.sem(f"{tag}_qk")
    s_v, s_vc = m.sem(f"{tag}_v"), m.sem(f"{tag}_vc")
    s_sc, s_ms = m.sem(f"{tag}_sc"), m.sem(f"{tag}_ms")
    s_nm, s_ex = m.sem(f"{tag}_nm"), m.sem(f"{tag}_ex")
    s_pt, s_ptc = m.sem(f"{tag}_pt"), m.sem(f"{tag}_ptc")
    s_pv, s_rc, s_o = m.sem(f"{tag}_pv"), m.sem(f"{tag}_rc"), m.sem(f"{tag}_o")
    s_ot, s_otc = m.sem(f"{tag}_ot"), m.sem(f"{tag}_otc")
    s_y, s_x = m.sem(f"{tag}_y"), m.sem(f"{tag}_x")
    s_one, s_mask = m.sem(f"{tag}_one"), m.sem(f"{tag}_mask")
    CPT, CPV, COT, CY, CSC, CQK, CX, CV = 6, 1, 1, 4, 4, 2, 4, 1
    with ExitStack() as tmp:
        def sb(name, shape):
            return tmp.enter_context(nc.sbuf_tensor(f"{tag}_{name}", shape, F32))
        wq_sb = sb("wq", [P, KD, NV, P])
        wk_sb = sb("wk", [SK, KC, NV, P])
        wv_sb = sb("wv", [SK, KC, VH * HD])
        wo_sb = sb("wo", [2 * E, D])
        qkT = [sb("qT", [P, NTOK]), sb("kT", [P, NTOK])]
        prod = sb("prod", [P, 2, 2, HALF])
        V = sb("V", [P, NT, VH, HD + 1])
        S = sb("S", [P, 2, GH, W])
        nm = sb("nm", [P, 2, GH, 2])
        PT = sb("PT", [P, 3, GH, P])
        rec = sb("rec", [P, 2, GH, 1])
        O = sb("O", [P, NT, GH, HD])
        OT = sb("OT", [2 * E, NTOK // 2])
        mask = sb("mask", [P, W])
        if ctxT is not None:
            src = sb("ctxT", [SK, 1, NTOK])
        else:
            src = m.xnT
            cs = [sb("cos", [P, SEQ]), sb("sin", [P, SEQ])]
        pvb = m.bank[:, 7, 0:2 * GH * (HD + 1)].rearrange("p (c r d) -> p c r d", c=2, r=GH)
        PROJ = [(0, 0), (0, 1), (1, 0), (1, 1)]

        with nc.Block() as block:
            @block.sync
            def _(sp):
                if ctxT is not None:
                    sp.dma_start(src[:, 0, :], ctxT).then_inc(s_cst, 16)
                else:
                    sp.dma_start(cs[0][:], cos).then_inc(s_cst, 16)
                    sp.dma_start(cs[1][:], sin).then_inc(s_cst, 16)
                with sp.Fori(0, G) as g:
                    sp.wait_ge(s_v, g + CV)
                    sp.dma_start(wq_sb[:], wq[g]).then_inc(s_w, 16)
                    sp.dma_start(wk_sb[:], wk[g]).then_inc(s_w, 16)
                    sp.dma_start(wv_sb[:], wv[g]).then_inc(s_w, 16)
                    sp.wait_ge(s_y, g * 4 + CY)
                    for par in range(2):
                        sp.dma_start(wo_sb[E * par:E * par + E, :], wo[g]).then_inc(s_wo, 16)

            @block.gpsimd
            def _(pool):
                nc.gpsimd.memset(mask[:], 0.0).then_inc(s_mask, 1)
                pool.wait_ge(s_mask, 1)
                for o in (0, 2 * P):
                    nc.gpsimd.affine_select(out=mask[:, o:o + P], in_=mask[:, o:o + P], compare_op=ALU.is_ge,
                                            fill=-3.0e38, base=0, pattern=[[-1, P]],
                                            channel_multiplier=1).then_inc(s_mask, 1)
                nc.gpsimd.memset(V[:, :, :, HD:HD + 1], 1.0).then_inc(s_one, 1)
                if cos is not None:
                    pool.sem_inc(s_qk, CQK)
                    with pool.Fori(0, G) as g:
                        for j, (a, hf) in enumerate(PROJ):
                            pool.wait_ge(s_pair, g * 4 + j + 1)
                            pool.wait_ge(s_sc, g * 4 + CSC)
                            nc.gpsimd.tensor_tensor(qkT[a][:, HALF * hf:HALF * hf + HALF], prod[:, j % 2, 0, :],
                                                    prod[:, j % 2, 1, :], ALU.add).then_inc(s_qk, 1)

            @block.tensor
            def _(pe):
                pe.sem_inc(s_pt, CPT)
                pe.sem_inc(s_pv, CPV)
                pe.sem_inc(s_ot, COT)
                pe.sem_inc(s_y, CY)
                pe.sem_inc(s_sc, CSC)
                pe.sem_inc(s_v, CV)

                def scores(g, b):
                    if b:
                        pe.wait_ge(s_ms, g * 4 + b)
                    for r in range(GH):
                        q = qkT[0][32 * r:32 * r + HD, SEQ * b:SEQ * b + SEQ]
                        k = qkT[1][32 * r:32 * r + HD, SEQ * b:SEQ * b + SEQ]
                        nc.tensor.matmul(m.bank[:, r, 0:P], q[:, 0:P], k[:, 0:P], start=True, stop=True)
                        last = nc.tensor.matmul(m.bank[:, r, P:W], q[:, P:SEQ], k, start=True, stop=True)
                    last.then_inc(s_sc, 1)

                pe.wait_ge(s_cst, 16 if ctxT is not None else 32)
                with pe.Fori(0, G) as g:
                    pe.wait_ge(s_w, g * 48 + 48)
                    pe.wait_ge(s_x, g * 4 + CX)
                    for j, (a, hf) in enumerate(PROJ):
                        w, s, kt = (wq_sb, m.xnT, KD) if a == 0 else (wk_sb, src, KC)
                        for v in range(NV):
                            for k in range(kt):
                                last = nc.tensor.matmul(m.bank[:, 2 * j + v, :], w[:, k, v, :],
                                                        s[:, k, HALF * hf:HALF * hf + HALF],
                                                        start=(k == 0), stop=(k == kt - 1))
                        last.then_inc(s_proj, 1)
                    pe.wait_ge(s_pair, g * 4 + 1)
                    for t in range(NT):
                        for k in range(KC):
                            last = nc.tensor.matmul(m.bank[:, 0, VH * HD * t:VH * HD * t + VH * HD],
                                                    src[:, k, P * t:P * t + P], wv_sb[:, k, :],
                                                    start=(k == 0), stop=(k == KC - 1))
                    last.then_inc(s_v, 1)
                    pe.wait_ge(s_vc, g + 1)
                    pe.wait_ge(s_pair, g * 4 + 4)
                    pe.wait_ge(s_qk, g * 4 + 4 + CQK)
                    scores(g, 0)
                    for b in range(B):
                        if b + 1 < B:
                            scores(g, b + 1)
                        pe.wait_ge(s_ex, g * 4 + b + 1)
                        for n in range(3):
                            if b:
                                pe.wait_ge(s_ptc, g * 12 + 3 * b - 2 + n)
                            for r in range(GH):
                                last = nc.tensor.transpose(m.bank[:, 4 + n, P * r:P * r + P],
                                                           S[:, b % 2, r, P * n:P * n + P], m.ident[:, 0, :])
                            last.then_inc(s_pt, 1)
                        pe.wait_ge(s_ptc, g * 12 + 3 * b + 3)
                        if b:
                            pe.wait_ge(s_o, g * 4 + b)
                        for r in range(GH):
                            vr = min(r, VH - 1)
                            nc.tensor.matmul(pvb[:, 0, r, :], PT[:, 0, r, :], V[:, 2 * b, vr, :],
                                             start=True, stop=True)
                            nc.tensor.matmul(pvb[:, 1, r, :], PT[:, 1, r, :], V[:, 2 * b, vr, :],
                                             start=True, stop=False)
                            last = nc.tensor.matmul(pvb[:, 1, r, :], PT[:, 2, r, :], V[:, 2 * b + 1, vr, :],
                                                    start=False, stop=True)
                        last.then_inc(s_pv, 1)
                    pe.wait_ge(s_o, g * 4 + 4)
                    for n in range(NT // 2):
                        last = nc.tensor.transpose(m.bank[:, 4, P * n:P * n + P],
                                                   O[:, 2 * n:2 * n + 2, :, :].rearrange("p t r d -> p (t r d)"),
                                                   m.ident[:, 0, :])
                    last.then_inc(s_ot, 1)
                    pe.wait_ge(s_wo, g * 32 + 32)
                    pe.wait_ge(s_otc, g + 1)
                    for q in range(4):
                        par, hi = q // 2, q % 2
                        for j in range(2):
                            n = 2 * hi + j
                            last = nc.tensor.matmul(m.bank[:, q, D * j:D * j + D],
                                                    OT[E * par:E * par + E, P * n:P * n + P],
                                                    wo_sb[E * par:E * par + E, :], start=True, stop=True)
                        last.then_inc(s_y, 1)

            @block.scalar
            def _(act):
                act.wait_ge(s_one, 1)
                if cos is None:
                    act.sem_inc(s_qk, CQK)
                with act.Fori(0, G) as g:
                    if cos is None:
                        for j, (a, hf) in enumerate(PROJ):
                            act.wait_ge(s_proj, g * 4 + j + 1)
                            act.wait_ge(s_sc, g * 4 + CSC)
                            nc.scalar.activation(qkT[a][:, HALF * hf:HALF * hf + HALF], m.bank[:, 2 * j, :],
                                                 ACT.Copy).then_inc(s_qk, 1)
                            act.wait_ge(s_qk, g * 4 + j + 1 + CQK)
                            act.sem_inc(s_pair, 1)
                    act.wait_ge(s_v, g + 1 + CV)
                    act.wait_ge(s_pv, g * 4 + CPV)
                    nc.scalar.activation(V[:, :, :, 0:HD],
                                         m.bank[:, 0, 0:NT * VH * HD].rearrange("p (t r d) -> p t r d", t=NT, r=VH),
                                         ACT.Copy).then_inc(s_vc, 1)
                    for b in range(B):
                        act.wait_ge(s_nm, g * 4 + b + 1)
                        for r in range(GH):
                            for c in range(2):
                                s = S[:, b % 2, r, P * c:P + 2 * P * c]
                                last = nc.scalar.activation(s, s, ACT.Exp, bias=nm[:, b % 2, r, c:c + 1])
                        last.then_inc(s_ex, 1)
                        act.wait_ge(s_pv, g * 4 + b + CPV)
                        for n in range(3):
                            act.wait_ge(s_pt, g * 12 + 3 * b + n + 1 + CPT)
                            nc.scalar.activation(PT[:, n, :, :], m.bank[:, 4 + n, :].rearrange("p (r t) -> p r t", r=GH),
                                                 ACT.Copy).then_inc(s_ptc, 1)
                    act.wait_ge(s_ot, g + 1 + COT)
                    act.wait_ge(s_y, g * 4 + CY)
                    nc.scalar.activation(OT[:], m.bank[:, 4, :], ACT.Copy).then_inc(s_otc, 1)

            @block.vector
            def _(dve):
                dve.sem_inc(s_x, CX)
                dve.wait_ge(s_mask, 3)

                def softmax_in(g, b):
                    dve.wait_ge(s_sc, g * 4 + b + 1 + CSC)
                    dve.wait_ge(s_pt, g * 12 + 3 * b - 3 + CPT)
                    nc.vector.scalar_tensor_tensor(out=S[:, b % 2, :, :], in0=m.bank[:, 0:GH, 0:W], scalar=SCALE,
                                                   in1=mask[:].unsqueeze(1).to_broadcast([P, GH, W]),
                                                   op0=ALU.mult, op1=ALU.add).then_inc(s_ms, 1)
                    dve.wait_ge(s_ms, g * 4 + b + 1)
                    for c in range(2):
                        last = nc.vector.tensor_reduce(nm[:, b % 2, :, c], S[:, b % 2, :, P * c:P + 2 * P * c],
                                                       AX_X, ALU.max, negate=True)
                    last.then_inc(s_nm, 1)

                def normalise(g, b):
                    dve.wait_ge(s_pv, g * 4 + b + 1 + CPV)
                    dve.wait_ge(s_ot, g + COT)
                    nc.vector.reciprocal(rec[:], pvb[:, :, :, HD:HD + 1]).then_inc(s_rc, 1)
                    dve.wait_ge(s_rc, g * 4 + b + 1)
                    nc.vector.tensor_tensor(O[:, 2 * b:2 * b + 2, :, :], pvb[:, :, :, 0:HD],
                                            rec[:].to_broadcast([P, 2, GH, HD]), ALU.mult).then_inc(s_o, 1)

                if cos is not None:
                    dve.wait_ge(s_cst, 32)
                with dve.Fori(0, G) as g:
                    if cos is not None:
                        for j in range(4):
                            dve.wait_ge(s_proj, g * 4 + j + 1)
                            dve.wait_ge(s_qk, g * 4 + j - 1 + CQK)
                            for v in range(2):
                                last = nc.vector.tensor_tensor(
                                    prod[:, j % 2, v, :].rearrange("p (b t) -> p b t", b=2),
                                    m.bank[:, 2 * j + v, :].rearrange("p (b t) -> p b t", b=2),
                                    cs[v][:].unsqueeze(1).to_broadcast([P, 2, SEQ]), ALU.mult)
                            last.then_inc(s_pair, 1)
                    softmax_in(g, 0)
                    for b in range(B):
                        if b + 1 < B:
                            softmax_in(g, b + 1)
                        normalise(g, b)
                    for q in range(4):
                        dve.wait_ge(s_y, g * 4 + q + 1 + CY)
                        dve.wait_ge(s_x, g * 4 - 4 + q + 1 + CX)
                        t = 4 * (q % 2) + q // 2
                        nc.vector.tensor_tensor(m.x[:, t:t + 3:2, :], m.bank[:, q, :].rearrange("p (t n) -> p t n", t=2),
                                                m.x[:, t:t + 3:2, :], ALU.add).then_inc(s_x, 1)



def latent_attention(nc, m, d):
    L, LEN = 64, d["mla_ctxT"].shape[2]
    R, CQ, HK = 64, 192, P
    PAIRS = 8
    LT = (LEN + P - 1) // P
    LAST = LEN - (LT - 1) * P
    UNITS = 2 * NT
    CUT = 2 * BANK
    PART = [(0, CUT), (CUT, LEN)]
    GROUPS = [range(n, min(n + 4, LT)) for n in range(0, LT, 4)]
    names = ("w c1 c2 c3 c4 e1 e2 e3 e4 q qc sc nh nm ex tr pa pd pv rc cn ct ctc y x "
             "kin kc ks kt tin tc ts tt one")
    (s_w, s_c1, s_c2, s_c3, s_c4, s_e1, s_e2, s_e3, s_e4, s_q, s_qc, s_sc, s_nh, s_nm, s_ex, s_tr, s_pa, s_pd,
     s_pv, s_rc, s_cn, s_ct, s_ctc, s_y, s_x, s_kin, s_kc, s_ks, s_kt, s_tin, s_tc, s_ts, s_tt, s_one) = (
        m.sem(f"mla_{n}") for n in names.split())
    CX, CTR, CE3 = 4, 8, 1
    with ExitStack() as tmp:
        def sb(name, shape):
            return tmp.enter_context(nc.sbuf_tensor(f"mla_{name}", shape, F32))
        kvT = sb("kvT", [P, B, LEN])
        kv = sb("kv", [P, B, LT, L + 1])
        cosT, sinT = sb("cosT", [P, LEN]), sb("sinT", [P, LEN])
        swT = sb("swT", [P, 2, LEN])
        cosk, sink = sb("cosk", [P, LT, L]), sb("sink", [P, LT, L])
        raw = sb("raw", [P, 2, LT, L])
        swk = sb("swk", [P, 2, LT, L])
        wqr, wkr = sb("wqr", [R, 2, CQ]), sb("wkr", [R, 2, L])
        wcqA, wcqB = sb("wcqA", [P, 2, HK]), sb("wcqB", [CQ - P, 2, HK])
        wq, wkv, wo = sb("wq", [HK, 2, D]), sb("wkv", [HK, 2, L]), sb("wo", [HK, 2, D])
        f1A, f1B, f2 = sb("f1A", [P, 2, L]), sb("f1B", [CQ - P, 2, L]), sb("f2", [HK, 2, L])
        wfold = sb("wfold", [P, KD, 2 * L])
        wout = sb("wout", [2 * L, D])
        qT = sb("qT", [P, NTOK])
        prob = sb("prob", [P, 2, LEN])
        nh, nm = sb("nh", [P, 2, 2]), sb("nm", [P, 2])
        PT = sb("PT", [P, 2, LT, P])
        rec = sb("rec", [P, 1])
        cn = sb("cn", [P, NT, 2 * L])
        cT = sb("cT", [P, NTOK])
        sc = m.bank[:, 0:4, :].rearrange("p b n -> p (b n)")

        with nc.Block() as block:
            @block.sync
            def _(sp):
                sp.dma_start(cosT[:], d["mla_cosT"]).then_inc(s_kin, 16)
                sp.dma_start(sinT[:], d["mla_sinT"]).then_inc(s_kin, 16)
                for b in range(B):
                    sp.dma_start(kvT[:, b, :], d["mla_ctxT"][b]).then_inc(s_kin, 16)
                    if b >= 2:
                        sp.wait_ge(s_kt, b - 1)
                    sp.dma_start(swT[:, b % 2, :], d["mla_swT"][b]).then_inc(s_kin, 16)
                    sp.wait_ge(s_kin, 32 * b + 64)
                with sp.Fori(0, PAIRS) as i:
                    sp.wait_ge(s_c3, i + CE3)
                    for dst, src in ((wqr, "wqr"), (wkr, "wkr"), (wcqA, "wcqA"), (wcqB, "wcqB"), (wq, "wq"),
                                     (wkv, "wkv"), (wo, "wo")):
                        sp.dma_start(dst[:], d["mla_" + src][i]).then_inc(s_w, 16)

            @block.gpsimd
            def _(pool):
                nc.gpsimd.memset(kv[:, :, :, L:L + 1], 1.0).then_inc(s_one, 1)
                pool.dma_start(cosk[:], d["mla_cosk"]).then_inc(s_tin, 16)
                pool.dma_start(sink[:], d["mla_sink"]).then_inc(s_tin, 16)
                for b in range(B):
                    if b >= 2:
                        pool.wait_ge(s_tt, b - 1)
                    pool.dma_start(raw[:, b % 2, :, :], d["mla_ctxk"][b]).then_inc(s_tin, 16)
                    pool.dma_start(swk[:, b % 2, :, :], d["mla_swk"][b]).then_inc(s_tin, 16)
                    pool.wait_ge(s_tin, 32 * b + 64)
                    nc.gpsimd.tensor_tensor(raw[:, b % 2, :, :], raw[:, b % 2, :, :], cosk[:], ALU.mult).then_inc(s_tc, 1)
                    nc.gpsimd.tensor_tensor(swk[:, b % 2, :, :], swk[:, b % 2, :, :], sink[:], ALU.mult).then_inc(s_ts, 1)
                    pool.wait_ge(s_tc, b + 1)
                    pool.wait_ge(s_ts, b + 1)
                    nc.gpsimd.tensor_tensor(kv[:, b, :, 0:L], raw[:, b % 2, :, :], swk[:, b % 2, :, :],
                                            ALU.add).then_inc(s_tt, 1)

            @block.tensor
            def _(pe):
                pe.sem_inc(s_tr, CTR)
                pe.sem_inc(s_c3, CE3)

                def scores(i, u):
                    t, par = u // 2, u % 2
                    for h, (lo, hi) in enumerate(PART):
                        if u:
                            pe.wait_ge(s_ex, i * 2 * UNITS + 2 * u - 1 + h)
                        for n in range(lo, hi, BANK):
                            e = min(n + BANK, hi)
                            last = nc.tensor.matmul(sc[:, n:e], qT[L * par:L * par + L, P * t:P * t + P],
                                                    kvT[L * par:L * par + L, t // C, n:e], start=True, stop=True)
                        last.then_inc(s_sc, 1)

                def transposes(i, v):
                    pe.wait_ge(s_ex, i * 2 * UNITS + 2 * v + 2)
                    for n, tiles in enumerate(GROUPS):
                        if n == 0 and v:
                            pe.wait_ge(s_pd, i * 2 * UNITS + 2 * v)
                        if n == 2 and v:
                            pe.wait_ge(s_pa, i * 2 * UNITS + 2 * v)
                        if n == 3:
                            pe.wait_ge(s_pa, i * 2 * UNITS + 2 * v + 1)
                        for a, lt in enumerate(tiles):
                            k = min(P, LEN - P * lt)
                            last = nc.tensor.transpose(m.bank[0:k, 4 + n % 3, P * a:P * a + P],
                                                       prob[:, v % 2, P * lt:P * lt + k], m.ident[:, 0, :])
                        last.then_inc(s_tr, 1)

                def context(i, v):
                    pe.wait_ge(s_pa, i * 2 * UNITS + 2 * v + 2)
                    pe.wait_ge(s_pd, i * 2 * UNITS + 2 * v + 2)
                    if v:
                        pe.wait_ge(s_cn, i * UNITS + v)
                    for lt in range(LT):
                        k = min(P, LEN - P * lt)
                        last = nc.tensor.matmul(m.bank[:, 7, 0:L + 1], PT[0:k, v % 2, lt, :],
                                                kv[0:k, v // (2 * C), lt, :], start=(lt == 0), stop=(lt == LT - 1))
                    last.then_inc(s_pv, 1)

                with pe.Fori(0, PAIRS) as i:
                    pe.wait_ge(s_w, i * 112 + 112)
                    pe.wait_ge(s_x, i * 4 + CX)
                    for h in range(2):
                        nc.tensor.matmul(m.bank[:, 0, L * h:L * h + L], wqr[:, h, 0:P], wkr[:, h, :],
                                         start=True, stop=True)
                        last = nc.tensor.matmul(m.bank[0:CQ - P, 0, 2 * L + L * h:3 * L + L * h], wqr[:, h, P:CQ],
                                                wkr[:, h, :], start=True, stop=True)
                    last.then_inc(s_c1, 1)
                    for h in range(2):
                        last = nc.tensor.matmul(m.bank[L * h:L * h + L, 3, 0:D], wkv[:, h, :], wo[:, h, :],
                                                start=True, stop=True)
                    last.then_inc(s_c4, 1)
                    pe.wait_ge(s_e1, i + 1)
                    for h in range(2):
                        nc.tensor.matmul(m.bank[:, 1, L * h:L * h + L], wcqA[:, h, :], f1A[:, h, :],
                                         start=True, stop=False)
                        last = nc.tensor.matmul(m.bank[:, 1, L * h:L * h + L], wcqB[:, h, :], f1B[:, h, :],
                                                start=False, stop=True)
                    last.then_inc(s_c2, 1)
                    pe.wait_ge(s_e2, i + 1)
                    for k in range(KD):
                        for h in range(2):
                            n = 2 * L * k + L * h
                            last = nc.tensor.matmul(m.bank[:, 2, n:n + L], wq[:, h, P * k:P * k + P], f2[:, h, :],
                                                    start=True, stop=True)
                    last.then_inc(s_c3, 1)
                    pe.wait_ge(s_e3, i + 1)
                    for hf in range(2):
                        for k in range(KD):
                            last = nc.tensor.matmul(m.bank[:, 4 + hf, :], wfold[:, k, :],
                                                    m.xnT[:, k, BANK * hf:BANK * hf + BANK],
                                                    start=(k == 0), stop=(k == KD - 1))
                        last.then_inc(s_q, 1)
                    pe.wait_ge(s_qc, i * 2 + 2)
                    pe.wait_ge(s_kt, B)
                    pe.wait_ge(s_tt, B)
                    for u in range(UNITS + 2):
                        if u < UNITS:
                            scores(i, u)
                        if 1 <= u <= UNITS:
                            transposes(i, u - 1)
                        if u >= 2:
                            context(i, u - 2)
                    pe.wait_ge(s_cn, i * UNITS + UNITS)
                    for t in range(NT):
                        last = nc.tensor.transpose(m.bank[:, 4 + t // 4, P * (t % 4):P * (t % 4) + P], cn[:, t, :],
                                                   m.ident[:, 0, :])
                        if t % 4 == 3:
                            last.then_inc(s_ct, 1)
                    for t in range(NT):
                        if t % 4 == 0:
                            pe.wait_ge(s_ctc, i * 2 + t // 4 + 1)
                        last = nc.tensor.matmul(m.bank[:, t // 2, D * (t % 2):D * (t % 2) + D], cT[:, P * t:P * t + P],
                                                wout[:], start=True, stop=True)
                        if t % 2:
                            last.then_inc(s_y, 1)

            @block.scalar
            def _(act):
                with act.Fori(0, PAIRS) as i:
                    act.wait_ge(s_c1, i + 1)
                    nc.scalar.activation(f1A[:], m.bank[:, 0, 0:2 * L].rearrange("p (h n) -> p h n", h=2), ACT.Copy)
                    nc.scalar.activation(f1B[:], m.bank[0:CQ - P, 0, 2 * L:4 * L].rearrange("p (h n) -> p h n", h=2),
                                         ACT.Copy).then_inc(s_e1, 1)
                    act.wait_ge(s_c4, i + 1)
                    nc.scalar.activation(wout[:], m.bank[:, 3, 0:D], ACT.Copy).then_inc(s_e4, 1)
                    act.wait_ge(s_c2, i + 1)
                    nc.scalar.activation(f2[:], m.bank[:, 1, 0:2 * L].rearrange("p (h n) -> p h n", h=2),
                                         ACT.Copy).then_inc(s_e2, 1)
                    act.wait_ge(s_c3, i + 1 + CE3)
                    nc.scalar.activation(wfold[:], m.bank[:, 2, 0:KD * 2 * L].rearrange("p (k n) -> p k n", k=KD),
                                         ACT.Copy).then_inc(s_e3, 1)
                    for hf in range(2):
                        act.wait_ge(s_q, i * 2 + hf + 1)
                        nc.scalar.activation(qT[:, BANK * hf:BANK * hf + BANK], m.bank[:, 4 + hf, :],
                                             ACT.Copy).then_inc(s_qc, 1)

                    def copy(v, n):
                        act.wait_ge(s_tr, i * 4 * UNITS + 4 * v + n + 1 + CTR)
                        nc.scalar.activation(PT[:, v % 2, 4 * n:4 * n + 4, :],
                                             m.bank[:, 4 + n, :].rearrange("p (a t) -> p a t", a=4),
                                             ACT.Copy).then_inc(s_pa, 1)
                    for u in range(UNITS + 1):
                        if u:
                            if u > 2:
                                act.wait_ge(s_pv, i * UNITS + u - 2)
                            copy(u - 1, 0)
                        if u < UNITS:
                            act.wait_ge(s_nm, i * UNITS + u + 1)
                            act.wait_ge(s_tr, i * 4 * UNITS + 4 * u - 4 + CTR)
                            for lo, hi in PART:
                                nc.scalar.activation(prob[:, u % 2, lo:hi], sc[:, lo:hi], ACT.Exp,
                                                     bias=nm[:, u % 2:u % 2 + 1]).then_inc(s_ex, 1)
                        if u:
                            copy(u - 1, 2)
                    for hf in range(2):
                        act.wait_ge(s_ct, i * 2 + hf + 1)
                        nc.scalar.activation(cT[:, BANK * hf:BANK * hf + BANK], m.bank[:, 4 + hf, :],
                                             ACT.Copy).then_inc(s_ctc, 1)

            @block.vector
            def _(dve):
                dve.sem_inc(s_x, CX)
                for b in range(B):
                    dve.wait_ge(s_kin, 32 * b + 64)
                    nc.vector.tensor_tensor(kvT[:, b, :], kvT[:, b, :], cosT[:], ALU.mult).then_inc(s_kc, 1)
                    nc.vector.tensor_tensor(swT[:, b % 2, :], swT[:, b % 2, :], sinT[:], ALU.mult).then_inc(s_ks, 1)
                    dve.wait_ge(s_kc, b + 1)
                    dve.wait_ge(s_ks, b + 1)
                    nc.vector.tensor_tensor(kvT[:, b, :], kvT[:, b, :], swT[:, b % 2, :], ALU.add).then_inc(s_kt, 1)
                with dve.Fori(0, PAIRS) as i:
                    def copy(v, n):
                        dve.wait_ge(s_tr, i * 4 * UNITS + 4 * v + n + 1 + CTR)
                        if n < 3:
                            nc.vector.tensor_copy(PT[:, v % 2, 4 * n:4 * n + 4, :],
                                                  m.bank[:, 4 + n, :].rearrange("p (a t) -> p a t", a=4)).then_inc(s_pd, 1)
                        else:
                            nc.vector.tensor_copy(PT[0:LAST, v % 2, LT - 1, :], m.bank[0:LAST, 4, 0:P]).then_inc(s_pd, 1)
                    for u in range(UNITS + 2):
                        if u < UNITS:
                            for h, (lo, hi) in enumerate(PART):
                                dve.wait_ge(s_sc, i * 2 * UNITS + 2 * u + h + 1)
                                nc.vector.tensor_reduce(nh[:, u % 2, h:h + 1], sc[:, lo:hi], AX_X, ALU.max,
                                                        negate=True).then_inc(s_nh, 1)
                            dve.wait_ge(s_nh, i * 2 * UNITS + 2 * u + 2)
                            nc.vector.tensor_tensor(nm[:, u % 2:u % 2 + 1], nh[:, u % 2, 0:1], nh[:, u % 2, 1:2],
                                                    ALU.min).then_inc(s_nm, 1)
                        if 1 <= u <= UNITS:
                            if u > 2:
                                dve.wait_ge(s_pv, i * UNITS + u - 2)
                            copy(u - 1, 1)
                            copy(u - 1, 3)
                        if u >= 2:
                            v = u - 2
                            dve.wait_ge(s_pv, i * UNITS + v + 1)
                            nc.vector.reciprocal(rec[:], m.bank[:, 7, L:L + 1]).then_inc(s_rc, 1)
                            dve.wait_ge(s_rc, i * UNITS + v + 1)
                            nc.vector.tensor_scalar(cn[:, v // 2, L * (v % 2):L * (v % 2) + L], m.bank[:, 7, 0:L],
                                                    rec[:], None, ALU.mult).then_inc(s_cn, 1)
                    for q in range(4):
                        dve.wait_ge(s_y, i * 4 + q + 1)
                        dve.wait_ge(s_x, i * 4 - 4 + q + 1 + CX)
                        nc.vector.tensor_tensor(m.x[:, 2 * q:2 * q + 2, :],
                                                m.bank[:, q, :].rearrange("p (t n) -> p t n", t=2),
                                                m.x[:, 2 * q:2 * q + 2, :], ALU.add).then_inc(s_x, 1)



HK, GR, HW = 16, 2, P
HV = HK * GR
TAPS = 4


def delta_gates(nc, m, d, gates):
    (s_in, s_ba, s_t, s_beta, s_abs, s_rl, s_ex, s_u, s_den, s_ln, s_e0, s_num, s_dd, s_rd, s_n2, s_lp, s_sp, s_ea,
     s_g, s_al, s_cum, s_eg, s_out) = (m.sem(f"dg_{n}") for n in (
         "in ba t beta abs rl ex u den ln e0 num dd rd n2 lp sp ea g al cum eg out").split())
    with ExitStack() as tmp:
        def sb(name, shape):
            return tmp.enter_context(nc.sbuf_tensor(f"dg_{name}", shape, F32))
        w = sb("w", [P, KD, 2 * HV])
        dt, alog, ea = sb("dt", [P, HV]), sb("alog", [P, HV]), sb("ea", [P, HV])
        upper = sb("upper", [P, P])
        t, beta, ab, rl, ex, u, den, ln, e0, sp, g, al, eg = (sb(n, [P, NT, HV]) for n in (
            "t beta ab rl ex u den ln e0 sp g al eg").split())
        ba = m.bank[:, 0, :].rearrange("p (t q h) -> p t q h", t=NT, q=2)
        cum = m.bank[:, 1, 0:NT * HV].rearrange("p (t h) -> p t h", t=NT)
        with nc.Block() as block:
            @block.sync
            def _(sp_):
                sp_.dma_start(w[:], d["dn_wba"]).then_inc(s_in, 16)
                sp_.dma_start(dt[:], d["dn_dt"].partition_broadcast(P)).then_inc(s_in, 16)
                sp_.dma_start(alog[:], d["dn_alog"].partition_broadcast(P)).then_inc(s_in, 16)
                sp_.dma_start(upper[:], d["dn_upper"]).then_inc(s_in, 16)

            @block.tensor
            def _(pe):
                pe.wait_ge(s_in, 64)
                for n in range(NT):
                    for k in range(KD):
                        last = nc.tensor.matmul(m.bank[:, 0, 2 * HV * n:2 * HV * n + 2 * HV],
                                                m.xnT[:, k, P * n:P * n + P], w[:, k, :],
                                                start=(k == 0), stop=(k == KD - 1))
                last.then_inc(s_ba, 1)
                pe.wait_ge(s_g, 1)
                nc.tensor.matmul(m.bank[:, 1, 0:NT * HV], upper[:], g[:].rearrange("p t h -> p (t h)"),
                                 start=True, stop=True).then_inc(s_cum, 1)

            @block.vector
            def _(dve):
                v = nc.vector
                dve.wait_ge(s_in, 64)
                dve.wait_ge(s_beta, 1)
                v.tensor_tensor(t[:], ba[:, :, 1, :], dt[:].unsqueeze(1).to_broadcast([P, NT, HV]), ALU.add).then_inc(s_t, 1)
                dve.wait_ge(s_t, 1)
                v.scalar_tensor_tensor(out=ab[:], in0=t[:], scalar=-1.0, in1=t[:], op0=ALU.mult,
                                       op1=ALU.max).then_inc(s_abs, 1)
                v.tensor_scalar(rl[:], t[:], 0.0, None, ALU.max).then_inc(s_rl, 1)
                dve.wait_ge(s_ex, 1)
                v.tensor_scalar(u[:], ex[:], 1.0, None, ALU.add).then_inc(s_u, 1)
                dve.wait_ge(s_u, 1)
                v.tensor_scalar(den[:], u[:], 1.0, None, ALU.subtract).then_inc(s_den, 1)
                dve.wait_ge(s_den, 1)
                v.tensor_scalar(e0[:], den[:], 0.0, None, ALU.is_equal).then_inc(s_e0, 1)
                dve.wait_ge(s_e0, 1)
                dve.wait_ge(s_ln, 1)
                v.tensor_tensor(ln[:], ln[:], e0[:], ALU.add).then_inc(s_num, 1)
                v.tensor_tensor(den[:], den[:], e0[:], ALU.add).then_inc(s_dd, 1)
                dve.wait_ge(s_dd, 1)
                v.reciprocal(den[:], den[:]).then_inc(s_rd, 1)
                dve.wait_ge(s_num, 1)
                v.tensor_tensor(ln[:], ln[:], ex[:], ALU.mult).then_inc(s_n2, 1)
                dve.wait_ge(s_n2, 1)
                dve.wait_ge(s_rd, 1)
                v.tensor_tensor(ln[:], ln[:], den[:], ALU.mult).then_inc(s_lp, 1)
                dve.wait_ge(s_lp, 1)
                dve.wait_ge(s_rl, 1)
                v.tensor_tensor(sp[:], ln[:], rl[:], ALU.add).then_inc(s_sp, 1)
                dve.wait_ge(s_sp, 1)
                dve.wait_ge(s_ea, 1)
                v.tensor_tensor(g[:], sp[:], ea[:].unsqueeze(1).to_broadcast([P, NT, HV]), ALU.mult).then_inc(s_g, 1)
                dve.wait_ge(s_al, 1)
                dve.wait_ge(s_eg, 1)
                for q, a in enumerate((al, beta, eg)):
                    v.tensor_copy(gates[:, :, q, :, :], a[:].rearrange("p t (h r) -> p h t r", r=GR)).then_inc(s_out, 1)

            @block.scalar
            def _(act):
                a = nc.scalar
                act.wait_ge(s_ba, 1)
                a.activation(beta[:], ba[:, :, 0, :], ACT.Sigmoid).then_inc(s_beta, 1)
                act.wait_ge(s_in, 64)
                a.activation(ea[:], alog[:], ACT.Exp).then_inc(s_ea, 1)
                act.wait_ge(s_abs, 1)
                a.activation(ex[:], ab[:], ACT.Exp, scale=-1.0).then_inc(s_ex, 1)
                act.wait_ge(s_u, 1)
                a.activation(ln[:], u[:], ACT.Ln).then_inc(s_ln, 1)
                act.wait_ge(s_g, 1)
                a.activation(al[:], g[:], ACT.Exp, scale=-1.0).then_inc(s_al, 1)
                act.wait_ge(s_cum, 1)
                a.activation(eg[:], cum, ACT.Exp, scale=-1.0).then_inc(s_eg, 1)


class Count:

    def __init__(self, sem, names):
        self.sem, self.n = sem, len(names)
        self.index = {name: k for k, name in enumerate(names)}
        assert len(self.index) == self.n

    def credit(self):
        return 2 * self.n

    def after(self, e, name):
        return e * self.n + self.index[name] + 1 + 2 * self.n


def delta_attention(nc, m, d):
    with nc.sbuf_tensor("dn_gates", [P, HK, 3, NT, GR], F32) as gates:
        delta_gates(nc, m, d, gates)
        delta_rounds(nc, m, d, gates)


def delta_rounds(nc, m, d, gates):
    GS = [(h, c) for h in range(GR) for c in range(C)]
    LEVELS = 7
    CH = range(2 + GR)
    NCH = len(CH)
    FRONT = [("ss",)] + [("a", g) for g in range(4)] + [("kk", c) for c in range(C)] + [("k",)]
    FRONT += [("v", g) for g in range(4)] + [("qk", c) for c in range(C)] + [("n", g) for g in range(4)]
    LEVEL_JOBS = []
    for l in range(1, LEVELS):
        LEVEL_JOBS += [("t1", l, g) for g in range(4)] + [("x", l, g) for g in range(4)]
        if l < LEVELS - 1:
            LEVEL_JOBS += [("y", l, g) for g in range(4)]
    TAIL = [("u0", 0), ("u0", 1), ("s", 0), ("s", 1), ("o0", 0), ("o0", 1), ("z", 0), ("ks", 0), ("ks", 1), ("qs", 0),
            ("qs", 1), ("u1", 0), ("u1", 1), ("z", 1), ("o1", 0), ("o1", 1), ("z", 2), ("z", 3)]
    for c in range(C):
        TAIL += [("xt", c, h) for h in range(GR)] + [("out", 2 * c + a) for a in range(2)]
    ZJ = [("z", q) for q in range(4)]
    PJ = [("p", ch, hf) for ch in CH for hf in range(2)]
    PROJ = PJ + ZJ
    RING = FRONT + PJ + LEVEL_JOBS + TAIL
    assert len(RING) % 8 == 0
    EARLY = 2
    V_PROJ = [("conv", ch, j) for ch in CH for j in range(TAPS)]
    A_PROJ = [("raw", ch, hf) for ch in CH for hf in range(2)] + [("silu", ch) for ch in CH] + ZJ
    P_PROJ = ["cur", "wos"]
    P_AHEAD = [("sq", a) for a in range(2)] + [("da", g) for g in range(4)]
    V = ["ss"] + [("e", g) for g in range(4)] + [("kd", h) for h in range(GR)]
    V += [("n", h, c) for c in range(C) for h in range(GR)] + [("v", g) for g in range(4)] + [("a", h, c) for c in range(C) for h in range(GR)]
    V += [("x0", g) for g in range(4)]
    for l in range(1, LEVELS):
        V += [("t1", l, g) for g in range(4)] + [("x", l, g) for g in range(4)]
    V += [("u0", h) for h in range(GR)] + [("o0", h) for h in range(GR)] + [("ks", h) for h in range(GR)]
    V += [("qs", h) for h in range(GR)] + [(n, 0, h) for h in range(GR) for n in ("r2", "ms")]
    V += [("u1", h) for h in range(GR)] + [("o1", h) for h in range(GR)]
    V += [(n, 1, h) for h in range(GR) for n in ("r2", "ms")] + [("x+", q) for q in range(4)]
    A = [("y", l, g) for l in range(1, LEVELS - 1) for g in range(4)] + [("s", h) for h in range(GR)]
    A += [(n, c, h) for n in ("sq", "xt") for c in range(C) for h in range(GR)]
    G = ["r", "nk", "rq", "r2", "c2"]
    G += [("ec", g) for g in range(4)] + [(n, g) for g in range(4) for n in ("ym", "yi", "xi")] + ["z"]
    G += [("r", h) for h in range(GR)]
    G += [(n, 0, h) for h in range(GR) for n in ("rp", "xn")]
    G += [("xg", h) for h in range(GR)] + [(n, 1, h) for h in range(GR) for n in ("rp", "xn")]
    pj, vj, aj, gj = (Count(m.sem(f"dn_proj_{n}"), s) for n, s in (("pe", PROJ), ("dve", V_PROJ), ("act", A_PROJ),
                                                                 ("pool", P_PROJ)))
    pm, vm, am, gm = (Count(m.sem(f"dn_mat_{n}"), s) for n, s in (("pe", [j for j in RING if j not in PROJ]), ("dve", V), ("act", A), ("pool", G)))
    gh = Count(m.sem("dn_ahead_pool"), P_AHEAD)
    s_w, s_cst, s_pad = (m.sem(f"dn_{n}") for n in ("w", "cst", "pad"))
    s_cw, s_wo = ([m.sem(f"dn_{n}{s}") for s in range(2)] for n in ("cw", "wo"))

    def reader(job):
        n = job[0]
        if n == "ss":
            return vm, "ss"
        if n == "a":
            return vm, ("e", job[1])
        if n == "k":
            return vm, ("kd", 1)
        if n in ("kk", "qk"):
            return vm, ("n" if n == "kk" else "a", GR - 1, job[1])
        if n == "n":
            return vm, ("x0", job[1])
        if n in ("y", "s", "xt"):
            return am, job
        if n == "out":
            return vm, ("x+", job[1])
        return vm, job

    def bank_of(job):
        return RING.index(job) % 8

    def rounds(eng, front, project, rest, gates_ahead):
        def body(e, s):
            front(e, s)
            project(e + 1, 1 - s)
            rest(e, s)
        project(0, 0)
        gates_ahead(0, 0)
        with eng.Fori(0, HK // 2 - 1) as i:
            body(2 * i, 0)
            body(2 * i + 1, 1)
        body(HK - 2, 0)
        front(HK - 1, 1)
        rest(HK - 1, 1)

    def first(e):
        return isinstance(e, int) and e == 0

    def last_round(e):
        return isinstance(e, int) and e == HK - 1

    with ExitStack() as tmp:
        def sb(name, shape):
            return tmp.enter_context(nc.sbuf_tensor(f"dn_{name}", shape, F32))
        w = sb("w", [P, KD, (NCH + GR) * HW])
        cw = [sb(f"cw{s}", [P, NCH, TAPS]) for s in range(2)]
        wo = [sb(f"wo{s}", [HW, GR, D]) for s in range(2)]
        wos = [sb(f"wos{s}", [HW, GR, D]) for s in range(2)]
        nw = sb("nw", [HW, 1])
        ones = sb("ones", [P, P])
        ident0 = sb("ident0", [P, 4, P])
        masks = sb("masks", [P, LEVELS + 1, P])
        raw = sb("raw", [P, NCH, B, TAPS - 1 + SEQ])
        ct = [sb(f"ct{s}", [P, NCH, B, SEQ]) for s in range(2)]
        z = [sb(f"z{s}", [P, NT, GR, HW]) for s in range(2)]
        cur = [sb(f"cur{s}", [P, 3, NT, GR]) for s in range(2)]
        xg = sb("xg", [P, GR, NT, HW])
        ssv, rr, = sb("ssv", [P, 2, NT]), sb("rr", [P, 2, NT])
        nk, rq, r2 = sb("nk", [P, NT]), sb("rq", [P, NT]), sb("r2", [P, NT])
        c2 = sb("c2", [P, NT, GR])
        E = sb("E", [P, 4, 4, P])
        sq = E[:].rearrange("p g b n -> p (g b n)").rearrange("p (a n) -> p a n", a=2)
        T1 = sb("T1", [P, 4, 4, P])
        Ec = T1
        sqx = T1
        MT = sb("MT", [P, 4, 4, P])
        xn = MT
        AT = sb("AT", [P, 4, 4, P])
        da = raw[:, :, :, TAPS - 1:TAPS - 1 + P]
        X = sb("X", [P, 4, 4, P])
        xT = X
        Y = sb("Y", [P, 4, 4, P])
        vp = sb("vp", [P, GR, NT, HW])
        kd = sb("kd", [P, GR, B, HW])
        U = sb("U", [P, GR, B, HW])
        S = sb("S", [HW, GR, B, HW])
        R = sb("R", [P, GR, B, HW])
        ks = sb("ks", [P, GR, B, HW])
        os_ = ks
        qs = sb("qs", [P, GR, B, HW])
        ssx, rx = sb("ssx", [P, GR, C, B]), sb("rx", [P, GR, C, B])

        def four(bank):
            return m.bank[:, bank, :].rearrange("p (b n) -> p b n", b=4)

        def cols(a):
            return a.unsqueeze(2).to_broadcast([P, 4, P])

        with nc.Block() as block:
            @block.sync
            def _(sp):
                for dst, src in ((ident0, "ident0"), (masks, "masks"), (nw, "nw")):
                    sp.dma_start(dst[:], d["dn_" + src]).then_inc(s_cst, 16)

                def load(e, s):
                    sp.wait_ge(pj.sem, pj.after(e - 1, ZJ[-1]))
                    sp.dma_start(w[:], d["dn_w"][e]).then_inc(s_w, 16)
                    sp.wait_ge(vj.sem, vj.after(e - 2, ("conv", NCH - 1, TAPS - 1)))
                    sp.dma_start(cw[s][:], d["dn_cw"][e]).then_inc(s_cw[s], 16)
                    sp.wait_ge(gj.sem, gj.after(e - 2, "wos"))
                    sp.dma_start(wo[s][:], d["dn_wo"][e]).then_inc(s_wo[s], 16)
                two_slots(sp, HK, load, lambda e, s: None)

            @block.tensor
            def _(pe):
                pe.sem_inc(pj.sem, pj.credit())
                pe.sem_inc(pm.sem, pm.credit())
                pe.wait_ge(s_cst, 48)
                pe.wait_ge(s_pad, 2)

                def take(job, e, now):
                    n = RING.index(job)
                    if first(e) and job in PROJ:
                        return n % 8
                    k, r = n - 8, now
                    if k < 0:
                        k, r = k + len(RING), now - 1
                    while last_round(r) and RING[k] in PROJ:
                        k -= 8
                        if k < 0:
                            k, r = k + len(RING), r - 1
                    if RING[k] in PROJ:
                        step = ("raw",) + RING[k][1:] if RING[k][0] == "p" else RING[k]
                        pe.wait_ge(aj.sem, aj.after(r + 1, step))
                    else:
                        c_, step = reader(RING[k])
                        pe.wait_ge(c_.sem, c_.after(r, step))
                    return n % 8

                def gate_job(e, s, job):
                    if first(e):
                        pe.wait_ge(aj.sem, aj.after(0, ("raw", NCH - 1, 1)))
                    bank = take(job, e, e - 1)
                    for a in range(2):
                        t = 2 * job[1] + a
                        for k in range(KD):
                            last = nc.tensor.matmul(m.bank[:, bank, GR * HW * a:GR * HW * a + GR * HW],
                                                    m.xnT[:, k, P * t:P * t + P], w[:, k, NCH * HW:],
                                                    start=(k == 0), stop=(k == KD - 1))
                    last.then_inc(pj.sem, 1)

                def gates_ahead(e, s):
                    for job in ZJ:
                        gate_job(e, s, job)
                    pe.wait_ge(aj.sem, aj.after(0, ZJ[-1]))

                def project(e, s):
                    pe.wait_ge(s_w, e * 16 + 16)
                    for job in PJ:
                        bank = take(job, e, e - 1)
                        _, ch, hf = job
                        for k in range(KD):
                            last = nc.tensor.matmul(m.bank[:, bank, :], w[:, k, HW * ch:HW * ch + HW],
                                                    m.xnT[:, k, BANK * hf:BANK * hf + BANK],
                                                    start=(k == 0), stop=(k == KD - 1))
                        last.then_inc(pj.sem, 1)

                def front(e, s):
                    q, k = ct[s][:, 0], ct[s][:, 1]
                    bank = take(("ss",), e, e)
                    pe.wait_ge(gh.sem, gh.after(e, ("sq", 1)))
                    for a in range(2):
                        for t in range(NT):
                            last = nc.tensor.matmul(m.bank[:, bank, NT * a + t:NT * a + t + 1],
                                                    sq[:, a, P * t:P * t + P], ones[:, 0:1], start=True, stop=True)
                    last.then_inc(pm.sem, 1)
                    for g in range(4):
                        bank = take(("a", g), e, e)
                        pe.wait_ge(gh.sem, gh.after(e, ("da", g)))
                        nc.tensor.matmul(four(bank), ones[:], da[:, g],
                                         start=True, stop=True).then_inc(pm.sem, 1)
                    pe.wait_ge(aj.sem, aj.after(e, ("silu", 1)))
                    for c in range(C):
                        bank = take(("kk", c), e, e)
                        for b in range(B):
                            last = nc.tensor.matmul(m.bank[:, bank, P * b:P * b + P], k[:, b, P * c:P * c + P],
                                                    k[:, b, P * c:P * c + P], start=True, stop=True)
                        last.then_inc(pm.sem, 1)
                    bank = take(("k",), e, e)
                    for b in range(B):
                        last = nc.tensor.transpose(m.bank[:, bank, P * b:P * b + P], k[:, b, 0:P], m.ident[:, 0, :])
                    last.then_inc(pm.sem, 1)
                    for g, (h, c) in enumerate(GS):
                        bank = take(("v", g), e, e)
                        pe.wait_ge(aj.sem, aj.after(e, ("silu", 2 + h)))
                        for b in range(B):
                            last = nc.tensor.transpose(m.bank[:, bank, P * b:P * b + P],
                                                       ct[s][:, 2 + h, b, P * c:P * c + P], m.ident[:, 0, :])
                        last.then_inc(pm.sem, 1)
                    for c in range(C):
                        bank = take(("qk", c), e, e)
                        for b in range(B):
                            last = nc.tensor.matmul(m.bank[:, bank, P * b:P * b + P], k[:, b, P * c:P * c + P],
                                                    q[:, b, P * c:P * c + P], start=True, stop=True)
                        last.then_inc(pm.sem, 1)
                    for g, (h, c) in enumerate(GS):
                        bank = take(("n", g), e, e)
                        pe.wait_ge(vm.sem, vm.after(e, ("n", h, c)))
                        for b in range(B):
                            last = nc.tensor.transpose(m.bank[:, bank, P * b:P * b + P], MT[:, g, b, :],
                                                       m.ident[:, 0, :])
                        last.then_inc(pm.sem, 1)

                def rest(e, s):
                    q, k = ct[s][:, 0], ct[s][:, 1]

                    def job(name):
                        return take(name, e, e)

                    def ahead(name):
                        if not last_round(e):
                            gate_job(e + 1, 1 - s, name)

                    def product(name, lhsT, rhs):
                        bank = job(name)
                        for b in range(B):
                            last = nc.tensor.matmul(m.bank[:, bank, P * b:P * b + P], lhsT(b), rhs(b),
                                                    start=True, stop=True)
                        last.then_inc(pm.sem, 1)

                    for l in range(1, LEVELS):
                        for g in range(4):
                            if l == 1:
                                pe.wait_ge(gm.sem, gm.after(e, ("xi", g)))
                            else:
                                pe.wait_ge(vm.sem, vm.after(e, ("x", l - 1, g)))
                            product(("t1", l, g), lambda b: MT[:, g, b, :], lambda b: X[:, g, b, :])
                        for g in range(4):
                            pe.wait_ge(vm.sem, vm.after(e, ("t1", l, g)))
                            if l > 1:
                                pe.wait_ge(am.sem, am.after(e, ("y", l - 1, g)))
                            if l < LEVELS - 1:
                                product(("x", l, g), lambda b: Y[:, g, b, :], lambda b: T1[:, g, b, :])
                            else:
                                product(("x", l, g), lambda b: T1[:, g, b, :], lambda b: Y[:, g, b, :])
                        if l < LEVELS - 1:
                            for g in range(4):
                                bank = job(("y", l, g))
                                pe.wait_ge(vm.sem, vm.after(e, ("x", l, g)))
                                for b in range(B):
                                    last = nc.tensor.transpose(m.bank[:, bank, P * b:P * b + P], X[:, g, b, :],
                                                               m.ident[:, 0, :])
                                last.then_inc(pm.sem, 1)

                    for h in range(GR):
                        pe.wait_ge(vm.sem, vm.after(e, ("x", LEVELS - 1, 2 * h)))
                        product(("u0", h), lambda b: Y[:, 2 * h, b, :], lambda b: vp[:, h, C * b, :])
                    for h in range(GR):
                        pe.wait_ge(vm.sem, vm.after(e, ("u0", h)))
                        product(("s", h), lambda b: kd[:, h, b, :], lambda b: U[:, h, b, :])
                    for h in range(GR):
                        product(("o0", h), lambda b: AT[:, 2 * h, b, :], lambda b: U[:, h, b, :])
                    ahead(("z", 0))
                    for h in range(GR):
                        pe.wait_ge(am.sem, am.after(e, ("s", h)))
                        product(("ks", h), lambda b: k[:, b, P:SEQ], lambda b: S[:, h, b, :])
                    for h in range(GR):
                        product(("qs", h), lambda b: q[:, b, P:SEQ], lambda b: S[:, h, b, :])
                    for h in range(GR):
                        pe.wait_ge(gm.sem, gm.after(e, ("r", h)))
                        product(("u1", h), lambda b: Y[:, 2 * h + 1, b, :], lambda b: R[:, h, b, :])
                    ahead(("z", 1))
                    for h in range(GR):
                        pe.wait_ge(vm.sem, vm.after(e, ("u1", h)))
                        product(("o1", h), lambda b: AT[:, 2 * h + 1, b, :], lambda b: U[:, h, b, :])
                    ahead(("z", 2))
                    ahead(("z", 3))
                    pe.wait_ge(gj.sem, gj.after(e, "wos"))
                    for c in range(C):
                        for h in range(GR):
                            bank = job(("xt", c, h))
                            pe.wait_ge(gm.sem, gm.after(e, ("xn", c, h)))
                            for b in range(B):
                                last = nc.tensor.transpose(m.bank[:, bank, P * b:P * b + P], xn[:, 2 * h + c, b, :],
                                                           m.ident[:, 0, :])
                            last.then_inc(pm.sem, 1)
                        for n in range(2):
                            bank = job(("out", 2 * c + n))
                            pe.wait_ge(am.sem, am.after(e, ("xt", c, GR - 1)))
                            for a in range(2):
                                for h in range(GR):
                                    last = nc.tensor.matmul(m.bank[:, bank, D * a:D * a + D],
                                                            xT[:, 2 * h + c, 2 * n + a, :], wos[s][:, h, :],
                                                            start=(h == 0), stop=(h == GR - 1))
                            last.then_inc(pm.sem, 1)
                rounds(pe, front, project, rest, gates_ahead)

            @block.scalar
            def _(act):
                act.sem_inc(aj.sem, aj.credit())
                act.sem_inc(am.sem, am.credit())

                def gate(e, s, n):
                    act.wait_ge(pj.sem, pj.after(e, ("z", n)))
                    act.wait_ge(gm.sem, gm.after(e - 2, ("xg", GR - 1)))
                    nc.scalar.activation(z[s][:, 2 * n:2 * n + 2, :, :],
                                         m.bank[:, bank_of(("z", n)), :].rearrange("p (t h n) -> p t h n", t=2, h=GR),
                                         ACT.Silu).then_inc(aj.sem, 1)

                def gates_ahead(e, s):
                    for n in range(4):
                        gate(e, s, n)

                def silu(e, s, ch):
                    act.wait_ge(vj.sem, vj.after(e, ("conv", ch, TAPS - 1)))
                    nc.scalar.activation(ct[s][:, ch], ct[s][:, ch], ACT.Silu).then_inc(aj.sem, 1)

                def project(e, s):
                    act.wait_ge(pm.sem, pm.after(e - 1, ("a", 3)))
                    for ch in CH:
                        act.wait_ge(vj.sem, vj.after(e - 1, ("conv", ch, TAPS - 1)))
                        for hf in range(2):
                            act.wait_ge(pj.sem, pj.after(e, ("p", ch, hf)))
                            nc.scalar.activation(raw[:, ch, 2 * hf:2 * hf + 2, TAPS - 1:],
                                                 m.bank[:, bank_of(("p", ch, hf)), :].rearrange("p (b t) -> p b t", b=2),
                                                 ACT.Copy).then_inc(aj.sem, 1)
                    for ch in range(NCH if first(e) else EARLY):
                        silu(e, s, ch)

                def rest(e, s):
                    def bank(name):
                        act.wait_ge(pm.sem, pm.after(e, name))
                        return four(bank_of(name))
                    for l in range(1, LEVELS - 1):
                        for g in range(4):
                            nc.scalar.activation(Y[:, g], bank(("y", l, g)), ACT.Copy).then_inc(am.sem, 1)
                        if EARLY + l - 1 < NCH and not last_round(e):
                            silu(e + 1, 1 - s, EARLY + l - 1)
                    for h in range(GR):
                        nc.scalar.activation(S[:, h], bank(("s", h)), ACT.Copy).then_inc(am.sem, 1)

                    def ahead(n):
                        if not last_round(e):
                            gate(e + 1, 1 - s, n)

                    def square(c, h):
                        nc.scalar.activation(sqx[:, 2 * h + c], xg[:, h, c::C, :], ACT.Square).then_inc(am.sem, 1)
                    ahead(0)
                    for h in range(GR):
                        act.wait_ge(vm.sem, vm.after(e, ("o0", h)))
                        square(0, h)
                    ahead(1)
                    ahead(2)
                    for h in range(GR):
                        act.wait_ge(gm.sem, gm.after(e, ("xg", h)))
                        square(1, h)
                    ahead(3)
                    for c in range(C):
                        for h in range(GR):
                            nc.scalar.activation(xT[:, 2 * h + c], bank(("xt", c, h)), ACT.Copy).then_inc(am.sem, 1)
                rounds(act, lambda e, s: None, project, rest, gates_ahead)

            @block.gpsimd
            def _(pool):
                t = nc.gpsimd
                t.memset(raw[:, :, :, 0:TAPS - 1], 0.0).then_inc(s_pad, 1)
                t.memset(ones[:], 1.0).then_inc(s_pad, 1)
                pool.sem_inc(gj.sem, gj.credit())
                pool.sem_inc(gm.sem, gm.credit())
                pool.sem_inc(gh.sem, gh.credit())
                pool.wait_ge(s_cst, 48)

                def project(e, s):
                    t.tensor_copy(cur[s][:], gates[:, e]).then_inc(gj.sem, 1)
                    pool.wait_ge(s_wo[s], (e - s) * 8 + 16)
                    pool.wait_ge(pm.sem, pm.after(e - 2, ("out", 3)))
                    t.tensor_tensor(wos[s][:], wo[s][:], nw[:].unsqueeze(2).to_broadcast([HW, GR, D]), ALU.mult).then_inc(gj.sem, 1)

                def squares_and_decays(e, s):
                    pool.wait_ge(vm.sem, vm.after(e - 1, ("a", GR - 1, C - 1)))
                    for a in range(2):
                        pool.wait_ge(aj.sem, aj.after(e, ("silu", a)))
                        v = ct[s][:, a].rearrange("p b t -> p (b t)")
                        t.tensor_tensor(sq[:, a, :], v, v, ALU.mult).then_inc(gh.sem, 1)
                    pool.wait_ge(gj.sem, gj.after(e, "cur"))
                    pool.wait_ge(vj.sem, vj.after(e, ("conv", NCH - 1, TAPS - 1)))
                    for g, (h, c) in enumerate(GS):
                        t.tensor_tensor(da[:, g], ident0[:], cols(cur[s][:, 0, c::C, h]), ALU.mult).then_inc(gh.sem, 1)

                def front(e, s):
                    beta = cur[s][:, 1]
                    pool.wait_ge(vm.sem, vm.after(e, "ss"))
                    t.tensor_tensor(rr[:], ssv[:], m.neghalf[:].rearrange("p (a t) -> p a t", a=2), ALU.pow).then_inc(gm.sem, 1)
                    pool.wait_ge(gm.sem, gm.after(e, "r"))
                    t.tensor_tensor(nk[:], ssv[:, 1], rr[:, 1], ALU.mult).then_inc(gm.sem, 1)
                    t.tensor_scalar(rq[:], rr[:, 0], float(HW) ** -0.5, None, ALU.mult).then_inc(gm.sem, 1)
                    t.tensor_tensor(r2[:], rr[:, 1], rr[:, 1], ALU.mult).then_inc(gm.sem, 1)
                    pool.wait_ge(gm.sem, gm.after(e, "r2"))
                    t.tensor_tensor(c2[:], beta, r2[:].unsqueeze(2).to_broadcast([P, NT, GR]), ALU.mult).then_inc(gm.sem, 1)
                    pool.wait_ge(gm.sem, gm.after(e, "c2"))
                    for g, (h, c) in enumerate(GS):
                        pool.wait_ge(vm.sem, vm.after(e, ("e", g)))
                        t.tensor_tensor(Ec[:, g], E[:, g], cols(c2[:, c::C, h]), ALU.mult).then_inc(gm.sem, 1)
                    for g, (h, c) in enumerate(GS):
                        pool.wait_ge(vm.sem, vm.after(e, ("n", h, c)))
                        t.tensor_tensor(Y[:, g], MT[:, g], masks[:, LEVELS:LEVELS + 1, :].to_broadcast([P, 4, P]),
                                        ALU.mult).then_inc(gm.sem, 1)
                        pool.wait_ge(gm.sem, gm.after(e, ("ym", g)))
                        t.tensor_tensor(Y[:, g], m.ident[:], Y[:, g], ALU.subtract).then_inc(gm.sem, 1)
                        pool.wait_ge(vm.sem, vm.after(e, ("x0", g)))
                        t.tensor_tensor(X[:, g], m.ident[:], X[:, g], ALU.subtract).then_inc(gm.sem, 1)

                def rest(e, s):
                    if not last_round(e):
                        squares_and_decays(e + 1, 1 - s)
                    pool.wait_ge(aj.sem, aj.after(e, ("z", 3)))
                    zz = z[s][:].rearrange("p t h n -> p t (h n)")
                    t.tensor_tensor(zz, zz, rq[:].unsqueeze(2).to_broadcast([P, NT, GR * HW]), ALU.mult).then_inc(gm.sem, 1)
                    for h in range(GR):
                        pool.wait_ge(vm.sem, vm.after(e, ("ks", h)))
                        t.tensor_tensor(R[:, h], vp[:, h, 1::C, :], ks[:, h], ALU.subtract).then_inc(gm.sem, 1)

                    def rms(c, h):
                        pool.wait_ge(vm.sem, vm.after(e, ("ms", c, h)))
                        t.tensor_tensor(rx[:, h, c], ssx[:, h, c], m.neghalf[:, 0:4], ALU.pow).then_inc(gm.sem, 1)
                        pool.wait_ge(gm.sem, gm.after(e, ("rp", c, h)))
                        t.tensor_tensor(xn[:, 2 * h + c], xg[:, h, c::C, :], cols(rx[:, h, c]), ALU.mult).then_inc(gm.sem, 1)
                    for h in range(GR):
                        rms(0, h)
                    for h in range(GR):
                        pool.wait_ge(vm.sem, vm.after(e, ("o1", h)))
                        t.tensor_tensor(xg[:, h, 1::C, :], os_[:, h], z[s][:, 1::C, h, :], ALU.mult).then_inc(gm.sem, 1)
                    for h in range(GR):
                        rms(1, h)
                rounds(pool, front, project, rest, squares_and_decays)

            @block.vector
            def _(dve):
                t = nc.vector
                dve.sem_inc(vj.sem, vj.credit())
                dve.sem_inc(vm.sem, vm.credit())
                dve.wait_ge(s_cst, 48)
                dve.wait_ge(s_pad, 1)

                def conv(e, s, ch):
                    dve.wait_ge(aj.sem, aj.after(e, ("raw", ch, 1)))
                    for j in range(TAPS):
                        src = raw[:, ch, :, j:j + SEQ]
                        if j == 0:
                            t.tensor_scalar(ct[s][:, ch], src, cw[s][:, ch, 0:1], None, ALU.mult).then_inc(vj.sem, 1)
                        else:
                            dve.wait_ge(vj.sem, vj.after(e, ("conv", ch, j - 1)))
                            t.scalar_tensor_tensor(out=ct[s][:, ch], in0=src, scalar=cw[s][:, ch, j:j + 1],
                                                   in1=ct[s][:, ch], op0=ALU.mult, op1=ALU.add).then_inc(vj.sem, 1)

                def project(e, s):
                    dve.wait_ge(s_cw[s], (e - s) * 8 + 16)
                    dve.wait_ge(pm.sem, pm.after(e - 2, ("qs", GR - 1)))
                    for ch in range(NCH if first(e) else EARLY):
                        conv(e, s, ch)

                def source(e, name):
                    dve.wait_ge(pm.sem, pm.after(e, name))
                    return four(bank_of(name))

                def front(e, s):
                    def bank(name):
                        return source(e, name)
                    n = bank_of(("ss",))
                    dve.wait_ge(pm.sem, pm.after(e, ("ss",)))
                    t.tensor_scalar(ssv[:].rearrange("p a t -> p (a t)"), m.bank[:, n, 0:2 * NT], 1e-6, None,
                                    ALU.add).then_inc(vm.sem, 1)
                    for g in range(4):
                        src = bank(("a", g)).rearrange("p b n -> p (b n)")
                        t.tensor_tensor_scan(E[:, g].rearrange("p b n -> p (b n)"), src,
                                             m.ident[:].rearrange("p b n -> p (b n)"), 0.0, ALU.mult,
                                             ALU.add).then_inc(vm.sem, 1)
                    src = bank(("k",))
                    dve.wait_ge(vm.sem, vm.after(e, ("e", 2)))
                    for h in range(GR):
                        t.tensor_tensor(kd[:, h], src, E[:, 2 * h, :, P - 1:P].to_broadcast([P, 4, P]),
                                        ALU.mult).then_inc(vm.sem, 1)
                    for c in range(C):
                        src = bank(("kk", c))
                        for h in range(GR):
                            dve.wait_ge(gm.sem, gm.after(e, ("ec", 2 * h + c)))
                            t.tensor_tensor(MT[:, 2 * h + c], src, Ec[:, 2 * h + c], ALU.mult).then_inc(vm.sem, 1)
                    dve.wait_ge(gm.sem, gm.after(e, "nk"))
                    for g, (h, c) in enumerate(GS):
                        t.tensor_tensor(vp[:, h, c::C, :], bank(("v", g)), cols(nk[:, c::C]), ALU.mult).then_inc(vm.sem, 1)
                    for c in range(C):
                        src = bank(("qk", c))
                        for h in range(GR):
                            t.tensor_tensor(AT[:, 2 * h + c], src, E[:, 2 * h + c], ALU.mult).then_inc(vm.sem, 1)
                    for g in range(4):
                        t.tensor_tensor(X[:, g], bank(("n", g)), masks[:, 0:1, :].to_broadcast([P, 4, P]),
                                        ALU.mult).then_inc(vm.sem, 1)

                def rest(e, s):
                    eg = cur[s][:, 2]

                    def bank(name):
                        return source(e, name)
                    for l in range(1, LEVELS):
                        for g in range(4):
                            t.tensor_tensor(T1[:, g], bank(("t1", l, g)), masks[:, l:l + 1, :].to_broadcast([P, 4, P]),
                                            ALU.mult).then_inc(vm.sem, 1)
                        for g in range(4):
                            old = X if l < LEVELS - 1 else Y
                            if l == 1:
                                dve.wait_ge(gm.sem, gm.after(e, ("xi", g)))
                            t.tensor_tensor(old[:, g], old[:, g], bank(("x", l, g)), ALU.subtract).then_inc(vm.sem, 1)
                        if EARLY + l - 1 < NCH and not last_round(e):
                            conv(e + 1, 1 - s, EARLY + l - 1)
                    for h in range(GR):
                        t.tensor_tensor(U[:, h], bank(("u0", h)), cols(c2[:, 0::C, h]), ALU.mult).then_inc(vm.sem, 1)
                    for h in range(GR):
                        dve.wait_ge(gm.sem, gm.after(e, "z"))
                        t.tensor_tensor(xg[:, h, 0::C, :], bank(("o0", h)), z[s][:, 0::C, h, :], ALU.mult).then_inc(vm.sem, 1)
                    for h in range(GR):
                        t.tensor_tensor(ks[:, h], bank(("ks", h)), cols(eg[:, 1::C, h]), ALU.mult).then_inc(vm.sem, 1)
                    for h in range(GR):
                        t.tensor_tensor(qs[:, h], bank(("qs", h)), cols(eg[:, 1::C, h]), ALU.mult).then_inc(vm.sem, 1)

                    def mean_square(c, h):
                        t.tensor_reduce(ssx[:, h, c], sqx[:, 2 * h + c], AX_X, ALU.add).then_inc(vm.sem, 1)
                        dve.wait_ge(vm.sem, vm.after(e, ("r2", c, h)))
                        t.tensor_scalar(ssx[:, h, c], ssx[:, h, c], 1.0 / HW, 1e-6, ALU.mult, ALU.add).then_inc(vm.sem, 1)

                    for h in range(GR):
                        dve.wait_ge(am.sem, am.after(e, ("sq", 0, h)))
                        mean_square(0, h)
                    for h in range(GR):
                        t.tensor_tensor(U[:, h], bank(("u1", h)), cols(c2[:, 1::C, h]), ALU.mult).then_inc(vm.sem, 1)
                    for h in range(GR):
                        dve.wait_ge(vm.sem, vm.after(e, ("qs", h)))
                        t.tensor_tensor(os_[:, h], bank(("o1", h)), qs[:, h], ALU.add).then_inc(vm.sem, 1)
                    for h in range(GR):
                        dve.wait_ge(am.sem, am.after(e, ("sq", 1, h)))
                        mean_square(1, h)
                    for n in range(4):
                        c, b = n // 2, 2 * (n % 2)
                        tiles = m.x[:, C * b + c:C * b + c + C + 1:C, :]
                        dve.wait_ge(pm.sem, pm.after(e, ("out", n)))
                        dve.wait_ge(vm.sem, vm.after(e - 1, ("x+", n)))
                        nb = bank_of(("out", n))
                        t.tensor_tensor(tiles, m.bank[:, nb, :].rearrange("p (t n) -> p t n", t=2), tiles,
                                        ALU.add).then_inc(vm.sem, 1)
                rounds(dve, front, project, rest, lambda e, s: None)



def program(nc, d, out):
    with ExitStack() as ctx:
        m = Shared(nc, ctx)
        start(nc, m, d["x"], d["ident4"])
        layer_norm(nc, m, "ln1")
        delta_attention(nc, m, d)
        m.end_layer()
        layer_norm(nc, m, "ln2")
        latent_attention(nc, m, d)
        m.end_layer()
        layer_norm(nc, m, "ln3")
        gated_mlp(nc, m, "ffn", 8, P, d["f0_gate"], d["f0_up"], d["f0_down"])
        m.end_layer()
        layer_norm(nc, m, "ln4")
        causal_attention(nc, m, "att", d["a1_wq"], d["a1_wk"], d["a1_wv"], d["a1_wo"], None, d["a1_cos"], d["a1_sin"])
        m.end_layer()
        layer_norm(nc, m, "ln5")
        causal_attention(nc, m, "xat", d["x1_wq"], d["x1_wk"], d["x1_wv"], d["x1_wo"], d["x1_ctxT"], None, None)
        m.end_layer()
        layer_norm(nc, m, "ln6")
        with nc.sbuf_tensor("moe_weight", [P, NT, 64], F32) as weight:
            route(nc, m, d["m1_route"], weight)
            gated_mlp(nc, m, "moe", 64, 96, d["m1_gate"], d["m1_up"], d["m1_down"], weight)
        finish(nc, m, out)


def kernel(**inputs):
    import numpy as np
    import concourse.bacc as bacc
    from concourse.bass_utils import run_bass_kernel_spmd

    def ktiles(w):
        return w.reshape(w.shape[0], KD, P, w.shape[2]).transpose(0, 2, 1, 3)

    arrays = {"x": inputs["x"], "ident4": np.tile(np.eye(P, dtype=np.float32), (1, 4))}
    arrays["f0_gate"] = ktiles(inputs["L0_ffn_w_gate"].reshape(8, P, D).transpose(0, 2, 1))
    arrays["f0_up"] = ktiles(inputs["L0_ffn_w_up"].reshape(8, P, D).transpose(0, 2, 1))
    arrays["f0_down"] = inputs["L0_ffn_w_down"].T.reshape(8, P, D)
    arrays["m1_route"] = ktiles(inputs["L1_ffn_gate_weight"].T[None])[0]
    arrays["m1_gate"] = ktiles(inputs["L1_ffn_w_gate"])
    arrays["m1_up"] = ktiles(inputs["L1_ffn_w_up"])
    arrays["m1_down"] = inputs["L1_ffn_w_down"]
    GQ, GH, HD = 4, 4, 16

    def heads32(w, swap):
        w = w.reshape(GQ, GH, HD, -1)
        if swap:
            w = np.concatenate([w[:, :, HD // 2:], w[:, :, :HD // 2]], 2)
        wide = np.zeros((GQ, GH, 32, w.shape[3]), w.dtype)
        wide[:, :, :HD] = w
        return wide.reshape(GQ, P, -1).transpose(0, 2, 1)

    def versions(w):
        return np.stack([ktiles(heads32(w, s)) for s in (False, True)], 3)

    wk = np.repeat(inputs["L1_attn_Wk"].reshape(GQ, 1, HD, D), GH, 1)
    arrays["a1_wq"] = versions(inputs["L1_attn_Wq"])
    arrays["a1_wk"] = versions(wk)
    arrays["a1_wv"] = ktiles(inputs["L1_attn_Wv"].reshape(GQ, HD, D).transpose(0, 2, 1))
    arrays["a1_wo"] = inputs["L1_attn_Wp"].T.reshape(GQ, GH * HD, D)
    half = HD // 2
    inv_freq = (1.0 / np.float32(10000.0) ** (np.arange(half, dtype=np.float32) / np.float32(half))).astype(np.float32)
    angle = np.arange(SEQ, dtype=np.float32)[None, :] * inv_freq[:, None]
    cos = np.zeros((GH, 32, SEQ), np.float32)
    sin = np.zeros((GH, 32, SEQ), np.float32)
    cos[:, :HD] = np.concatenate([np.cos(angle), np.cos(angle)])
    sin[:, :HD] = np.concatenate([-np.sin(angle), np.sin(angle)])
    arrays["a1_cos"], arrays["a1_sin"] = cos.reshape(P, SEQ), sin.reshape(P, SEQ)
    arrays["x1_wq"] = ktiles(heads32(inputs["L1_xattn_Wq"], False))[:, :, :, None]
    arrays["x1_wk"] = heads32(inputs["L1_xattn_Wkv_expand"][:D], False)[:, :, None, None]
    arrays["x1_wv"] = inputs["L1_xattn_Wkv_expand"][D:].reshape(GQ, GH * HD, -1).transpose(0, 2, 1)[:, :, None]
    arrays["x1_wo"] = inputs["L1_xattn_Wout"].T.reshape(GQ, GH * HD, D)
    arrays["x1_ctxT"] = inputs["ctx_512"][:, :SEQ].transpose(2, 0, 1).reshape(-1, NTOK)
    PAIRS, LAT, LEN = 8, 64, inputs["ctx_512"].shape[1]
    LT = (LEN + P - 1) // P

    def pairs(w):
        return w.reshape(PAIRS, 2, w.shape[1], w.shape[2]).transpose(0, 2, 1, 3)

    def twice(w):
        return np.concatenate([w, w], -2)

    def keys(w):
        pad = np.zeros(w.shape[:-2] + (LT * P, LAT), w.dtype)
        pad[..., :LEN, :] = w
        return np.moveaxis(pad.reshape(w.shape[:-2] + (LT, P, LAT)), -2, -3)

    wcq = inputs["L0_xattn_w_kc_q"].transpose(0, 2, 1)
    arrays["mla_wqr"] = pairs(inputs["L0_xattn_W_qr"].transpose(0, 2, 1))
    arrays["mla_wkr"] = pairs(inputs["L0_xattn_W_kr"].transpose(0, 2, 1))
    arrays["mla_wcqA"], arrays["mla_wcqB"] = pairs(wcq[:, :P]), pairs(wcq[:, P:])
    arrays["mla_wq"] = pairs(inputs["L0_xattn_Wq"].reshape(2 * PAIRS, P, D))
    arrays["mla_wkv"] = pairs(inputs["L0_xattn_w_kc_kv"])
    arrays["mla_wo"] = pairs(inputs["L0_xattn_Wo"].T.reshape(2 * PAIRS, P, D))
    ctx = inputs["ctx_512"]
    swapped = np.concatenate([ctx[:, :, LAT // 2:], ctx[:, :, :LAT // 2]], -1)
    inv = (1.0 / np.float32(10000.0) ** (np.arange(0, LAT, 2, dtype=np.float32) / np.float32(LAT))).astype(np.float32)
    freqs = np.arange(LEN, dtype=np.float32)[:, None] * inv[None, :]
    cosk = np.repeat(np.cos(freqs), 2, axis=-1)
    sink = np.repeat(np.sin(freqs), 2, axis=-1)
    sink = np.concatenate([-sink[:, :LAT // 2], sink[:, LAT // 2:]], -1)
    arrays["mla_cosT"], arrays["mla_sinT"] = twice(cosk.T), twice(sink.T)
    arrays["mla_cosk"], arrays["mla_sink"] = keys(cosk), keys(sink)
    arrays["mla_ctxT"], arrays["mla_swT"] = twice(ctx.transpose(0, 2, 1)), twice(swapped.transpose(0, 2, 1))
    arrays["mla_ctxk"], arrays["mla_swk"] = keys(ctx), keys(swapped)
    arrays["dn_w"] = ktiles(inputs["L0_attn_W_qkvz"].reshape(D, HK, -1).transpose(1, 0, 2))
    wba = inputs["L0_attn_W_ba"].reshape(D, HK, 2, GR).transpose(0, 2, 1, 3).reshape(1, D, 2 * HV)
    arrays["dn_wba"] = ktiles(wba)[0]
    arrays["dn_dt"], arrays["dn_alog"] = inputs["L0_attn_dt_bias"], inputs["L0_attn_A_log"]
    cw = inputs["L0_attn_conv_w"].reshape(-1, HW, TAPS)
    cw = np.concatenate([cw[:HK, None], cw[HK:2 * HK, None], cw[2 * HK:].reshape(HK, GR, HW, TAPS)], 1)
    arrays["dn_cw"] = cw.transpose(0, 2, 1, 3)
    arrays["dn_wo"] = inputs["L0_attn_W_out"].reshape(HK, GR, HW, D).transpose(0, 2, 1, 3)
    arrays["dn_nw"] = inputs["L0_attn_norm_weight"].reshape(HW, 1)
    arrays["dn_upper"] = np.triu(np.ones((P, P), np.float32))
    ident0 = np.eye(P, dtype=np.float32)
    ident0[0, 0] = 0.0
    arrays["dn_ident0"] = np.repeat(ident0[:, None], 4, 1)
    row, col = np.arange(P)[:, None], np.arange(P)[None, :]
    masks = [((row >> l) != (col >> l)) & ((row >> (l + 1)) == (col >> (l + 1))) & (row > col) for l in range(7)]
    arrays["dn_masks"] = np.stack(masks + [masks[0].T], 1).astype(np.float32)
    arrays = {k: np.ascontiguousarray(v) for k, v in arrays.items()}
    nc = bacc.Bacc("TRN2", target_bir_lowering=False, num_devices=1)
    d = {k: nc.dram_tensor("in_" + k, v.shape, mybir.dt.from_np(v.dtype), kind="ExternalInput").ap()
         for k, v in arrays.items()}
    out = nc.dram_tensor("out_x", (B, SEQ, D), F32, kind="ExternalOutput").ap()
    program(nc, d, out)
    r = run_bass_kernel_spmd(nc, [{"in_" + k: v for k, v in arrays.items()}], core_ids=[0])
    return r.results[0]["out_x"]
```

```python
from contextlib import ExitStack

import concourse.bass as bass
from concourse import mybir

F32 = mybir.dt.float32
ALU = mybir.AluOpType
ACT = mybir.ActivationFunctionType
AX_X = mybir.AxisListType.X

P = 128
B, SEQ, D = 4, 256, 256
NT = B * SEQ // P
KD = D // P
C = SEQ // P
NTOK = B * SEQ
BANK = 512


class Shared:

    def __init__(self, nc, ctx):
        self.nc, self.ctx = nc, ctx
        self.x = self.sb("x", [P, NT, D])
        self.xnT = self.sb("xnT", [P, KD, NTOK])
        self.ident = self.sb("ident", [P, 4, P])
        self.neghalf = self.sb("neghalf", [P, 16])
        self.sems = []
        self.bank = ctx.enter_context(nc.psum_tensor("bank", [P, 8, BANK], F32))

    def sb(self, name, shape):
        return self.ctx.enter_context(self.nc.sbuf_tensor(name, shape, F32))

    def sem(self, name):
        self.sems.append(self.nc.alloc_semaphore(name=name))
        return self.sems[-1]

    def end_layer(self):
        self.nc.clear_and_free_semaphores(self.sems)
        self.nc.all_engine_barrier()
        self.sems = []


def start(nc, m, x, ident4):
    s_load = m.sem("st_load")
    with nc.Block() as block:
        @block.sync
        def _(sp):
            for b in range(B):
                sp.dma_start(m.x[:, C * b:C * b + C, :], x[b].rearrange("(c p) d -> p c d", p=P)).then_inc(s_load, 16)
            sp.wait_ge(s_load, 16 * B + 16)

        @block.scalar
        def _(act):
            act.dma_start(m.ident[:], ident4.rearrange("p (n q) -> p n q", n=4)).then_inc(s_load, 16)

        @block.vector
        def _(dve):
            nc.vector.memset(m.neghalf[:], -0.5)


def finish(nc, m, out):
    s_out = m.sem("fin_out")
    with nc.Block() as block:
        @block.sync
        def _(sp):
            for b in range(B):
                sp.dma_start(out[b].rearrange("(c p) d -> p c d", p=P), m.x[:, C * b:C * b + C, :]).then_inc(s_out, 16)
            sp.wait_ge(s_out, 16 * B)


def layer_norm(nc, m, tag, fetch=None):
    s_stat, s_mv, s_eps, s_rstd = (m.sem(f"{tag}_{n}") for n in ("stat", "mv", "eps", "rstd"))
    s_xn, s_tr, s_copied = (m.sem(f"{tag}_{n}") for n in ("xn", "tr", "copied"))
    with ExitStack() as tmp:
        def sb(name, shape):
            return tmp.enter_context(nc.sbuf_tensor(f"{tag}_{name}", shape, F32))
        stat = sb("stats", [P, NT, 6])
        mv = sb("meanvar", [P, NT, 2])
        vare = sb("vare", [P, NT])
        rstd = sb("rstdv", [P, NT])
        xn = sb("xnorm", [P, NT, D])
        with nc.Block() as block:
            if fetch is not None:
                @block.sync
                def _(sp):
                    fetch(sp)

            @block.vector
            def _(dve):
                for t in range(NT):
                    nc.vector.bn_stats(stat[:, t, :], m.x[:, t, :]).then_inc(s_stat, 1)
                for t in range(NT):
                    dve.wait_ge(s_stat, t + 1)
                    nc.vector.bn_aggr(mv[:, t, :], stat[:, t, :]).then_inc(s_mv, 1)
                dve.wait_ge(s_mv, NT)
                nc.vector.tensor_scalar(vare[:], mv[:, :, 1], 1e-5, None, ALU.add).then_inc(s_eps, 1)
                dve.wait_ge(s_rstd, 1)
                for t in range(NT):
                    nc.vector.tensor_scalar(xn[:, t, :], m.x[:, t, :], mv[:, t, 0:1], rstd[:, t:t + 1],
                                            ALU.subtract, ALU.mult).then_inc(s_xn, 1)

            @block.gpsimd
            def _(pool):
                pool.wait_ge(s_eps, 1)
                nc.gpsimd.tensor_tensor(rstd[:], vare[:], m.neghalf[:, 0:NT], ALU.pow).then_inc(s_rstd, 1)

            @block.tensor
            def _(pe):
                for t in range(NT):
                    pe.wait_ge(s_xn, t + 1)
                    for k in range(KD):
                        last = nc.tensor.transpose(m.bank[:, 2 * k + t // 4, P * (t % 4):P * (t % 4) + P],
                                                   xn[:, t, P * k:P * k + P], m.ident[:, 0, :])
                    last.then_inc(s_tr, 1)

            @block.scalar
            def _(act):
                for h in range(2):
                    act.wait_ge(s_tr, 4 * h + 4)
                    for k in range(KD):
                        nc.scalar.activation(m.xnT[:, k, BANK * h:BANK * h + BANK], m.bank[:, 2 * k + h, :],
                                             ACT.Copy).then_inc(s_copied, 1)
                act.wait_ge(s_copied, 2 * KD)


def two_slots(eng, n, lead, lag):
    lead(0, 0)
    with eng.Fori(0, n // 2 - 1) as p:
        lead(2 * p + 1, 1)
        lag(2 * p, 0)
        lead(2 * p + 2, 0)
        lag(2 * p + 1, 1)
    lead(n - 1, 1)
    lag(n - 2, 0)
    lag(n - 1, 1)


def gated_mlp(nc, m, before, tag, n, width, w_gate, w_up, w_down, weight=None):
    s_w = [m.sem(f"{tag}_w{s}") for s in range(2)]
    s_wd = [m.sem(f"{tag}_wd{s}") for s in range(2)]
    s_gu = m.sem(f"{tag}_gu")
    s_sg = m.sem(f"{tag}_sg")
    s_h = m.sem(f"{tag}_h")
    s_y = m.sem(f"{tag}_y")
    s_x = m.sem(f"{tag}_x")
    s_wc = m.sem(f"{tag}_wc")
    CY, CX, CH, CG = NT // 2, NT, 2, 4
    HALF = NTOK // 2
    with ExitStack() as tmp:
        def sb(name, shape):
            return tmp.enter_context(nc.sbuf_tensor(f"{tag}_{name}", shape, F32))
        wg = [sb(f"wg{s}", [P, KD, width]) for s in range(2)]
        wu = [sb(f"wu{s}", [P, KD, width]) for s in range(2)]
        wd = [sb(f"wd{s}", [width, D]) for s in range(2)]
        hT = [sb(f"hT{s}", [width, NTOK]) for s in range(2)]
        sg = sb("silu", [width, 2, HALF])
        wc = [sb(f"wc{s}", [P, NT]) for s in range(2)]

        def fetch(sp):
            sp.dma_start(wg[0][:], w_gate[0]).then_inc(s_w[0], 16)
            sp.dma_start(wu[0][:], w_up[0]).then_inc(s_w[0], 16)
            sp.dma_start(wd[0][:], w_down[0]).then_inc(s_wd[0], 16)
        before(fetch)

        def yb(t):
            return m.bank[:, 4 + t // 2, D * (t % 2):D * (t % 2) + D]

        with nc.Block() as block:
            @block.sync
            def _(sp):
                def load(e, s):
                    if isinstance(e, int) and e == 0:
                        return
                    sp.wait_ge(s_gu, e * 2 - 2 + CG)
                    sp.dma_start(wg[s][:], w_gate[e]).then_inc(s_w[s], 16)
                    sp.dma_start(wu[s][:], w_up[e]).then_inc(s_w[s], 16)
                    sp.wait_ge(s_y, e * (NT // 2) + CY - NT // 2)
                    sp.dma_start(wd[s][:], w_down[e]).then_inc(s_wd[s], 16)
                two_slots(sp, n, load, lambda e, s: None)

            @block.tensor
            def _(pe):
                pe.sem_inc(s_y, CY)
                pe.sem_inc(s_gu, CG)

                def gate_up(e, s):
                    pe.wait_ge(s_w[s], (e - s) * 16 + 32)
                    for hf in range(2):
                        pe.wait_ge(s_h, e * 2 - 1 + hf + CH)
                        for bank, w in ((hf, wg), (2 + hf, wu)):
                            for k in range(KD):
                                last = nc.tensor.matmul(m.bank[0:width, bank, :], w[s][:, k, :],
                                                        m.xnT[:, k, HALF * hf:HALF * hf + HALF],
                                                        start=(k == 0), stop=(k == KD - 1))
                        last.then_inc(s_gu, 1)

                def down(e, s):
                    pe.wait_ge(s_wd[s], (e - s) * 8 + 16)
                    for t in range(NT):
                        if t % 4 == 0:
                            pe.wait_ge(s_h, e * 2 + t // 4 + 1 + CH)
                        if t % 2 == 0:
                            pe.wait_ge(s_x, e * NT - NT + t + 2 + CX)
                        last = nc.tensor.matmul(yb(t), hT[s][:, P * t:P * t + P], wd[s][:], start=True, stop=True)
                        if t % 2:
                            last.then_inc(s_y, 1)
                two_slots(pe, n, gate_up, down)

            @block.scalar
            def _(act):
                def silu(e, s):
                    for hf in range(2):
                        act.wait_ge(s_gu, e * 2 + hf + 1 + CG)
                        act.wait_ge(s_h, e * 2 - 1 + hf + CH)
                        nc.scalar.activation(sg[:, hf, :], m.bank[0:width, hf, :], ACT.Silu).then_inc(s_sg, 1)
                two_slots(act, n, silu, lambda e, s: None)

            @block.vector
            def _(dve):
                dve.sem_inc(s_h, CH)
                dve.sem_inc(s_x, CX)

                def hidden(e, s):
                    for hf in range(2):
                        dve.wait_ge(s_sg, e * 2 + hf + 1)
                        if not (isinstance(e, int) and e == 0):
                            dve.wait_ge(s_y, e * (NT // 2) + CY - NT // 2)
                        nc.vector.tensor_tensor(hT[s][:, HALF * hf:HALF * hf + HALF], m.bank[0:width, 2 + hf, :],
                                                sg[:, hf, :], ALU.mult).then_inc(s_h, 1)

                def add(e, s):
                    if weight is not None:
                        dve.wait_ge(s_wc, e + 1)
                    for t in range(NT):
                        if t % 2 == 0:
                            dve.wait_ge(s_y, e * (NT // 2) + t // 2 + 1 + CY)
                        dve.wait_ge(s_x, e * NT - NT + t + 1 + CX)
                        if weight is None:
                            nc.vector.tensor_tensor(m.x[:, t, :], yb(t), m.x[:, t, :], ALU.add).then_inc(s_x, 1)
                        else:
                            nc.vector.scalar_tensor_tensor(out=m.x[:, t, :], in0=yb(t), scalar=wc[s][:, t:t + 1],
                                                           in1=m.x[:, t, :], op0=ALU.mult,
                                                           op1=ALU.add).then_inc(s_x, 1)
                two_slots(dve, n, hidden, add)

            if weight is not None:
                @block.gpsimd
                def _(pool):
                    def pick(e, s):
                        if not (isinstance(e, int) and e == 0):
                            pool.wait_ge(s_x, e * NT - NT + CX)
                        nc.gpsimd.tensor_copy(wc[s][:], weight[:, :, e]).then_inc(s_wc, 1)
                    two_slots(pool, n, pick, lambda e, s: None)


def route(nc, m, norm, fetch, gate_w, weight):
    E, TOP = 64, 8
    s_in, s_lg, s_cp, s_mx, s_rep, s_sel, s_sub, s_exp, s_em, s_sum, s_rec, s_w = (
        m.sem(f"rt_{n}") for n in ("in", "lg", "cp", "mx", "rep", "sel", "sub", "exp", "em", "sum", "rec", "w"))
    with ExitStack() as tmp:
        def sb(name, shape):
            return tmp.enter_context(nc.sbuf_tensor(f"rt_{name}", shape, F32))
        gw = sb("gw", [P, KD, E])
        lg = sb("logits", [P, NT, E])
        top = sb("top", [P, NT, TOP])
        rest = sb("rest", [P, NT, E])
        sel = sb("sel", [P, NT, E])
        ex = sb("ex", [P, NT, E])
        em = sb("em", [P, NT, E])
        tot = sb("tot", [P, NT])
        rec = sb("rec", [P, NT])

        def fetch_all(sp):
            sp.dma_start(gw[:], gate_w).then_inc(s_in, 16)
            fetch(sp)
        layer_norm(nc, m, norm, fetch_all)
        lgp = m.bank[:, 0, :].rearrange("p (t e) -> p t e", e=E)
        with nc.Block() as block:
            @block.tensor
            def _(pe):
                pe.wait_ge(s_in, 16)
                for t in range(NT):
                    for k in range(KD):
                        last = nc.tensor.matmul(lgp[:, t, :], m.xnT[:, k, P * t:P * t + P], gw[:, k, :],
                                                start=(k == 0), stop=(k == KD - 1))
                last.then_inc(s_lg, 1)

            @block.vector
            def _(dve):
                dve.wait_ge(s_lg, 1)
                nc.vector.tensor_copy(lg[:], lgp).then_inc(s_cp, 1)
                dve.wait_ge(s_cp, 1)
                for t in range(NT):
                    nc.vector.max(top[:, t, :], lg[:, t, :]).then_inc(s_mx, 1)
                for t in range(NT):
                    dve.wait_ge(s_mx, t + 1)
                    nc.vector.match_replace(rest[:, t, :], top[:, t, :], lg[:, t, :], -3.0e38).then_inc(s_rep, 1)
                dve.wait_ge(s_rep, NT)
                nc.vector.tensor_tensor(sel[:], rest[:], lg[:], ALU.not_equal).then_inc(s_sel, 1)
                nc.vector.tensor_tensor(ex[:], lg[:], top[:, :, 0:1].to_broadcast([P, NT, E]),
                                        ALU.subtract).then_inc(s_sub, 1)
                dve.wait_ge(s_exp, 1)
                dve.wait_ge(s_sel, 1)
                nc.vector.tensor_tensor(em[:], ex[:], sel[:], ALU.mult).then_inc(s_em, 1)
                dve.wait_ge(s_em, 1)
                nc.vector.tensor_reduce(tot[:], em[:], AX_X, ALU.add).then_inc(s_sum, 1)
                dve.wait_ge(s_sum, 1)
                nc.vector.reciprocal(rec[:], tot[:]).then_inc(s_rec, 1)
                dve.wait_ge(s_rec, 1)
                nc.vector.tensor_tensor(weight[:], em[:], rec[:].unsqueeze(2).to_broadcast([P, NT, E]),
                                        ALU.mult).then_inc(s_w, 1)

            @block.scalar
            def _(act):
                act.wait_ge(s_sub, 1)
                nc.scalar.activation(ex[:], ex[:], ACT.Exp).then_inc(s_exp, 1)



def causal_attention(nc, m, norm, tag, wq, wk, wv, wo, ctxT, cos, sin):
    G, GH, HD = wq.shape[0], 4, 16
    NV = wq.shape[3]
    VH = wv.shape[3] // HD
    SCALE = float(HD) ** -0.5
    KC, SK = (wk.shape[2], wk.shape[1])
    HALF = NTOK // 2
    E = GH * HD
    W = P + 2 * P
    s_w, s_wo, s_cst = m.sem(f"{tag}_w"), m.sem(f"{tag}_wo"), m.sem(f"{tag}_cst")
    s_proj = m.sem(f"{tag}_proj")
    s_pair = m.sem(f"{tag}_pair")
    s_qk = m.sem(f"{tag}_qk")
    s_kz, s_zero = m.sem(f"{tag}_kz"), m.sem(f"{tag}_zero")
    s_v, s_vc = m.sem(f"{tag}_v"), m.sem(f"{tag}_vc")
    s_sc, s_ms = m.sem(f"{tag}_sc"), m.sem(f"{tag}_ms")
    s_nm, s_ex = m.sem(f"{tag}_nm"), m.sem(f"{tag}_ex")
    s_pt, s_ptc = m.sem(f"{tag}_pt"), m.sem(f"{tag}_ptc")
    s_pv, s_rc, s_o = m.sem(f"{tag}_pv"), m.sem(f"{tag}_rc"), m.sem(f"{tag}_o")
    s_ot, s_otc = m.sem(f"{tag}_ot"), m.sem(f"{tag}_otc")
    s_y, s_x = m.sem(f"{tag}_y"), m.sem(f"{tag}_x")
    s_one, s_mask = m.sem(f"{tag}_one"), m.sem(f"{tag}_mask")
    CPT, CPV, COT, CY, CSC, CQK, CX, CV = 6, 1, 1, 4, 4, 2, 4, 1
    with ExitStack() as tmp:
        def sb(name, shape):
            return tmp.enter_context(nc.sbuf_tensor(f"{tag}_{name}", shape, F32))
        wq_sb = sb("wq", [P, KD, NV, P])
        wk_sb = sb("wk", [SK, KC, NV, P])
        wv_sb = sb("wv", [SK, KC, VH * HD])
        wo_sb = sb("wo", [2 * E, D])
        if ctxT is not None:
            src = sb("ctxT", [SK, 1, NTOK])
        else:
            src = m.xnT
            cs = [sb("cos", [P, SEQ]), sb("sin", [P, SEQ])]

        def load_projections(eng, g):
            for dst, w in ((wq_sb, wq), (wk_sb, wk), (wv_sb, wv)):
                eng.dma_start(dst[:], w[g]).then_inc(s_w, 16)

        def load_output(eng, g):
            for par in range(2):
                eng.dma_start(wo_sb[E * par:E * par + E, :], wo[g]).then_inc(s_wo, 16)

        def fetch(sp):
            load_projections(sp, 0)
            if ctxT is not None:
                sp.dma_start(src[:, 0, :], ctxT).then_inc(s_cst, 16)
            else:
                sp.dma_start(cs[0][:], cos).then_inc(s_cst, 16)
                sp.dma_start(cs[1][:], sin).then_inc(s_cst, 16)
            load_output(sp, 0)
        layer_norm(nc, m, norm, fetch)

        qkT = [sb("qT", [P, NTOK]), sb("kT", [P, NTOK])]
        kz = sb("kz", [P, GH, NTOK])
        prod = sb("prod", [P, 2, 2, HALF])
        V = sb("V", [P, NT, VH, HD + 1])
        S = sb("S", [P, 2, GH, W])
        nm = sb("nm", [P, 2, GH, 2])
        PT = sb("PT", [P, 3, GH, P])
        rec = sb("rec", [P, 2, GH, 1])
        O = sb("O", [P, NT, GH, HD])
        OT = sb("OT", [2 * E, NTOK // 2])
        mask = sb("mask", [P, W])
        pvb = m.bank[:, 7, 0:2 * GH * (HD + 1)].rearrange("p (c r d) -> p c r d", c=2, r=GH)
        PROJ = [(0, 0), (0, 1), (1, 0), (1, 1)]

        with nc.Block() as block:
            @block.sync
            def _(sp):
                with sp.Fori(0, G - 1) as g:
                    sp.wait_ge(s_v, g + 1 + CV)
                    load_projections(sp, g + 1)
                    sp.wait_ge(s_y, g * 4 + 4 + CY)
                    load_output(sp, g + 1)

            @block.gpsimd
            def _(pool):
                nc.gpsimd.memset(kz[:], 0.0).then_inc(s_zero, 1)
                nc.gpsimd.memset(mask[:], 0.0).then_inc(s_mask, 1)
                pool.wait_ge(s_mask, 1)
                for o in (0, 2 * P):
                    nc.gpsimd.affine_select(out=mask[:, o:o + P], in_=mask[:, o:o + P], compare_op=ALU.is_ge,
                                            fill=-3.0e38, base=0, pattern=[[-1, P]],
                                            channel_multiplier=1).then_inc(s_mask, 1)
                nc.gpsimd.memset(V[:, :, :, HD:HD + 1], 1.0).then_inc(s_one, 1)
                if cos is not None:
                    pool.sem_inc(s_qk, CQK)
                    with pool.Fori(0, G) as g:
                        for j, (a, hf) in enumerate(PROJ):
                            pool.wait_ge(s_pair, g * 4 + j + 1)
                            pool.wait_ge(s_sc, g * 4 + CSC)
                            nc.gpsimd.tensor_tensor(qkT[a][:, HALF * hf:HALF * hf + HALF], prod[:, j % 2, 0, :],
                                                    prod[:, j % 2, 1, :], ALU.add).then_inc(s_qk, 1)

            @block.tensor
            def _(pe):
                pe.sem_inc(s_pt, CPT)
                pe.sem_inc(s_pv, CPV)
                pe.sem_inc(s_ot, COT)
                pe.sem_inc(s_y, CY)
                pe.sem_inc(s_sc, CSC)
                pe.sem_inc(s_v, CV)

                def scores(g, b):
                    if b:
                        pe.wait_ge(s_ms, g * 4 + b)
                    at = SEQ * b
                    nc.tensor.matmul(m.bank[:, 0, :].rearrange("p (r n) -> p r n", r=GH), qkT[0][:, at:at + P],
                                     kz[:, :, at:at + P], start=True, stop=True)
                    for r in range(0, GH, 2):
                        last = nc.tensor.matmul(m.bank[:, 1 + r // 2, :].rearrange("p (r n) -> p r n", r=2),
                                                qkT[0][:, at + P:at + SEQ], kz[:, r:r + 2, at:at + SEQ],
                                                start=True, stop=True)
                    last.then_inc(s_sc, 1)

                pe.wait_ge(s_cst, 16 if ctxT is not None else 32)
                with pe.Fori(0, G) as g:
                    pe.wait_ge(s_w, g * 48 + 48)
                    pe.wait_ge(s_x, g * 4 + CX)
                    for j, (a, hf) in enumerate(PROJ):
                        w, s, kt = (wq_sb, m.xnT, KD) if a == 0 else (wk_sb, src, KC)
                        for v in range(NV):
                            for k in range(kt):
                                last = nc.tensor.matmul(m.bank[:, 2 * j + v, :], w[:, k, v, :],
                                                        s[:, k, HALF * hf:HALF * hf + HALF],
                                                        start=(k == 0), stop=(k == kt - 1))
                        last.then_inc(s_proj, 1)
                    pe.wait_ge(s_pair, g * 4 + 1)
                    for t in range(NT):
                        for k in range(KC):
                            last = nc.tensor.matmul(m.bank[:, 0, VH * HD * t:VH * HD * t + VH * HD],
                                                    src[:, k, P * t:P * t + P], wv_sb[:, k, :],
                                                    start=(k == 0), stop=(k == KC - 1))
                    last.then_inc(s_v, 1)
                    pe.wait_ge(s_vc, g + 1)
                    pe.wait_ge(s_pair, g * 4 + 4)
                    pe.wait_ge(s_qk, g * 4 + 4 + CQK)
                    pe.wait_ge(s_kz, g * 2 + 2)
                    scores(g, 0)
                    for b in range(B):
                        if b + 1 < B:
                            scores(g, b + 1)
                        pe.wait_ge(s_ex, g * 4 + b + 1)
                        for n in range(3):
                            if b:
                                pe.wait_ge(s_ptc, g * 12 + 3 * b - 2 + n)
                            for r in range(GH):
                                last = nc.tensor.transpose(m.bank[:, 4 + n, P * r:P * r + P],
                                                           S[:, b % 2, r, P * n:P * n + P], m.ident[:, 0, :])
                            last.then_inc(s_pt, 1)
                        pe.wait_ge(s_ptc, g * 12 + 3 * b + 3)
                        if b:
                            pe.wait_ge(s_o, g * 4 + b)
                        for r in range(GH):
                            vr = min(r, VH - 1)
                            nc.tensor.matmul(pvb[:, 0, r, :], PT[:, 0, r, :], V[:, 2 * b, vr, :],
                                             start=True, stop=True)
                            nc.tensor.matmul(pvb[:, 1, r, :], PT[:, 1, r, :], V[:, 2 * b, vr, :],
                                             start=True, stop=False)
                            last = nc.tensor.matmul(pvb[:, 1, r, :], PT[:, 2, r, :], V[:, 2 * b + 1, vr, :],
                                                    start=False, stop=True)
                        last.then_inc(s_pv, 1)
                    pe.wait_ge(s_o, g * 4 + 4)
                    for n in range(NT // 2):
                        last = nc.tensor.transpose(m.bank[:, 4, P * n:P * n + P],
                                                   O[:, 2 * n:2 * n + 2, :, :].rearrange("p t r d -> p (t r d)"),
                                                   m.ident[:, 0, :])
                    last.then_inc(s_ot, 1)
                    pe.wait_ge(s_wo, g * 32 + 32)
                    pe.wait_ge(s_otc, g + 1)
                    for q in range(4):
                        par, hi = q // 2, q % 2
                        for j in range(2):
                            n = 2 * hi + j
                            last = nc.tensor.matmul(m.bank[:, q, D * j:D * j + D],
                                                    OT[E * par:E * par + E, P * n:P * n + P],
                                                    wo_sb[E * par:E * par + E, :], start=True, stop=True)
                        last.then_inc(s_y, 1)

            @block.scalar
            def _(act):
                act.wait_ge(s_one, 1)
                if cos is None:
                    act.sem_inc(s_qk, CQK)
                act.wait_ge(s_zero, 1)
                with act.Fori(0, G) as g:
                    if cos is None:
                        for j, (a, hf) in enumerate(PROJ):
                            act.wait_ge(s_proj, g * 4 + j + 1)
                            act.wait_ge(s_sc, g * 4 + CSC)
                            nc.scalar.activation(qkT[a][:, HALF * hf:HALF * hf + HALF], m.bank[:, 2 * j, :],
                                                 ACT.Copy).then_inc(s_qk, 1)
                            act.wait_ge(s_qk, g * 4 + j + 1 + CQK)
                            act.sem_inc(s_pair, 1)
                    for hf in range(2):
                        act.wait_ge(s_qk, g * 4 + 3 + hf + CQK)
                        act.wait_ge(s_sc, g * 4 + CSC)
                        for r in range(GH):
                            rows, half = slice(32 * r, 32 * r + 32), slice(HALF * hf, HALF * hf + HALF)
                            last = nc.scalar.activation(kz[rows, r, half], qkT[1][rows, half], ACT.Copy)
                        last.then_inc(s_kz, 1)
                    act.wait_ge(s_v, g + 1 + CV)
                    act.wait_ge(s_pv, g * 4 + CPV)
                    nc.scalar.activation(V[:, :, :, 0:HD],
                                         m.bank[:, 0, 0:NT * VH * HD].rearrange("p (t r d) -> p t r d", t=NT, r=VH),
                                         ACT.Copy).then_inc(s_vc, 1)
                    for b in range(B):
                        act.wait_ge(s_nm, g * 4 + b + 1)
                        for r in range(GH):
                            for c in range(2):
                                s = S[:, b % 2, r, P * c:P + 2 * P * c]
                                last = nc.scalar.activation(s, s, ACT.Exp, bias=nm[:, b % 2, r, c:c + 1])
                        last.then_inc(s_ex, 1)
                        act.wait_ge(s_pv, g * 4 + b + CPV)
                        for n in range(3):
                            act.wait_ge(s_pt, g * 12 + 3 * b + n + 1 + CPT)
                            nc.scalar.activation(PT[:, n, :, :], m.bank[:, 4 + n, :].rearrange("p (r t) -> p r t", r=GH),
                                                 ACT.Copy).then_inc(s_ptc, 1)
                    act.wait_ge(s_ot, g + 1 + COT)
                    act.wait_ge(s_y, g * 4 + CY)
                    nc.scalar.activation(OT[:], m.bank[:, 4, :], ACT.Copy).then_inc(s_otc, 1)

            @block.vector
            def _(dve):
                dve.sem_inc(s_x, CX)
                dve.wait_ge(s_mask, 3)

                def softmax_in(g, b):
                    dve.wait_ge(s_sc, g * 4 + b + 1 + CSC)
                    dve.wait_ge(s_pt, g * 12 + 3 * b - 3 + CPT)
                    for lo, hi, bank in ((0, P, m.bank[:, 0, :]), (P, W, m.bank[:, 1:3, :].rearrange("p b n -> p (b n)"))):
                        last = nc.vector.scalar_tensor_tensor(
                            out=S[:, b % 2, :, lo:hi], in0=bank.rearrange("p (r n) -> p r n", r=GH), scalar=SCALE,
                            in1=mask[:, lo:hi].unsqueeze(1).to_broadcast([P, GH, hi - lo]), op0=ALU.mult, op1=ALU.add)
                    last.then_inc(s_ms, 1)
                    dve.wait_ge(s_ms, g * 4 + b + 1)
                    for c in range(2):
                        last = nc.vector.tensor_reduce(nm[:, b % 2, :, c], S[:, b % 2, :, P * c:P + 2 * P * c],
                                                       AX_X, ALU.max, negate=True)
                    last.then_inc(s_nm, 1)

                def normalise(g, b):
                    dve.wait_ge(s_pv, g * 4 + b + 1 + CPV)
                    dve.wait_ge(s_ot, g + COT)
                    nc.vector.reciprocal(rec[:], pvb[:, :, :, HD:HD + 1]).then_inc(s_rc, 1)
                    dve.wait_ge(s_rc, g * 4 + b + 1)
                    nc.vector.tensor_tensor(O[:, 2 * b:2 * b + 2, :, :], pvb[:, :, :, 0:HD],
                                            rec[:].to_broadcast([P, 2, GH, HD]), ALU.mult).then_inc(s_o, 1)

                if cos is not None:
                    dve.wait_ge(s_cst, 32)
                with dve.Fori(0, G) as g:
                    if cos is not None:
                        for j in range(4):
                            dve.wait_ge(s_proj, g * 4 + j + 1)
                            dve.wait_ge(s_qk, g * 4 + j - 1 + CQK)
                            for v in range(2):
                                last = nc.vector.tensor_tensor(
                                    prod[:, j % 2, v, :].rearrange("p (b t) -> p b t", b=2),
                                    m.bank[:, 2 * j + v, :].rearrange("p (b t) -> p b t", b=2),
                                    cs[v][:].unsqueeze(1).to_broadcast([P, 2, SEQ]), ALU.mult)
                            last.then_inc(s_pair, 1)
                    softmax_in(g, 0)
                    for b in range(B):
                        if b + 1 < B:
                            softmax_in(g, b + 1)
                        normalise(g, b)
                    for q in range(4):
                        dve.wait_ge(s_y, g * 4 + q + 1 + CY)
                        dve.wait_ge(s_x, g * 4 - 4 + q + 1 + CX)
                        t = 4 * (q % 2) + q // 2
                        nc.vector.tensor_tensor(m.x[:, t:t + 3:2, :], m.bank[:, q, :].rearrange("p (t n) -> p t n", t=2),
                                                m.x[:, t:t + 3:2, :], ALU.add).then_inc(s_x, 1)



def latent_attention(nc, m, tag, d):
    L, LEN = 64, d["mla_ctxT"].shape[2]
    R, CQ, HK = 64, 192, P
    PAIRS = 8
    LT = (LEN + P - 1) // P
    LAST = LEN - (LT - 1) * P
    UNITS = 2 * NT
    CUT = 2 * BANK
    PART = [(0, CUT), (CUT, LEN)]
    GROUPS = [range(n, min(n + 4, LT)) for n in range(0, LT, 4)]
    names = ("c1 c2 c3 c4 e1 e2 e3 e4 q qc sc nh nm ex tr pa pd pv rc cn ct ctc y x "
             "kc ks kt kh kx tt tk one wf")
    (s_c1, s_c2, s_c3, s_c4, s_e1, s_e2, s_e3, s_e4, s_q, s_qc, s_sc, s_nh, s_nm, s_ex, s_tr, s_pa, s_pd,
     s_pv, s_rc, s_cn, s_ct, s_ctc, s_y, s_x, s_kc, s_ks, s_kt, s_kh, s_kx, s_tt, s_tk, s_one, s_wf) = (
        m.sem(f"mla_{n}") for n in names.split())
    s_w, s_kin = ([m.sem(f"mla_{n}{s}") for s in range(2)] for n in ("w", "kin"))
    CX, CTR, CE3 = 4, 8, 1
    with ExitStack() as tmp:
        def sb(name, shape):
            return tmp.enter_context(nc.sbuf_tensor(f"mla_{name}", shape, F32))
        rot = sb("rot", [P, 2, LEN])
        sw = sb("sw", [P, 2, LEN])
        cosT, sinT = sb("cosT", [P, LEN]), sb("sinT", [P, LEN])

        def fetch_latents(sp):
            sp.dma_start(cosT[:], d["mla_cosT"]).then_inc(s_kin[0], 16)
            sp.dma_start(sinT[:], d["mla_sinT"]).then_inc(s_kin[0], 16)
            for j in range(2):
                sp.dma_start(rot[:, j, :], d["mla_ctxT"][j]).then_inc(s_kin[j], 16)
                sp.dma_start(sw[:, j, :], d["mla_swT"][j]).then_inc(s_kin[j], 16)

        tall, low = sb("tall", [P, 2, 2 * (HK + D + L + D)]), sb("low", [R, 2, 2 * (CQ + L + HK)])

        def load(eng, i, s):
            eng.dma_start(low[:, s], d["mla_low"][i]).then_inc(s_w[s], 16)
            eng.dma_start(tall[:, s], d["mla_tall"][i]).then_inc(s_w[s], 16)

        def part(t, at, width, s, h):
            return t[:, s, 2 * at + h * width:2 * at + (h + 1) * width]

        def wqr(s, h): return part(low, 0, CQ, s, h)
        def wkr(s, h): return part(low, CQ, L, s, h)
        def wcqB(s, h): return part(low, CQ + L, HK, s, h)
        def wcqA(s, h): return part(tall, 0, HK, s, h)
        def wq(s, h): return part(tall, HK, D, s, h)
        def wkv(s, h): return part(tall, HK + D, L, s, h)
        def wo(s, h): return part(tall, HK + D + L, D, s, h)

        def fetch(sp):
            load(sp, 0, 0)
            fetch_latents(sp)
            load(sp, 1, 1)
        layer_norm(nc, m, tag, fetch)

        kvT = sb("kvT", [P, B, LEN])
        kv = sb("kv", [P, B, LT, L + 1])
        f1A, f1B, f2 = sb("f1A", [P, 2, 2, L]), sb("f1B", [CQ - P, 2, 2, L]), sb("f2", [HK, 2, L])
        wfolds = sb("wfolds", [P, PAIRS, KD, 2 * L])
        wfold = sb("wfold", [P, KD, 2 * L])
        wouts = sb("wouts", [2 * L, PAIRS, D])
        qT = sb("qT", [P, NTOK])
        prob = sw
        nh, nm = sb("nh", [P, 2, 2]), sb("nm", [P, 2])
        PT = sb("PT", [P, 2, LT, P])
        rec = sb("rec", [P, 1])
        cn = sb("cn", [P, NT, 2 * L])
        cT = sb("cT", [P, NTOK])
        sc = m.bank[:, 0:4, :].rearrange("p b n -> p (b n)")

        with nc.Block() as block:
            @block.sync
            def _(sp):
                with sp.Fori(0, PAIRS // 2 - 1) as p:
                    for s in range(2):
                        sp.wait_ge(s_c3, 2 * p + s + 1 + CE3)
                        load(sp, 2 * p + s + 2, s)

            @block.gpsimd
            def _(pool):
                nc.gpsimd.memset(kv[:, :, :, L:L + 1], 1.0).then_inc(s_one, 1)
                for j in range(2):
                    pool.wait_ge(s_kt, j + 1)
                    pool.dma_start(kvT[L:2 * L, j, :], rot[0:L, j, :]).then_inc(s_kx, 16)
                    pool.dma_start(kvT[0:L, j + 2, :], rot[L:2 * L, j, :]).then_inc(s_kx, 16)
                    if j:
                        pool.wait_ge(s_kh, 2)
                    else:
                        pool.wait_ge(s_one, 1)
                    nc.gpsimd.tensor_copy(kvT[0:L, j, :], rot[0:L, j, :]).then_inc(s_kh, 1)
                    pool.wait_ge(s_kh, 2 * j + 1)
                    nc.gpsimd.tensor_copy(kvT[L:2 * L, j + 2, :], rot[L:2 * L, j, :]).then_inc(s_kh, 1)
                pool.wait_ge(s_kx, 64)
                pool.wait_ge(s_kh, 4)
                pool.wait_ge(s_e3, PAIRS + 1)
                with pool.Fori(0, PAIRS - 1) as i:
                    pool.wait_ge(s_q, i * 2 + 2)
                    nc.gpsimd.tensor_copy(wfold[:], wfolds[:, i + 1]).then_inc(s_wf, 1)

            @block.tensor
            def _(pe):
                pe.sem_inc(s_tr, CTR)
                pe.sem_inc(s_c3, CE3)

                def scores(i, u):
                    t, par = u // 2, u % 2
                    for h, (lo, hi) in enumerate(PART):
                        if u == 0:
                            pe.wait_ge(s_x, i * 4 - 2 + 2 * h + CX)
                        else:
                            pe.wait_ge(s_ex, i * 2 * UNITS + 2 * u - 1 + h)
                        for n in range(lo, hi, BANK):
                            e = min(n + BANK, hi)
                            last = nc.tensor.matmul(sc[:, n:e], qT[L * par:L * par + L, P * t:P * t + P],
                                                    kvT[L * par:L * par + L, t // C, n:e], start=True, stop=True)
                        last.then_inc(s_sc, 1)

                def transposes(i, v):
                    pe.wait_ge(s_ex, i * 2 * UNITS + 2 * v + 2)
                    for n, tiles in enumerate(GROUPS):
                        if n == 0 and v:
                            pe.wait_ge(s_pd, i * 2 * UNITS + 2 * v)
                        if n == 2 and v:
                            pe.wait_ge(s_pa, i * 2 * UNITS + 2 * v)
                        if n == 3:
                            pe.wait_ge(s_pa, i * 2 * UNITS + 2 * v + 1)
                        for a, lt in enumerate(tiles):
                            k = min(P, LEN - P * lt)
                            last = nc.tensor.transpose(m.bank[0:k, 4 + n % 3, P * a:P * a + P],
                                                       prob[:, v % 2, P * lt:P * lt + k], m.ident[:, 0, :])
                        last.then_inc(s_tr, 1)

                def context(i, v):
                    pe.wait_ge(s_pa, i * 2 * UNITS + 2 * v + 2)
                    pe.wait_ge(s_pd, i * 2 * UNITS + 2 * v + 2)
                    if v:
                        pe.wait_ge(s_cn, i * UNITS + v)
                    for lt in range(LT):
                        k = min(P, LEN - P * lt)
                        last = nc.tensor.matmul(m.bank[:, 7, 0:L + 1], PT[0:k, v % 2, lt, :],
                                                kv[0:k, v // (2 * C), lt, :], start=(lt == 0), stop=(lt == LT - 1))
                    last.then_inc(s_pv, 1)

                def fold1(i, s):
                    pe.wait_ge(s_w[s], (i - s) * 16 + 32)
                    pe.wait_ge(s_e1, i + 1)
                    for h in range(2):
                        nc.tensor.matmul(m.bank[:, 0, L * h:L * h + L], wqr(s, h)[:, 0:P], wkr(s, h),
                                         start=True, stop=True)
                        last = nc.tensor.matmul(m.bank[0:CQ - P, 0, 2 * L + L * h:3 * L + L * h], wqr(s, h)[:, P:CQ],
                                                wkr(s, h), start=True, stop=True)
                    last.then_inc(s_c1, 1)
                    pe.wait_ge(s_e4, i + 1)
                    for h in range(2):
                        last = nc.tensor.matmul(m.bank[L * h:L * h + L, 3, 0:D], wkv(s, h), wo(s, h),
                                                start=True, stop=True)
                    last.then_inc(s_c4, 1)

                def fold2(i, s):
                    pe.wait_ge(s_e1, i + 2)
                    pe.wait_ge(s_e2, i + 1)
                    for h in range(2):
                        nc.tensor.matmul(m.bank[:, 1, L * h:L * h + L], wcqA(s, h), f1A[:, s, h, :],
                                         start=True, stop=False)
                        last = nc.tensor.matmul(m.bank[:, 1, L * h:L * h + L], wcqB(s, h), f1B[:, s, h, :],
                                                start=False, stop=True)
                    last.then_inc(s_c2, 1)
                    pe.wait_ge(s_e2, i + 2)
                    pe.wait_ge(s_e3, i + 1)
                    for k in range(KD):
                        for h in range(2):
                            n = 2 * L * k + L * h
                            last = nc.tensor.matmul(m.bank[:, 2, n:n + L], wq(s, h)[:, P * k:P * k + P], f2[:, h, :],
                                                    start=True, stop=True)
                    last.then_inc(s_c3, 1)
                two_slots(pe, PAIRS, fold1, fold2)

                for j in range(2):
                    pe.wait_ge(s_kt, j + 1)
                    for n, tiles in enumerate(GROUPS):
                        if j:
                            pe.wait_ge(s_tk, n + 1)
                        for a, lt in enumerate(tiles):
                            k = min(P, LEN - P * lt)
                            last = nc.tensor.transpose(m.bank[0:k, 4 + n, P * a:P * a + P],
                                                       rot[:, j, P * lt:P * lt + k], m.ident[:, 0, :])
                        last.then_inc(s_tt, 1)
                pe.wait_ge(s_tk, 2 * len(GROUPS))

                def queries(w):
                    for hf in range(2):
                        for k in range(KD):
                            last = nc.tensor.matmul(m.bank[:, 4 + hf, :], w(k), m.xnT[:, k, BANK * hf:BANK * hf + BANK],
                                                    start=(k == 0), stop=(k == KD - 1))
                        last.then_inc(s_q, 1)
                pe.wait_ge(s_e3, PAIRS + 1)
                pe.wait_ge(s_e4, PAIRS + 1)
                queries(lambda k: wfolds[:, 0, k, :])
                pe.wait_ge(s_one, 1)
                pe.wait_ge(s_kh, 4)
                pe.wait_ge(s_kx, 64)

                def pair(i, more):
                    pe.wait_ge(s_qc, i * 2 + 2)
                    for u in range(UNITS + 2):
                        if u < UNITS:
                            scores(i, u)
                        if 1 <= u <= UNITS:
                            transposes(i, u - 1)
                        if u >= 2:
                            context(i, u - 2)
                    if more:
                        pe.wait_ge(s_wf, i + 1)
                        queries(lambda k: wfold[:, k, :])
                    pe.wait_ge(s_cn, i * UNITS + UNITS)
                    for t in range(NT):
                        last = nc.tensor.transpose(m.bank[:, 6 + t // 4, P * (t % 4):P * (t % 4) + P], cn[:, t, :],
                                                   m.ident[:, 0, :])
                        if t % 4 == 3:
                            last.then_inc(s_ct, 1)
                    for t in range(NT):
                        if t % 4 == 0:
                            pe.wait_ge(s_ctc, i * 2 + t // 4 + 1)
                        last = nc.tensor.matmul(m.bank[:, t // 2, D * (t % 2):D * (t % 2) + D], cT[:, P * t:P * t + P],
                                                wouts[:, i, :], start=True, stop=True)
                        if t % 2:
                            last.then_inc(s_y, 1)
                with pe.Fori(0, PAIRS - 1) as i:
                    pair(i, True)
                pair(PAIRS - 1, False)

            @block.scalar
            def _(act):
                for s_e in (s_e1, s_e2, s_e3, s_e4):
                    act.sem_inc(s_e, 1)

                def fold1(i, s):
                    act.wait_ge(s_c1, i + 1)
                    nc.scalar.activation(f1A[:, s], m.bank[:, 0, 0:2 * L].rearrange("p (h n) -> p h n", h=2), ACT.Copy)
                    nc.scalar.activation(f1B[:, s], m.bank[0:CQ - P, 0, 2 * L:4 * L].rearrange("p (h n) -> p h n", h=2),
                                         ACT.Copy).then_inc(s_e1, 1)
                    act.wait_ge(s_c4, i + 1)
                    nc.scalar.activation(wouts[:, i, :], m.bank[:, 3, 0:D], ACT.Copy).then_inc(s_e4, 1)

                def fold2(i, s):
                    act.wait_ge(s_c2, i + 1)
                    nc.scalar.activation(f2[:], m.bank[:, 1, 0:2 * L].rearrange("p (h n) -> p h n", h=2),
                                         ACT.Copy).then_inc(s_e2, 1)
                    act.wait_ge(s_c3, i + 1 + CE3)
                    nc.scalar.activation(wfolds[:, i], m.bank[:, 2, 0:KD * 2 * L].rearrange("p (k n) -> p k n", k=KD),
                                         ACT.Copy).then_inc(s_e3, 1)
                two_slots(act, PAIRS, fold1, fold2)
                for j in range(2):
                    for n, tiles in enumerate(GROUPS):
                        act.wait_ge(s_tt, j * len(GROUPS) + n + 1)
                        k = LAST if n == len(GROUPS) - 1 else P
                        nc.scalar.activation(kv[0:k, j::2, 4 * n:4 * n + len(tiles), 0:L].rearrange("p b a n -> p a b n"),
                                             m.bank[0:k, 4 + n, 0:P * len(tiles)].rearrange("p (a b n) -> p a b n", b=2, n=L),
                                             ACT.Copy).then_inc(s_tk, 1)

                def queries(i):
                    for hf in range(2):
                        act.wait_ge(s_q, i * 2 + hf + 1)
                        nc.scalar.activation(qT[:, BANK * hf:BANK * hf + BANK], m.bank[:, 4 + hf, :],
                                             ACT.Copy).then_inc(s_qc, 1)
                queries(0)

                def pair(i, more):
                    def copy(v, n):
                        act.wait_ge(s_tr, i * 4 * UNITS + 4 * v + n + 1 + CTR)
                        nc.scalar.activation(PT[:, v % 2, 4 * n:4 * n + 4, :],
                                             m.bank[:, 4 + n, :].rearrange("p (a t) -> p a t", a=4),
                                             ACT.Copy).then_inc(s_pa, 1)
                    for u in range(UNITS + 1):
                        if u:
                            if u > 2:
                                act.wait_ge(s_pv, i * UNITS + u - 2)
                            copy(u - 1, 0)
                        if u < UNITS:
                            act.wait_ge(s_nm, i * UNITS + u + 1)
                            act.wait_ge(s_tr, i * 4 * UNITS + 4 * u - 4 + CTR)
                            for lo, hi in PART:
                                nc.scalar.activation(prob[:, u % 2, lo:hi], sc[:, lo:hi], ACT.Exp,
                                                     bias=nm[:, u % 2:u % 2 + 1]).then_inc(s_ex, 1)
                        if u:
                            copy(u - 1, 2)
                    if more:
                        queries(i + 1)
                    for hf in range(2):
                        act.wait_ge(s_ct, i * 2 + hf + 1)
                        nc.scalar.activation(cT[:, BANK * hf:BANK * hf + BANK], m.bank[:, 6 + hf, :],
                                             ACT.Copy).then_inc(s_ctc, 1)
                with act.Fori(0, PAIRS - 1) as i:
                    pair(i, True)
                pair(PAIRS - 1, False)

            @block.vector
            def _(dve):
                dve.sem_inc(s_x, CX)
                for j in range(2):
                    dve.wait_ge(s_kin[0], 64)
                    if j:
                        dve.wait_ge(s_kin[1], 32)
                    nc.vector.tensor_tensor(rot[:, j, :], rot[:, j, :], cosT[:], ALU.mult).then_inc(s_kc, 1)
                    nc.vector.tensor_tensor(sw[:, j, :], sw[:, j, :], sinT[:], ALU.mult).then_inc(s_ks, 1)
                    dve.wait_ge(s_kc, j + 1)
                    dve.wait_ge(s_ks, j + 1)
                    nc.vector.tensor_tensor(rot[:, j, :], rot[:, j, :], sw[:, j, :], ALU.add).then_inc(s_kt, 1)
                with dve.Fori(0, PAIRS) as i:
                    def copy(v, n):
                        dve.wait_ge(s_tr, i * 4 * UNITS + 4 * v + n + 1 + CTR)
                        if n < 3:
                            nc.vector.tensor_copy(PT[:, v % 2, 4 * n:4 * n + 4, :],
                                                  m.bank[:, 4 + n, :].rearrange("p (a t) -> p a t", a=4)).then_inc(s_pd, 1)
                        else:
                            nc.vector.tensor_copy(PT[0:LAST, v % 2, LT - 1, :], m.bank[0:LAST, 4, 0:P]).then_inc(s_pd, 1)
                    for u in range(UNITS + 2):
                        if u < UNITS:
                            for h, (lo, hi) in enumerate(PART):
                                dve.wait_ge(s_sc, i * 2 * UNITS + 2 * u + h + 1)
                                nc.vector.tensor_reduce(nh[:, u % 2, h:h + 1], sc[:, lo:hi], AX_X, ALU.max,
                                                        negate=True).then_inc(s_nh, 1)
                            dve.wait_ge(s_nh, i * 2 * UNITS + 2 * u + 2)
                            nc.vector.tensor_tensor(nm[:, u % 2:u % 2 + 1], nh[:, u % 2, 0:1], nh[:, u % 2, 1:2],
                                                    ALU.min).then_inc(s_nm, 1)
                        if 1 <= u <= UNITS:
                            if u > 2:
                                dve.wait_ge(s_pv, i * UNITS + u - 2)
                            copy(u - 1, 1)
                            copy(u - 1, 3)
                        if u >= 2:
                            v = u - 2
                            dve.wait_ge(s_pv, i * UNITS + v + 1)
                            nc.vector.reciprocal(rec[:], m.bank[:, 7, L:L + 1]).then_inc(s_rc, 1)
                            dve.wait_ge(s_rc, i * UNITS + v + 1)
                            nc.vector.tensor_scalar(cn[:, v // 2, L * (v % 2):L * (v % 2) + L], m.bank[:, 7, 0:L],
                                                    rec[:], None, ALU.mult).then_inc(s_cn, 1)
                    for q in range(4):
                        dve.wait_ge(s_y, i * 4 + q + 1)
                        dve.wait_ge(s_x, i * 4 - 4 + q + 1 + CX)
                        nc.vector.tensor_tensor(m.x[:, 2 * q:2 * q + 2, :],
                                                m.bank[:, q, :].rearrange("p (t n) -> p t n", t=2),
                                                m.x[:, 2 * q:2 * q + 2, :], ALU.add).then_inc(s_x, 1)



HK, GR, HW = 16, 2, P
HV = HK * GR
TAPS = 4


def delta_gates(nc, m, d, gates):
    (s_in, s_ba, s_t, s_beta, s_abs, s_rl, s_ex, s_u, s_den, s_ln, s_e0, s_num, s_dd, s_rd, s_n2, s_lp, s_sp, s_ea,
     s_g, s_al, s_cum, s_eg, s_out) = (m.sem(f"dg_{n}") for n in (
         "in ba t beta abs rl ex u den ln e0 num dd rd n2 lp sp ea g al cum eg out").split())
    with ExitStack() as tmp:
        def sb(name, shape):
            return tmp.enter_context(nc.sbuf_tensor(f"dg_{name}", shape, F32))
        w = sb("w", [P, KD, 2 * HV])
        dt, alog, ea = sb("dt", [P, HV]), sb("alog", [P, HV]), sb("ea", [P, HV])
        upper = sb("upper", [P, P])
        t, beta, ab, rl, ex, u, den, ln, e0, sp, g, al, eg = (sb(n, [P, NT, HV]) for n in (
            "t beta ab rl ex u den ln e0 sp g al eg").split())
        ba = m.bank[:, 0, :].rearrange("p (t q h) -> p t q h", t=NT, q=2)
        cum = m.bank[:, 1, 0:NT * HV].rearrange("p (t h) -> p t h", t=NT)
        with nc.Block() as block:
            @block.sync
            def _(sp_):
                sp_.dma_start(w[:], d["dn_wba"]).then_inc(s_in, 16)
                sp_.dma_start(dt[:], d["dn_dt"].partition_broadcast(P)).then_inc(s_in, 16)
                sp_.dma_start(alog[:], d["dn_alog"].partition_broadcast(P)).then_inc(s_in, 16)
                sp_.dma_start(upper[:], d["dn_upper"]).then_inc(s_in, 16)

            @block.tensor
            def _(pe):
                pe.wait_ge(s_in, 64)
                for n in range(NT):
                    for k in range(KD):
                        last = nc.tensor.matmul(m.bank[:, 0, 2 * HV * n:2 * HV * n + 2 * HV],
                                                m.xnT[:, k, P * n:P * n + P], w[:, k, :],
                                                start=(k == 0), stop=(k == KD - 1))
                last.then_inc(s_ba, 1)
                pe.wait_ge(s_g, 1)
                nc.tensor.matmul(m.bank[:, 1, 0:NT * HV], upper[:], g[:].rearrange("p t h -> p (t h)"),
                                 start=True, stop=True).then_inc(s_cum, 1)

            @block.vector
            def _(dve):
                v = nc.vector
                dve.wait_ge(s_in, 64)
                dve.wait_ge(s_beta, 1)
                v.tensor_tensor(t[:], ba[:, :, 1, :], dt[:].unsqueeze(1).to_broadcast([P, NT, HV]), ALU.add).then_inc(s_t, 1)
                dve.wait_ge(s_t, 1)
                v.scalar_tensor_tensor(out=ab[:], in0=t[:], scalar=-1.0, in1=t[:], op0=ALU.mult,
                                       op1=ALU.max).then_inc(s_abs, 1)
                v.tensor_scalar(rl[:], t[:], 0.0, None, ALU.max).then_inc(s_rl, 1)
                dve.wait_ge(s_ex, 1)
                v.tensor_scalar(u[:], ex[:], 1.0, None, ALU.add).then_inc(s_u, 1)
                dve.wait_ge(s_u, 1)
                v.tensor_scalar(den[:], u[:], 1.0, None, ALU.subtract).then_inc(s_den, 1)
                dve.wait_ge(s_den, 1)
                v.tensor_scalar(e0[:], den[:], 0.0, None, ALU.is_equal).then_inc(s_e0, 1)
                dve.wait_ge(s_e0, 1)
                dve.wait_ge(s_ln, 1)
                v.tensor_tensor(ln[:], ln[:], e0[:], ALU.add).then_inc(s_num, 1)
                v.tensor_tensor(den[:], den[:], e0[:], ALU.add).then_inc(s_dd, 1)
                dve.wait_ge(s_dd, 1)
                v.reciprocal(den[:], den[:]).then_inc(s_rd, 1)
                dve.wait_ge(s_num, 1)
                v.tensor_tensor(ln[:], ln[:], ex[:], ALU.mult).then_inc(s_n2, 1)
                dve.wait_ge(s_n2, 1)
                dve.wait_ge(s_rd, 1)
                v.tensor_tensor(ln[:], ln[:], den[:], ALU.mult).then_inc(s_lp, 1)
                dve.wait_ge(s_lp, 1)
                dve.wait_ge(s_rl, 1)
                v.tensor_tensor(sp[:], ln[:], rl[:], ALU.add).then_inc(s_sp, 1)
                dve.wait_ge(s_sp, 1)
                dve.wait_ge(s_ea, 1)
                v.tensor_tensor(g[:], sp[:], ea[:].unsqueeze(1).to_broadcast([P, NT, HV]), ALU.mult).then_inc(s_g, 1)
                dve.wait_ge(s_al, 1)
                dve.wait_ge(s_eg, 1)
                for q, a in enumerate((al, beta, eg)):
                    v.tensor_copy(gates[:, :, q, :, :], a[:].rearrange("p t (h r) -> p h t r", r=GR)).then_inc(s_out, 1)

            @block.scalar
            def _(act):
                a = nc.scalar
                act.wait_ge(s_ba, 1)
                a.activation(beta[:], ba[:, :, 0, :], ACT.Sigmoid).then_inc(s_beta, 1)
                act.wait_ge(s_in, 64)
                a.activation(ea[:], alog[:], ACT.Exp).then_inc(s_ea, 1)
                act.wait_ge(s_abs, 1)
                a.activation(ex[:], ab[:], ACT.Exp, scale=-1.0).then_inc(s_ex, 1)
                act.wait_ge(s_u, 1)
                a.activation(ln[:], u[:], ACT.Ln).then_inc(s_ln, 1)
                act.wait_ge(s_g, 1)
                a.activation(al[:], g[:], ACT.Exp, scale=-1.0).then_inc(s_al, 1)
                act.wait_ge(s_cum, 1)
                a.activation(eg[:], cum, ACT.Exp, scale=-1.0).then_inc(s_eg, 1)


class Count:

    def __init__(self, sem, names):
        self.sem, self.n = sem, len(names)
        self.index = {name: k for k, name in enumerate(names)}
        assert len(self.index) == self.n

    def credit(self):
        return 2 * self.n

    def after(self, e, name):
        return e * self.n + self.index[name] + 1 + 2 * self.n


def delta_attention(nc, m, d):
    with nc.sbuf_tensor("dn_gates", [P, HK, 3, NT, GR], F32) as gates:
        delta_gates(nc, m, d, gates)
        delta_rounds(nc, m, d, gates)


def delta_rounds(nc, m, d, gates):
    GS = [(h, c) for h in range(GR) for c in range(C)]
    LEVELS = 7

    def corners(l):
        n = 2 ** l
        return [(slice(a, a + n), slice(a + n, a + 2 * n)) for a in range(0, P, 2 * n)] if n >= 32 else []
    CH = range(2 + GR)
    NCH = len(CH)
    FRONT = [("ss",)] + [("a", g) for g in range(4)] + [("kk", c) for c in range(C)] + [("k",)]
    FRONT += [("v", g) for g in range(4)] + [("qk", c) for c in range(C)] + [("n", g) for g in range(4)]
    LEVEL_JOBS = []
    for l in range(1, LEVELS):
        LEVEL_JOBS += [("t1", l, g) for g in range(4)] + [("x", l, g) for g in range(4)]
        if l < LEVELS - 1:
            LEVEL_JOBS += [("y", l, g) for g in range(4)]
    TAIL = [("u0", 0), ("u0", 1), ("s", 0), ("s", 1), ("o0", 0), ("o0", 1), ("z", 0), ("ks", 0), ("ks", 1), ("qs", 0),
            ("qs", 1), ("u1", 0), ("u1", 1), ("z", 1), ("o1", 0), ("o1", 1), ("z", 2), ("z", 3)]
    for c in range(C):
        TAIL += [("xt", c, h) for h in range(GR)] + [("out", 2 * c + a) for a in range(2)]
    ZJ = [("z", q) for q in range(4)]
    PJ = [("p", ch, hf) for ch in CH for hf in range(2)]
    PROJ = PJ + ZJ
    RING = FRONT + PJ + LEVEL_JOBS + TAIL
    assert len(RING) % 8 == 0
    EARLY = 2
    V_PROJ = [("conv", ch, j) for ch in CH for j in range(TAPS)]
    A_PROJ = [("raw", ch, hf) for ch in CH for hf in range(2)] + [("silu", ch) for ch in CH] + ZJ
    P_PROJ = ["cur", "wos"]
    P_AHEAD = [("sq", a) for a in range(2)] + [("da", g) for g in range(4)]
    V = ["ss"] + [("e", g) for g in range(4)] + [("kd", h) for h in range(GR)]
    V += [("n", h, c) for c in range(C) for h in range(GR)] + [("v", g) for g in range(4)] + [("a", h, c) for c in range(C) for h in range(GR)]
    V += [("x0", g) for g in range(4)]
    for l in range(1, LEVELS):
        V += [("t1", l, g) for g in range(4)] + [("x", l, g) for g in range(4)]
    V += [("u0", h) for h in range(GR)] + [("o0", h) for h in range(GR)] + [("ks", h) for h in range(GR)]
    V += [("qs", h) for h in range(GR)] + [(n, 0, h) for h in range(GR) for n in ("r2", "ms")]
    V += [("u1", h) for h in range(GR)] + [("o1", h) for h in range(GR)]
    V += [(n, 1, h) for h in range(GR) for n in ("r2", "ms")] + [("x+", q) for q in range(4)]
    A = [("y", l, g) for l in range(1, LEVELS - 1) for g in range(4)] + [("s", h) for h in range(GR)]
    A += [(n, c, h) for n in ("sq", "xt") for c in range(C) for h in range(GR)]
    G = ["r", "nk", "rq", "r2", "c2"]
    G += [("ec", g) for g in range(4)] + [(n, g) for g in range(4) for n in ("ym", "yi", "xi")] + ["z"]
    G += [("r", h) for h in range(GR)]
    G += [(n, 0, h) for h in range(GR) for n in ("rp", "xn")]
    G += [("xg", h) for h in range(GR)] + [(n, 1, h) for h in range(GR) for n in ("rp", "xn")]
    pj, vj, aj, gj = (Count(m.sem(f"dn_proj_{n}"), s) for n, s in (("pe", PROJ), ("dve", V_PROJ), ("act", A_PROJ),
                                                                 ("pool", P_PROJ)))
    pm, vm, am, gm = (Count(m.sem(f"dn_mat_{n}"), s) for n, s in (("pe", [j for j in RING if j not in PROJ]), ("dve", V), ("act", A), ("pool", G)))
    gh = Count(m.sem("dn_ahead_pool"), P_AHEAD)
    s_w, s_cst, s_pad = (m.sem(f"dn_{n}") for n in ("w", "cst", "pad"))
    s_cw, s_wo = ([m.sem(f"dn_{n}{s}") for s in range(2)] for n in ("cw", "wo"))

    def reader(job):
        n = job[0]
        if n == "ss":
            return vm, "ss"
        if n == "a":
            return vm, ("e", job[1])
        if n == "k":
            return vm, ("kd", 1)
        if n in ("kk", "qk"):
            return vm, ("n" if n == "kk" else "a", GR - 1, job[1])
        if n == "n":
            return vm, ("x0", job[1])
        if n in ("y", "s", "xt"):
            return am, job
        if n == "out":
            return vm, ("x+", job[1])
        return vm, job

    def bank_of(job):
        return RING.index(job) % 8

    def rounds(eng, front, project, rest, gates_ahead):
        def body(e, s):
            front(e, s)
            project(e + 1, 1 - s)
            rest(e, s)
        project(0, 0)
        gates_ahead(0, 0)
        with eng.Fori(0, HK // 2 - 1) as i:
            body(2 * i, 0)
            body(2 * i + 1, 1)
        body(HK - 2, 0)
        front(HK - 1, 1)
        rest(HK - 1, 1)

    def first(e):
        return isinstance(e, int) and e == 0

    def last_round(e):
        return isinstance(e, int) and e == HK - 1

    with ExitStack() as tmp:
        def sb(name, shape):
            return tmp.enter_context(nc.sbuf_tensor(f"dn_{name}", shape, F32))
        w = sb("w", [P, KD, (NCH + GR) * HW])
        cw = [sb(f"cw{s}", [P, NCH, TAPS]) for s in range(2)]
        wo = [sb(f"wo{s}", [HW, GR, D]) for s in range(2)]
        wos = [sb(f"wos{s}", [HW, GR, D]) for s in range(2)]
        nw = sb("nw", [HW, 1])
        ones = sb("ones", [P, P])
        ident0 = sb("ident0", [P, 4, P])
        masks = sb("masks", [P, LEVELS + 1, P])
        raw = sb("raw", [P, NCH, B, TAPS - 1 + SEQ])
        ct = [sb(f"ct{s}", [P, NCH, B, SEQ]) for s in range(2)]
        z = [sb(f"z{s}", [P, NT, GR, HW]) for s in range(2)]
        cur = [sb(f"cur{s}", [P, 3, NT, GR]) for s in range(2)]
        xg = sb("xg", [P, GR, NT, HW])
        ssv, rr, = sb("ssv", [P, 2, NT]), sb("rr", [P, 2, NT])
        nk, rq, r2 = sb("nk", [P, NT]), sb("rq", [P, NT]), sb("r2", [P, NT])
        c2 = sb("c2", [P, NT, GR])
        E = sb("E", [P, 4, 4, P])
        sq = E[:].rearrange("p g b n -> p (g b n)").rearrange("p (a n) -> p a n", a=2)
        T1 = sb("T1", [P, 4, 4, P])
        Ec = T1
        sqx = T1
        MT = sb("MT", [P, 4, 4, P])
        xn = MT
        AT = sb("AT", [P, 4, 4, P])
        da = raw[:, :, :, TAPS - 1:TAPS - 1 + P]
        X = sb("X", [P, 4, 4, P])
        xT = X
        Y = sb("Y", [P, 4, 4, P])
        vp = sb("vp", [P, GR, NT, HW])
        kd = sb("kd", [P, GR, B, HW])
        U = sb("U", [P, GR, B, HW])
        S = sb("S", [HW, GR, B, HW])
        R = sb("R", [P, GR, B, HW])
        ks = sb("ks", [P, GR, B, HW])
        os_ = ks
        qs = sb("qs", [P, GR, B, HW])
        ssx, rx = sb("ssx", [P, GR, C, B]), sb("rx", [P, GR, C, B])

        def four(bank):
            return m.bank[:, bank, :].rearrange("p (b n) -> p b n", b=4)

        def cols(a):
            return a.unsqueeze(2).to_broadcast([P, 4, P])

        with nc.Block() as block:
            @block.sync
            def _(sp):
                for dst, src in ((ident0, "ident0"), (masks, "masks"), (nw, "nw")):
                    sp.dma_start(dst[:], d["dn_" + src]).then_inc(s_cst, 16)

                def load(e, s):
                    sp.wait_ge(pj.sem, pj.after(e - 1, ZJ[-1]))
                    sp.dma_start(w[:], d["dn_w"][e]).then_inc(s_w, 16)
                    sp.wait_ge(vj.sem, vj.after(e - 2, ("conv", NCH - 1, TAPS - 1)))
                    sp.dma_start(cw[s][:], d["dn_cw"][e]).then_inc(s_cw[s], 16)
                    sp.wait_ge(gj.sem, gj.after(e - 2, "wos"))
                    sp.dma_start(wo[s][:], d["dn_wo"][e]).then_inc(s_wo[s], 16)
                two_slots(sp, HK, load, lambda e, s: None)

            @block.tensor
            def _(pe):
                pe.sem_inc(pj.sem, pj.credit())
                pe.sem_inc(pm.sem, pm.credit())
                pe.wait_ge(s_cst, 48)
                pe.wait_ge(s_pad, 2)

                def take(job, e, now):
                    n = RING.index(job)
                    if first(e) and job in PROJ:
                        return n % 8
                    k, r = n - 8, now
                    if k < 0:
                        k, r = k + len(RING), now - 1
                    while last_round(r) and RING[k] in PROJ:
                        k -= 8
                        if k < 0:
                            k, r = k + len(RING), r - 1
                    if RING[k] in PROJ:
                        step = ("raw",) + RING[k][1:] if RING[k][0] == "p" else RING[k]
                        pe.wait_ge(aj.sem, aj.after(r + 1, step))
                    else:
                        c_, step = reader(RING[k])
                        pe.wait_ge(c_.sem, c_.after(r, step))
                    return n % 8

                def gate_job(e, s, job):
                    if first(e):
                        pe.wait_ge(aj.sem, aj.after(0, ("raw", NCH - 1, 1)))
                    bank = take(job, e, e - 1)
                    for a in range(2):
                        t = 2 * job[1] + a
                        for k in range(KD):
                            last = nc.tensor.matmul(m.bank[:, bank, GR * HW * a:GR * HW * a + GR * HW],
                                                    m.xnT[:, k, P * t:P * t + P], w[:, k, NCH * HW:],
                                                    start=(k == 0), stop=(k == KD - 1))
                    last.then_inc(pj.sem, 1)

                def gates_ahead(e, s):
                    for job in ZJ:
                        gate_job(e, s, job)
                    pe.wait_ge(aj.sem, aj.after(0, ZJ[-1]))

                def project(e, s):
                    pe.wait_ge(s_w, e * 16 + 16)
                    for job in PJ:
                        bank = take(job, e, e - 1)
                        _, ch, hf = job
                        for k in range(KD):
                            last = nc.tensor.matmul(m.bank[:, bank, :], w[:, k, HW * ch:HW * ch + HW],
                                                    m.xnT[:, k, BANK * hf:BANK * hf + BANK],
                                                    start=(k == 0), stop=(k == KD - 1))
                        last.then_inc(pj.sem, 1)

                def front(e, s):
                    q, k = ct[s][:, 0], ct[s][:, 1]
                    bank = take(("ss",), e, e)
                    pe.wait_ge(gh.sem, gh.after(e, ("sq", 1)))
                    for a in range(2):
                        for t in range(NT):
                            last = nc.tensor.matmul(m.bank[:, bank, NT * a + t:NT * a + t + 1],
                                                    sq[:, a, P * t:P * t + P], ones[:, 0:1], start=True, stop=True)
                    last.then_inc(pm.sem, 1)
                    for g in range(4):
                        bank = take(("a", g), e, e)
                        pe.wait_ge(gh.sem, gh.after(e, ("da", g)))
                        nc.tensor.matmul(four(bank), ones[:], da[:, g],
                                         start=True, stop=True).then_inc(pm.sem, 1)
                    pe.wait_ge(aj.sem, aj.after(e, ("silu", 1)))
                    for c in range(C):
                        bank = take(("kk", c), e, e)
                        for b in range(B):
                            last = nc.tensor.matmul(m.bank[:, bank, P * b:P * b + P], k[:, b, P * c:P * c + P],
                                                    k[:, b, P * c:P * c + P], start=True, stop=True)
                        last.then_inc(pm.sem, 1)
                    bank = take(("k",), e, e)
                    for b in range(B):
                        last = nc.tensor.transpose(m.bank[:, bank, P * b:P * b + P], k[:, b, 0:P], m.ident[:, 0, :])
                    last.then_inc(pm.sem, 1)
                    for g, (h, c) in enumerate(GS):
                        bank = take(("v", g), e, e)
                        pe.wait_ge(aj.sem, aj.after(e, ("silu", 2 + h)))
                        for b in range(B):
                            last = nc.tensor.transpose(m.bank[:, bank, P * b:P * b + P],
                                                       ct[s][:, 2 + h, b, P * c:P * c + P], m.ident[:, 0, :])
                        last.then_inc(pm.sem, 1)
                    for c in range(C):
                        bank = take(("qk", c), e, e)
                        for b in range(B):
                            last = nc.tensor.matmul(m.bank[:, bank, P * b:P * b + P], k[:, b, P * c:P * c + P],
                                                    q[:, b, P * c:P * c + P], start=True, stop=True)
                        last.then_inc(pm.sem, 1)
                    for g, (h, c) in enumerate(GS):
                        bank = take(("n", g), e, e)
                        pe.wait_ge(vm.sem, vm.after(e, ("n", h, c)))
                        for b in range(B):
                            last = nc.tensor.transpose(m.bank[:, bank, P * b:P * b + P], MT[:, g, b, :],
                                                       m.ident[:, 0, :])
                        last.then_inc(pm.sem, 1)

                def rest(e, s):
                    q, k = ct[s][:, 0], ct[s][:, 1]

                    def job(name):
                        return take(name, e, e)

                    def ahead(name):
                        if not last_round(e):
                            gate_job(e + 1, 1 - s, name)

                    def corner_products(name, parts):
                        bank = job(name)
                        for b in range(B):
                            for rows, columns, lhsT, rhs in parts:
                                last = nc.tensor.matmul(four(bank)[rows, b, columns], lhsT[:, b], rhs[:, b],
                                                        start=True, stop=True)
                        last.then_inc(pm.sem, 1)

                    def product(name, lhsT, rhs):
                        bank = job(name)
                        for b in range(B):
                            last = nc.tensor.matmul(m.bank[:, bank, P * b:P * b + P], lhsT(b), rhs(b),
                                                    start=True, stop=True)
                        last.then_inc(pm.sem, 1)

                    for l in range(1, LEVELS):
                        for g in range(4):
                            if l == 1:
                                pe.wait_ge(gm.sem, gm.after(e, ("xi", g)))
                            else:
                                pe.wait_ge(vm.sem, vm.after(e, ("x", l - 1, g)))
                            if not corners(l):
                                product(("t1", l, g), lambda b: MT[:, g, b, :], lambda b: X[:, g, b, :])
                            else:
                                corner_products(("t1", l, g), [(hi, lo, MT[:, g, :, hi], X[:, g, :, lo])
                                                               for lo, hi in corners(l)])
                        for g in range(4):
                            pe.wait_ge(vm.sem, vm.after(e, ("t1", l, g)))
                            if l > 1:
                                pe.wait_ge(am.sem, am.after(e, ("y", l - 1, g)))
                            if not corners(l):
                                product(("x", l, g), lambda b: Y[:, g, b, :], lambda b: T1[:, g, b, :])
                            elif l < LEVELS - 1:
                                corner_products(("x", l, g), [(hi, lo, Y[:, g, :, hi], T1[:, g, :, lo])
                                                              for lo, hi in corners(l)])
                            else:
                                corner_products(("x", l, g), [(lo, hi, T1[:, g, :, lo], Y[:, g, :, hi])
                                                              for lo, hi in corners(l)])
                        if l < LEVELS - 1:
                            for g in range(4):
                                bank = job(("y", l, g))
                                pe.wait_ge(vm.sem, vm.after(e, ("x", l, g)))
                                for b in range(B):
                                    last = nc.tensor.transpose(m.bank[:, bank, P * b:P * b + P], X[:, g, b, :],
                                                               m.ident[:, 0, :])
                                last.then_inc(pm.sem, 1)

                    for h in range(GR):
                        pe.wait_ge(vm.sem, vm.after(e, ("x", LEVELS - 1, 2 * h)))
                        product(("u0", h), lambda b: Y[:, 2 * h, b, :], lambda b: vp[:, h, C * b, :])
                    for h in range(GR):
                        pe.wait_ge(vm.sem, vm.after(e, ("u0", h)))
                        product(("s", h), lambda b: kd[:, h, b, :], lambda b: U[:, h, b, :])
                    for h in range(GR):
                        product(("o0", h), lambda b: AT[:, 2 * h, b, :], lambda b: U[:, h, b, :])
                    ahead(("z", 0))
                    for h in range(GR):
                        pe.wait_ge(am.sem, am.after(e, ("s", h)))
                        product(("ks", h), lambda b: k[:, b, P:SEQ], lambda b: S[:, h, b, :])
                    for h in range(GR):
                        product(("qs", h), lambda b: q[:, b, P:SEQ], lambda b: S[:, h, b, :])
                    for h in range(GR):
                        pe.wait_ge(gm.sem, gm.after(e, ("r", h)))
                        product(("u1", h), lambda b: Y[:, 2 * h + 1, b, :], lambda b: R[:, h, b, :])
                    ahead(("z", 1))
                    for h in range(GR):
                        pe.wait_ge(vm.sem, vm.after(e, ("u1", h)))
                        product(("o1", h), lambda b: AT[:, 2 * h + 1, b, :], lambda b: U[:, h, b, :])
                    ahead(("z", 2))
                    ahead(("z", 3))
                    pe.wait_ge(gj.sem, gj.after(e, "wos"))
                    for c in range(C):
                        for h in range(GR):
                            bank = job(("xt", c, h))
                            pe.wait_ge(gm.sem, gm.after(e, ("xn", c, h)))
                            for b in range(B):
                                last = nc.tensor.transpose(m.bank[:, bank, P * b:P * b + P], xn[:, 2 * h + c, b, :],
                                                           m.ident[:, 0, :])
                            last.then_inc(pm.sem, 1)
                        for n in range(2):
                            bank = job(("out", 2 * c + n))
                            pe.wait_ge(am.sem, am.after(e, ("xt", c, GR - 1)))
                            for a in range(2):
                                for h in range(GR):
                                    last = nc.tensor.matmul(m.bank[:, bank, D * a:D * a + D],
                                                            xT[:, 2 * h + c, 2 * n + a, :], wos[s][:, h, :],
                                                            start=(h == 0), stop=(h == GR - 1))
                            last.then_inc(pm.sem, 1)
                rounds(pe, front, project, rest, gates_ahead)

            @block.scalar
            def _(act):
                act.sem_inc(aj.sem, aj.credit())
                act.sem_inc(am.sem, am.credit())

                def gate(e, s, n):
                    act.wait_ge(pj.sem, pj.after(e, ("z", n)))
                    act.wait_ge(gm.sem, gm.after(e - 2, ("xg", GR - 1)))
                    nc.scalar.activation(z[s][:, 2 * n:2 * n + 2, :, :],
                                         m.bank[:, bank_of(("z", n)), :].rearrange("p (t h n) -> p t h n", t=2, h=GR),
                                         ACT.Silu).then_inc(aj.sem, 1)

                def gates_ahead(e, s):
                    for n in range(4):
                        gate(e, s, n)

                def silu(e, s, ch):
                    act.wait_ge(vj.sem, vj.after(e, ("conv", ch, TAPS - 1)))
                    nc.scalar.activation(ct[s][:, ch], ct[s][:, ch], ACT.Silu).then_inc(aj.sem, 1)

                def project(e, s):
                    act.wait_ge(pm.sem, pm.after(e - 1, ("a", 3)))
                    for ch in CH:
                        act.wait_ge(vj.sem, vj.after(e - 1, ("conv", ch, TAPS - 1)))
                        for hf in range(2):
                            act.wait_ge(pj.sem, pj.after(e, ("p", ch, hf)))
                            nc.scalar.activation(raw[:, ch, 2 * hf:2 * hf + 2, TAPS - 1:],
                                                 m.bank[:, bank_of(("p", ch, hf)), :].rearrange("p (b t) -> p b t", b=2),
                                                 ACT.Copy).then_inc(aj.sem, 1)
                    for ch in range(NCH if first(e) else EARLY):
                        silu(e, s, ch)

                def rest(e, s):
                    def bank(name):
                        act.wait_ge(pm.sem, pm.after(e, name))
                        return four(bank_of(name))
                    for l in range(1, LEVELS - 1):
                        for g in range(4):
                            nc.scalar.activation(Y[:, g], bank(("y", l, g)), ACT.Copy).then_inc(am.sem, 1)
                        if EARLY + l - 1 < NCH and not last_round(e):
                            silu(e + 1, 1 - s, EARLY + l - 1)
                    for h in range(GR):
                        nc.scalar.activation(S[:, h], bank(("s", h)), ACT.Copy).then_inc(am.sem, 1)

                    def ahead(n):
                        if not last_round(e):
                            gate(e + 1, 1 - s, n)

                    def square(c, h):
                        nc.scalar.activation(sqx[:, 2 * h + c], xg[:, h, c::C, :], ACT.Square).then_inc(am.sem, 1)
                    ahead(0)
                    for h in range(GR):
                        act.wait_ge(vm.sem, vm.after(e, ("o0", h)))
                        square(0, h)
                    ahead(1)
                    ahead(2)
                    for h in range(GR):
                        act.wait_ge(gm.sem, gm.after(e, ("xg", h)))
                        square(1, h)
                    ahead(3)
                    for c in range(C):
                        for h in range(GR):
                            nc.scalar.activation(xT[:, 2 * h + c], bank(("xt", c, h)), ACT.Copy).then_inc(am.sem, 1)
                rounds(act, lambda e, s: None, project, rest, gates_ahead)

            @block.gpsimd
            def _(pool):
                t = nc.gpsimd
                t.memset(raw[:, :, :, 0:TAPS - 1], 0.0).then_inc(s_pad, 1)
                t.memset(ones[:], 1.0).then_inc(s_pad, 1)
                pool.sem_inc(gj.sem, gj.credit())
                pool.sem_inc(gm.sem, gm.credit())
                pool.sem_inc(gh.sem, gh.credit())
                pool.wait_ge(s_cst, 48)

                def project(e, s):
                    t.tensor_copy(cur[s][:], gates[:, e]).then_inc(gj.sem, 1)
                    pool.wait_ge(s_wo[s], (e - s) * 8 + 16)
                    pool.wait_ge(pm.sem, pm.after(e - 2, ("out", 3)))
                    t.tensor_tensor(wos[s][:], wo[s][:], nw[:].unsqueeze(2).to_broadcast([HW, GR, D]), ALU.mult).then_inc(gj.sem, 1)

                def squares_and_decays(e, s):
                    pool.wait_ge(vm.sem, vm.after(e - 1, ("a", GR - 1, C - 1)))
                    for a in range(2):
                        pool.wait_ge(aj.sem, aj.after(e, ("silu", a)))
                        v = ct[s][:, a].rearrange("p b t -> p (b t)")
                        t.tensor_tensor(sq[:, a, :], v, v, ALU.mult).then_inc(gh.sem, 1)
                    pool.wait_ge(gj.sem, gj.after(e, "cur"))
                    pool.wait_ge(vj.sem, vj.after(e, ("conv", NCH - 1, TAPS - 1)))
                    for g, (h, c) in enumerate(GS):
                        t.tensor_tensor(da[:, g], ident0[:], cols(cur[s][:, 0, c::C, h]), ALU.mult).then_inc(gh.sem, 1)

                def front(e, s):
                    beta = cur[s][:, 1]
                    pool.wait_ge(vm.sem, vm.after(e, "ss"))
                    t.tensor_tensor(rr[:], ssv[:], m.neghalf[:].rearrange("p (a t) -> p a t", a=2), ALU.pow).then_inc(gm.sem, 1)
                    pool.wait_ge(gm.sem, gm.after(e, "r"))
                    t.tensor_tensor(nk[:], ssv[:, 1], rr[:, 1], ALU.mult).then_inc(gm.sem, 1)
                    t.tensor_scalar(rq[:], rr[:, 0], float(HW) ** -0.5, None, ALU.mult).then_inc(gm.sem, 1)
                    t.tensor_tensor(r2[:], rr[:, 1], rr[:, 1], ALU.mult).then_inc(gm.sem, 1)
                    pool.wait_ge(gm.sem, gm.after(e, "r2"))
                    t.tensor_tensor(c2[:], beta, r2[:].unsqueeze(2).to_broadcast([P, NT, GR]), ALU.mult).then_inc(gm.sem, 1)
                    pool.wait_ge(gm.sem, gm.after(e, "c2"))
                    for g, (h, c) in enumerate(GS):
                        pool.wait_ge(vm.sem, vm.after(e, ("e", g)))
                        t.tensor_tensor(Ec[:, g], E[:, g], cols(c2[:, c::C, h]), ALU.mult).then_inc(gm.sem, 1)
                    for g, (h, c) in enumerate(GS):
                        pool.wait_ge(vm.sem, vm.after(e, ("n", h, c)))
                        t.tensor_tensor(Y[:, g], MT[:, g], masks[:, LEVELS:LEVELS + 1, :].to_broadcast([P, 4, P]),
                                        ALU.mult).then_inc(gm.sem, 1)
                        pool.wait_ge(gm.sem, gm.after(e, ("ym", g)))
                        t.tensor_tensor(Y[:, g], m.ident[:], Y[:, g], ALU.subtract).then_inc(gm.sem, 1)
                        pool.wait_ge(vm.sem, vm.after(e, ("x0", g)))
                        t.tensor_tensor(X[:, g], m.ident[:], X[:, g], ALU.subtract).then_inc(gm.sem, 1)

                def rest(e, s):
                    if not last_round(e):
                        squares_and_decays(e + 1, 1 - s)
                    pool.wait_ge(aj.sem, aj.after(e, ("z", 3)))
                    zz = z[s][:].rearrange("p t h n -> p t (h n)")
                    t.tensor_tensor(zz, zz, rq[:].unsqueeze(2).to_broadcast([P, NT, GR * HW]), ALU.mult).then_inc(gm.sem, 1)
                    for h in range(GR):
                        pool.wait_ge(vm.sem, vm.after(e, ("ks", h)))
                        t.tensor_tensor(R[:, h], vp[:, h, 1::C, :], ks[:, h], ALU.subtract).then_inc(gm.sem, 1)

                    def rms(c, h):
                        pool.wait_ge(vm.sem, vm.after(e, ("ms", c, h)))
                        t.tensor_tensor(rx[:, h, c], ssx[:, h, c], m.neghalf[:, 0:4], ALU.pow).then_inc(gm.sem, 1)
                        pool.wait_ge(gm.sem, gm.after(e, ("rp", c, h)))
                        t.tensor_tensor(xn[:, 2 * h + c], xg[:, h, c::C, :], cols(rx[:, h, c]), ALU.mult).then_inc(gm.sem, 1)
                    for h in range(GR):
                        rms(0, h)
                    for h in range(GR):
                        pool.wait_ge(vm.sem, vm.after(e, ("o1", h)))
                        t.tensor_tensor(xg[:, h, 1::C, :], os_[:, h], z[s][:, 1::C, h, :], ALU.mult).then_inc(gm.sem, 1)
                    for h in range(GR):
                        rms(1, h)
                rounds(pool, front, project, rest, squares_and_decays)

            @block.vector
            def _(dve):
                t = nc.vector
                dve.sem_inc(vj.sem, vj.credit())
                dve.sem_inc(vm.sem, vm.credit())
                dve.wait_ge(s_cst, 48)
                dve.wait_ge(s_pad, 1)

                def conv(e, s, ch):
                    dve.wait_ge(aj.sem, aj.after(e, ("raw", ch, 1)))
                    for j in range(TAPS):
                        src = raw[:, ch, :, j:j + SEQ]
                        if j == 0:
                            t.tensor_scalar(ct[s][:, ch], src, cw[s][:, ch, 0:1], None, ALU.mult).then_inc(vj.sem, 1)
                        else:
                            dve.wait_ge(vj.sem, vj.after(e, ("conv", ch, j - 1)))
                            t.scalar_tensor_tensor(out=ct[s][:, ch], in0=src, scalar=cw[s][:, ch, j:j + 1],
                                                   in1=ct[s][:, ch], op0=ALU.mult, op1=ALU.add).then_inc(vj.sem, 1)

                def project(e, s):
                    dve.wait_ge(s_cw[s], (e - s) * 8 + 16)
                    dve.wait_ge(pm.sem, pm.after(e - 2, ("qs", GR - 1)))
                    for ch in range(NCH if first(e) else EARLY):
                        conv(e, s, ch)

                def source(e, name):
                    dve.wait_ge(pm.sem, pm.after(e, name))
                    return four(bank_of(name))

                def front(e, s):
                    def bank(name):
                        return source(e, name)
                    n = bank_of(("ss",))
                    dve.wait_ge(pm.sem, pm.after(e, ("ss",)))
                    t.tensor_scalar(ssv[:].rearrange("p a t -> p (a t)"), m.bank[:, n, 0:2 * NT], 1e-6, None,
                                    ALU.add).then_inc(vm.sem, 1)
                    for g in range(4):
                        src = bank(("a", g)).rearrange("p b n -> p (b n)")
                        t.tensor_tensor_scan(E[:, g].rearrange("p b n -> p (b n)"), src,
                                             m.ident[:].rearrange("p b n -> p (b n)"), 0.0, ALU.mult,
                                             ALU.add).then_inc(vm.sem, 1)
                    src = bank(("k",))
                    dve.wait_ge(vm.sem, vm.after(e, ("e", 2)))
                    for h in range(GR):
                        t.tensor_tensor(kd[:, h], src, E[:, 2 * h, :, P - 1:P].to_broadcast([P, 4, P]),
                                        ALU.mult).then_inc(vm.sem, 1)
                    for c in range(C):
                        src = bank(("kk", c))
                        for h in range(GR):
                            dve.wait_ge(gm.sem, gm.after(e, ("ec", 2 * h + c)))
                            t.tensor_tensor(MT[:, 2 * h + c], src, Ec[:, 2 * h + c], ALU.mult).then_inc(vm.sem, 1)
                    dve.wait_ge(gm.sem, gm.after(e, "nk"))
                    for g, (h, c) in enumerate(GS):
                        t.tensor_tensor(vp[:, h, c::C, :], bank(("v", g)), cols(nk[:, c::C]), ALU.mult).then_inc(vm.sem, 1)
                    for c in range(C):
                        src = bank(("qk", c))
                        for h in range(GR):
                            t.tensor_tensor(AT[:, 2 * h + c], src, E[:, 2 * h + c], ALU.mult).then_inc(vm.sem, 1)
                    for g in range(4):
                        t.tensor_tensor(X[:, g], bank(("n", g)), masks[:, 0:1, :].to_broadcast([P, 4, P]),
                                        ALU.mult).then_inc(vm.sem, 1)

                def rest(e, s):
                    eg = cur[s][:, 2]

                    def bank(name):
                        return source(e, name)
                    for l in range(1, LEVELS):
                        for g in range(4):
                            if not corners(l):
                                t.tensor_tensor(T1[:, g], bank(("t1", l, g)), masks[:, l:l + 1, :].to_broadcast([P, 4, P]),
                                                ALU.mult).then_inc(vm.sem, 1)
                            else:
                                src = bank(("t1", l, g))
                                for lo, hi in corners(l):
                                    last = t.tensor_copy(T1[hi, g, :, lo], src[hi, :, lo])
                                last.then_inc(vm.sem, 1)
                        for g in range(4):
                            if l == 1:
                                dve.wait_ge(gm.sem, gm.after(e, ("xi", g)))
                            src = bank(("x", l, g))
                            parts = [(X, slice(0, P), slice(0, P))]
                            if corners(l):
                                parts = [(X, hi, lo) if l < LEVELS - 1 else (Y, lo, hi) for lo, hi in corners(l)]
                            for old, rows, columns in parts:
                                part = old[rows, g, :, columns]
                                last = t.tensor_tensor(part, part, src[rows, :, columns], ALU.subtract)
                            last.then_inc(vm.sem, 1)
                        if EARLY + l - 1 < NCH and not last_round(e):
                            conv(e + 1, 1 - s, EARLY + l - 1)
                    for h in range(GR):
                        t.tensor_tensor(U[:, h], bank(("u0", h)), cols(c2[:, 0::C, h]), ALU.mult).then_inc(vm.sem, 1)
                    for h in range(GR):
                        dve.wait_ge(gm.sem, gm.after(e, "z"))
                        t.tensor_tensor(xg[:, h, 0::C, :], bank(("o0", h)), z[s][:, 0::C, h, :], ALU.mult).then_inc(vm.sem, 1)
                    for h in range(GR):
                        t.tensor_tensor(ks[:, h], bank(("ks", h)), cols(eg[:, 1::C, h]), ALU.mult).then_inc(vm.sem, 1)
                    for h in range(GR):
                        t.tensor_tensor(qs[:, h], bank(("qs", h)), cols(eg[:, 1::C, h]), ALU.mult).then_inc(vm.sem, 1)

                    def mean_square(c, h):
                        t.tensor_reduce(ssx[:, h, c], sqx[:, 2 * h + c], AX_X, ALU.add).then_inc(vm.sem, 1)
                        dve.wait_ge(vm.sem, vm.after(e, ("r2", c, h)))
                        t.tensor_scalar(ssx[:, h, c], ssx[:, h, c], 1.0 / HW, 1e-6, ALU.mult, ALU.add).then_inc(vm.sem, 1)

                    for h in range(GR):
                        dve.wait_ge(am.sem, am.after(e, ("sq", 0, h)))
                        mean_square(0, h)
                    for h in range(GR):
                        t.tensor_tensor(U[:, h], bank(("u1", h)), cols(c2[:, 1::C, h]), ALU.mult).then_inc(vm.sem, 1)
                    for h in range(GR):
                        dve.wait_ge(vm.sem, vm.after(e, ("qs", h)))
                        t.tensor_tensor(os_[:, h], bank(("o1", h)), qs[:, h], ALU.add).then_inc(vm.sem, 1)
                    for h in range(GR):
                        dve.wait_ge(am.sem, am.after(e, ("sq", 1, h)))
                        mean_square(1, h)
                    for n in range(4):
                        c, b = n // 2, 2 * (n % 2)
                        tiles = m.x[:, C * b + c:C * b + c + C + 1:C, :]
                        dve.wait_ge(pm.sem, pm.after(e, ("out", n)))
                        dve.wait_ge(vm.sem, vm.after(e - 1, ("x+", n)))
                        nb = bank_of(("out", n))
                        t.tensor_tensor(tiles, m.bank[:, nb, :].rearrange("p (t n) -> p t n", t=2), tiles,
                                        ALU.add).then_inc(vm.sem, 1)
                rounds(dve, front, project, rest, lambda e, s: None)



def program(nc, d, out):
    with ExitStack() as ctx:
        m = Shared(nc, ctx)
        start(nc, m, d["x"], d["ident4"])
        layer_norm(nc, m, "ln1")
        delta_attention(nc, m, d)
        m.end_layer()
        latent_attention(nc, m, "ln2", d)
        m.end_layer()
        gated_mlp(nc, m, lambda fetch: layer_norm(nc, m, "ln3", fetch), "ffn", 8, P, d["f0_gate"], d["f0_up"], d["f0_down"])
        m.end_layer()
        causal_attention(nc, m, "ln4", "att", d["a1_wq"], d["a1_wk"], d["a1_wv"], d["a1_wo"], None, d["a1_cos"], d["a1_sin"])
        m.end_layer()
        causal_attention(nc, m, "ln5", "xat", d["x1_wq"], d["x1_wk"], d["x1_wv"], d["x1_wo"], d["x1_ctxT"], None, None)
        m.end_layer()
        with nc.sbuf_tensor("moe_weight", [P, NT, 64], F32) as weight:
            gated_mlp(nc, m, lambda fetch: route(nc, m, "ln6", fetch, d["m1_route"], weight), "moe", 64, 96, d["m1_gate"], d["m1_up"], d["m1_down"], weight)
        finish(nc, m, out)


def kernel(**inputs):
    import numpy as np
    import concourse.bacc as bacc
    from concourse.bass_utils import run_bass_kernel_spmd

    def ktiles(w):
        return w.reshape(w.shape[0], KD, P, w.shape[2]).transpose(0, 2, 1, 3)

    arrays = {"x": inputs["x"], "ident4": np.tile(np.eye(P, dtype=np.float32), (1, 4))}
    arrays["f0_gate"] = ktiles(inputs["L0_ffn_w_gate"].reshape(8, P, D).transpose(0, 2, 1))
    arrays["f0_up"] = ktiles(inputs["L0_ffn_w_up"].reshape(8, P, D).transpose(0, 2, 1))
    arrays["f0_down"] = inputs["L0_ffn_w_down"].T.reshape(8, P, D)
    arrays["m1_route"] = ktiles(inputs["L1_ffn_gate_weight"].T[None])[0]
    arrays["m1_gate"] = ktiles(inputs["L1_ffn_w_gate"])
    arrays["m1_up"] = ktiles(inputs["L1_ffn_w_up"])
    arrays["m1_down"] = inputs["L1_ffn_w_down"]
    GQ, GH, HD = 4, 4, 16

    def heads32(w, swap):
        w = w.reshape(GQ, GH, HD, -1)
        if swap:
            w = np.concatenate([w[:, :, HD // 2:], w[:, :, :HD // 2]], 2)
        wide = np.zeros((GQ, GH, 32, w.shape[3]), w.dtype)
        wide[:, :, :HD] = w
        return wide.reshape(GQ, P, -1).transpose(0, 2, 1)

    def versions(w):
        return np.stack([ktiles(heads32(w, s)) for s in (False, True)], 3)

    wk = np.repeat(inputs["L1_attn_Wk"].reshape(GQ, 1, HD, D), GH, 1)
    arrays["a1_wq"] = versions(inputs["L1_attn_Wq"])
    arrays["a1_wk"] = versions(wk)
    arrays["a1_wv"] = ktiles(inputs["L1_attn_Wv"].reshape(GQ, HD, D).transpose(0, 2, 1))
    arrays["a1_wo"] = inputs["L1_attn_Wp"].T.reshape(GQ, GH * HD, D)
    half = HD // 2
    inv_freq = (1.0 / np.float32(10000.0) ** (np.arange(half, dtype=np.float32) / np.float32(half))).astype(np.float32)
    angle = np.arange(SEQ, dtype=np.float32)[None, :] * inv_freq[:, None]
    cos = np.zeros((GH, 32, SEQ), np.float32)
    sin = np.zeros((GH, 32, SEQ), np.float32)
    cos[:, :HD] = np.concatenate([np.cos(angle), np.cos(angle)])
    sin[:, :HD] = np.concatenate([-np.sin(angle), np.sin(angle)])
    arrays["a1_cos"], arrays["a1_sin"] = cos.reshape(P, SEQ), sin.reshape(P, SEQ)
    arrays["x1_wq"] = ktiles(heads32(inputs["L1_xattn_Wq"], False))[:, :, :, None]
    arrays["x1_wk"] = heads32(inputs["L1_xattn_Wkv_expand"][:D], False)[:, :, None, None]
    arrays["x1_wv"] = inputs["L1_xattn_Wkv_expand"][D:].reshape(GQ, GH * HD, -1).transpose(0, 2, 1)[:, :, None]
    arrays["x1_wo"] = inputs["L1_xattn_Wout"].T.reshape(GQ, GH * HD, D)
    arrays["x1_ctxT"] = inputs["ctx_512"][:, :SEQ].transpose(2, 0, 1).reshape(-1, NTOK)
    PAIRS, LAT, LEN = 8, 64, inputs["ctx_512"].shape[1]

    def pairs(w):
        return w.reshape(PAIRS, 2, w.shape[1], w.shape[2]).transpose(0, 2, 1, 3).reshape(PAIRS, w.shape[1], -1)

    wcq = inputs["L0_xattn_w_kc_q"].transpose(0, 2, 1)
    arrays["mla_low"] = np.concatenate([pairs(inputs["L0_xattn_W_qr"].transpose(0, 2, 1)),
                                        pairs(inputs["L0_xattn_W_kr"].transpose(0, 2, 1)), pairs(wcq[:, P:])], -1)
    arrays["mla_tall"] = np.concatenate([pairs(wcq[:, :P]), pairs(inputs["L0_xattn_Wq"].reshape(2 * PAIRS, P, D)),
                                         pairs(inputs["L0_xattn_w_kc_kv"]),
                                         pairs(inputs["L0_xattn_Wo"].T.reshape(2 * PAIRS, P, D))], -1)
    ctx = inputs["ctx_512"]
    swapped = np.concatenate([ctx[:, :, LAT // 2:], ctx[:, :, :LAT // 2]], -1)
    inv = (1.0 / np.float32(10000.0) ** (np.arange(0, LAT, 2, dtype=np.float32) / np.float32(LAT))).astype(np.float32)
    freqs = np.arange(LEN, dtype=np.float32)[:, None] * inv[None, :]
    cosk = np.repeat(np.cos(freqs), 2, axis=-1)
    sink = np.repeat(np.sin(freqs), 2, axis=-1)
    sink = np.concatenate([-sink[:, :LAT // 2], sink[:, LAT // 2:]], -1)
    arrays["mla_cosT"], arrays["mla_sinT"] = np.tile(cosk.T, (2, 1)), np.tile(sink.T, (2, 1))
    arrays["mla_ctxT"], arrays["mla_swT"] = (
        w.transpose(0, 2, 1).reshape(2, 2, LAT, LEN).transpose(1, 0, 2, 3).reshape(2, 2 * LAT, LEN) for w in (ctx, swapped))
    arrays["dn_w"] = ktiles(inputs["L0_attn_W_qkvz"].reshape(D, HK, -1).transpose(1, 0, 2))
    wba = inputs["L0_attn_W_ba"].reshape(D, HK, 2, GR).transpose(0, 2, 1, 3).reshape(1, D, 2 * HV)
    arrays["dn_wba"] = ktiles(wba)[0]
    arrays["dn_dt"], arrays["dn_alog"] = inputs["L0_attn_dt_bias"], inputs["L0_attn_A_log"]
    cw = inputs["L0_attn_conv_w"].reshape(-1, HW, TAPS)
    cw = np.concatenate([cw[:HK, None], cw[HK:2 * HK, None], cw[2 * HK:].reshape(HK, GR, HW, TAPS)], 1)
    arrays["dn_cw"] = cw.transpose(0, 2, 1, 3)
    arrays["dn_wo"] = inputs["L0_attn_W_out"].reshape(HK, GR, HW, D).transpose(0, 2, 1, 3)
    arrays["dn_nw"] = inputs["L0_attn_norm_weight"].reshape(HW, 1)
    arrays["dn_upper"] = np.triu(np.ones((P, P), np.float32))
    ident0 = np.eye(P, dtype=np.float32)
    ident0[0, 0] = 0.0
    arrays["dn_ident0"] = np.repeat(ident0[:, None], 4, 1)
    row, col = np.arange(P)[:, None], np.arange(P)[None, :]
    masks = [((row >> l) != (col >> l)) & ((row >> (l + 1)) == (col >> (l + 1))) & (row > col) for l in range(7)]
    arrays["dn_masks"] = np.stack(masks + [masks[0].T], 1).astype(np.float32)
    arrays = {k: np.ascontiguousarray(v) for k, v in arrays.items()}
    nc = bacc.Bacc("TRN2", target_bir_lowering=False, num_devices=1)
    d = {k: nc.dram_tensor("in_" + k, v.shape, mybir.dt.from_np(v.dtype), kind="ExternalInput").ap()
         for k, v in arrays.items()}
    out = nc.dram_tensor("out_x", (B, SEQ, D), F32, kind="ExternalOutput").ap()
    program(nc, d, out)
    r = run_bass_kernel_spmd(nc, [{"in_" + k: v for k, v in arrays.items()}], core_ids=[0])
    return r.results[0]["out_x"]
```
